# Optimizing a Trainium2 kernel written in Bass

```python
import numpy as np
import jax
import jax.numpy as jnp

def _softmax(x, axis=-1):
    return jax.nn.softmax(x, axis=axis)

def _gelu(x):
    return jax.nn.gelu(x, approximate=True)

def _silu(x):
    return jax.nn.silu(x)

def _sigmoid(x):
    return jax.nn.sigmoid(x)

def _layernorm(x, axis=-1, eps=1e-05):
    m = jnp.mean(x, axis=axis, keepdims=True)
    v = jnp.var(x, axis=axis, keepdims=True)
    return (x - m) / jnp.sqrt(v + eps)

def _scatter_add(tgt, idx, src, axis=0):
    return tgt.at[idx].add(src)

def _segment_sum(src, seg, n):
    return jax.ops.segment_sum(src, seg, n)
kernel_name = 'mk_macaron_d2_jaxref_r8_506da8'

def setup_inputs(seed: int=0):
    np.random.seed(seed)
    _w = jnp.asarray

    def _L0_attn_setup():
        import jax, jax.numpy as jnp
        import numpy as np
        from jax import lax
        D_MODEL = 128
        D_STATE = 16
        D_CONV = 4
        EXPAND = 2
        D_INNER = EXPAND * D_MODEL
        DT_RANK = (D_MODEL + 15) // 16
        B_, T_ = (2, 256)

        def _mamba_forward(x, W_in, conv_w, conv_b, W_xproj, W_dt, b_dt, A_log, D_skip, W_out):
            B, T, D = x.shape
            xz = jnp.einsum('btd,ed->bte', x, W_in)
            x_in, z = (xz[..., :D_INNER], xz[..., D_INNER:])
            x_pad = jnp.pad(x_in, ((0, 0), (D_CONV - 1, 0), (0, 0)))
            xc = lax.conv_general_dilated(x_pad.transpose(0, 2, 1), conv_w[:, None, :], window_strides=(1,), padding='VALID', feature_group_count=D_INNER).transpose(0, 2, 1) + conv_b
            u = jax.nn.silu(xc)
            x_dbc = jnp.einsum('bte,re->btr', u, W_xproj)
            dt_lo = x_dbc[..., :DT_RANK]
            B_ssm = x_dbc[..., DT_RANK:DT_RANK + D_STATE]
            C_ssm = x_dbc[..., DT_RANK + D_STATE:]
            dt = jax.nn.softplus(jnp.einsum('btr,er->bte', dt_lo, W_dt) + b_dt)
            A = -jnp.exp(A_log)

            def step(h, inputs):
                dt_t, B_t, C_t, u_t = inputs
                dA = jnp.exp(dt_t[..., None] * A)
                h = h * dA + dt_t[..., None] * B_t[:, None, :] * u_t[..., None]
                y_t = jnp.sum(h * C_t[:, None, :], axis=-1)
                return (h, y_t)
            h0 = jnp.zeros((B, D_INNER, D_STATE), dtype=x.dtype)
            xs = (dt.transpose(1, 0, 2), B_ssm.transpose(1, 0, 2), C_ssm.transpose(1, 0, 2), u.transpose(1, 0, 2))
            _, ys = lax.scan(step, h0, xs)
            y = ys.transpose(1, 0, 2) + u * D_skip
            y = y * jax.nn.silu(z)
            return jnp.einsum('bte,de->btd', y, W_out)
        key = jax.random.key(seed)
        ks = jax.random.split(key, 10)
        s = 0.02
        x = jax.random.normal(ks[0], (B_, T_, D_MODEL), dtype=jnp.float32)
        W_in = jax.random.normal(ks[1], (2 * D_INNER, D_MODEL), dtype=jnp.float32) * s
        conv_w = jax.random.normal(ks[2], (D_INNER, D_CONV), dtype=jnp.float32) * s
        conv_b = jnp.zeros((D_INNER,), dtype=jnp.float32)
        W_xproj = jax.random.normal(ks[3], (DT_RANK + 2 * D_STATE, D_INNER), dtype=jnp.float32) * s
        W_dt = jax.random.normal(ks[4], (D_INNER, DT_RANK), dtype=jnp.float32) * s
        b_dt = jax.random.normal(ks[5], (D_INNER,), dtype=jnp.float32) * s
        A_log = jnp.log(jnp.broadcast_to(jnp.arange(1, D_STATE + 1, dtype=jnp.float32), (D_INNER, D_STATE)))
        D_skip = jnp.ones((D_INNER,), dtype=jnp.float32)
        W_out = jax.random.normal(ks[6], (D_MODEL, D_INNER), dtype=jnp.float32) * s
        return {'x': x, 'W_in': W_in, 'conv_w': conv_w, 'conv_b': conv_b, 'W_xproj': W_xproj, 'W_dt': W_dt, 'b_dt': b_dt, 'A_log': A_log, 'D_skip': D_skip, 'W_out': W_out}
    _L0_attn_in = _L0_attn_setup()

    def _L0_ffn_setup():
        import jax, jax.numpy as jnp
        import numpy as np
        DIM = 128
        NUM_EXPERTS = 8
        TOP_K = 2
        HIDDEN = int(DIM * 1.5)
        key = jax.random.key(seed)
        k_x, k_r, k_w1, k_w2, k_w3 = jax.random.split(key, 5)
        B, T = (2, 512)
        s_in = 1.0 / np.sqrt(DIM)
        s_h = 1.0 / np.sqrt(HIDDEN)
        return {'x': jax.random.normal(k_x, (B, T, DIM), dtype=jnp.float32), 'Wr': jax.random.uniform(k_r, (DIM, NUM_EXPERTS), minval=-s_in, maxval=s_in, dtype=jnp.float32), 'W1': jax.random.uniform(k_w1, (NUM_EXPERTS, DIM, HIDDEN), minval=-s_in, maxval=s_in, dtype=jnp.float32), 'W2': jax.random.uniform(k_w2, (NUM_EXPERTS, HIDDEN, DIM), minval=-s_h, maxval=s_h, dtype=jnp.float32), 'W3': jax.random.uniform(k_w3, (NUM_EXPERTS, DIM, HIDDEN), minval=-s_in, maxval=s_in, dtype=jnp.float32)}
    _L0_ffn_in = _L0_ffn_setup()

    def _L1_attn_setup():
        import jax, jax.numpy as jnp
        import numpy as np
        EPS = 1e-08

        def unit_projection(x):
            f = jnp.fft.fft(x)
            f = f / (jnp.abs(f) + EPS)
            return jnp.fft.ifft(f).real

        def bind(a, b):
            return jnp.fft.ifft(jnp.fft.fft(a) * jnp.fft.fft(b)).real

        def unbind(s, a):
            return jnp.fft.ifft(jnp.fft.fft(s) * jnp.conj(jnp.fft.fft(a))).real
        key = jax.random.key(seed)
        B, S, D = (4, 512, 128)
        ks = jax.random.split(key, 7)
        scale = 1.0 / np.sqrt(D)
        x = jax.random.normal(ks[0], (B, S, D), dtype=jnp.float32)
        Wq = jax.random.uniform(ks[1], (D, D), jnp.float32, -scale, scale)
        bq = jax.random.uniform(ks[2], (D,), jnp.float32, -scale, scale)
        Wk = jax.random.uniform(ks[3], (D, D), jnp.float32, -scale, scale)
        bk = jax.random.uniform(ks[4], (D,), jnp.float32, -scale, scale)
        Wv = jax.random.uniform(ks[5], (D, D), jnp.float32, -scale, scale)
        bv = jax.random.uniform(ks[6], (D,), jnp.float32, -scale, scale)
        return {'x': x, 'Wq': Wq, 'bq': bq, 'Wk': Wk, 'bk': bk, 'Wv': Wv, 'bv': bv}
    _L1_attn_in = _L1_attn_setup()

    def _L1_ffn_setup():
        import jax, jax.numpy as jnp
        import numpy as np
        D, H, E, K, S = (128, 256, 8, 2, 1)
        B, L = (4, 256)
        key = jax.random.key(seed)
        ks = jax.random.split(key, 9)
        std = 0.02
        return {'x': jax.random.normal(ks[0], (B, L, D), dtype=jnp.float32), 'router_w': jax.random.normal(ks[1], (E, D), dtype=jnp.float32) * std, 'experts_bias': jnp.zeros((E,), dtype=jnp.float32), 'w1': jax.random.normal(ks[2], (E, D, H), dtype=jnp.float32) * std, 'w3': jax.random.normal(ks[3], (E, D, H), dtype=jnp.float32) * std, 'w2': jax.random.normal(ks[4], (E, H, D), dtype=jnp.float32) * std, 'sw1': jax.random.normal(ks[5], (S, D, H), dtype=jnp.float32) * std, 'sw3': jax.random.normal(ks[6], (S, D, H), dtype=jnp.float32) * std, 'sw2': jax.random.normal(ks[7], (S, H, D), dtype=jnp.float32) * std}
    _L1_ffn_in = _L1_ffn_setup()
    _d = {'L0_attn_x': _L0_attn_in['x'], 'L0_attn_W_in': _L0_attn_in['W_in'], 'L0_attn_conv_w': _L0_attn_in['conv_w'], 'L0_attn_conv_b': _L0_attn_in['conv_b'], 'L0_attn_W_xproj': _L0_attn_in['W_xproj'], 'L0_attn_W_dt': _L0_attn_in['W_dt'], 'L0_attn_b_dt': _L0_attn_in['b_dt'], 'L0_attn_A_log': _L0_attn_in['A_log'], 'L0_attn_D_skip': _L0_attn_in['D_skip'], 'L0_attn_W_out': _L0_attn_in['W_out'], 'L0_ffn_Wr': _L0_ffn_in['Wr'], 'L0_ffn_W1': _L0_ffn_in['W1'], 'L0_ffn_W2': _L0_ffn_in['W2'], 'L0_ffn_W3': _L0_ffn_in['W3'], 'L1_attn_Wq': _L1_attn_in['Wq'], 'L1_attn_bq': _L1_attn_in['bq'], 'L1_attn_Wk': _L1_attn_in['Wk'], 'L1_attn_bk': _L1_attn_in['bk'], 'L1_attn_Wv': _L1_attn_in['Wv'], 'L1_attn_bv': _L1_attn_in['bv'], 'L1_ffn_router_w': _L1_ffn_in['router_w'], 'L1_ffn_experts_bias': _L1_ffn_in['experts_bias'], 'L1_ffn_w1': _L1_ffn_in['w1'], 'L1_ffn_w3': _L1_ffn_in['w3'], 'L1_ffn_w2': _L1_ffn_in['w2'], 'L1_ffn_sw1': _L1_ffn_in['sw1'], 'L1_ffn_sw3': _L1_ffn_in['sw3'], 'L1_ffn_sw2': _L1_ffn_in['sw2']}
    _x0 = _d['L0_attn_x']
    _d['L0_attn_x'] = jax.random.normal(jax.random.fold_in(jax.random.key(seed), 1), (8, 512, 128), dtype=_x0.dtype)
    del _x0
    return _d

def reference(L0_attn_x, L0_attn_W_in, L0_attn_conv_w, L0_attn_conv_b, L0_attn_W_xproj, L0_attn_W_dt, L0_attn_b_dt, L0_attn_A_log, L0_attn_D_skip, L0_attn_W_out, L0_ffn_Wr, L0_ffn_W1, L0_ffn_W2, L0_ffn_W3, L1_attn_Wq, L1_attn_bq, L1_attn_Wk, L1_attn_bk, L1_attn_Wv, L1_attn_bv, L1_ffn_router_w, L1_ffn_experts_bias, L1_ffn_w1, L1_ffn_w3, L1_ffn_w2, L1_ffn_sw1, L1_ffn_sw3, L1_ffn_sw2):

    def _L0_attn_ref(x, W_in, conv_w, conv_b, W_xproj, W_dt, b_dt, A_log, D_skip, W_out):
        import jax, jax.numpy as jnp
        import numpy as np
        from jax import lax
        D_MODEL = 128
        D_STATE = 16
        D_CONV = 4
        EXPAND = 2
        D_INNER = EXPAND * D_MODEL
        DT_RANK = (D_MODEL + 15) // 16
        B_, T_ = (2, 256)

        def _mamba_forward(x, W_in, conv_w, conv_b, W_xproj, W_dt, b_dt, A_log, D_skip, W_out):
            B, T, D = x.shape
            xz = jnp.einsum('btd,ed->bte', x, W_in)
            x_in, z = (xz[..., :D_INNER], xz[..., D_INNER:])
            x_pad = jnp.pad(x_in, ((0, 0), (D_CONV - 1, 0), (0, 0)))
            xc = lax.conv_general_dilated(x_pad.transpose(0, 2, 1), conv_w[:, None, :], window_strides=(1,), padding='VALID', feature_group_count=D_INNER).transpose(0, 2, 1) + conv_b
            u = jax.nn.silu(xc)
            x_dbc = jnp.einsum('bte,re->btr', u, W_xproj)
            dt_lo = x_dbc[..., :DT_RANK]
            B_ssm = x_dbc[..., DT_RANK:DT_RANK + D_STATE]
            C_ssm = x_dbc[..., DT_RANK + D_STATE:]
            dt = jax.nn.softplus(jnp.einsum('btr,er->bte', dt_lo, W_dt) + b_dt)
            A = -jnp.exp(A_log)

            def step(h, inputs):
                dt_t, B_t, C_t, u_t = inputs
                dA = jnp.exp(dt_t[..., None] * A)
                h = h * dA + dt_t[..., None] * B_t[:, None, :] * u_t[..., None]
                y_t = jnp.sum(h * C_t[:, None, :], axis=-1)
                return (h, y_t)
            h0 = jnp.zeros((B, D_INNER, D_STATE), dtype=x.dtype)
            xs = (dt.transpose(1, 0, 2), B_ssm.transpose(1, 0, 2), C_ssm.transpose(1, 0, 2), u.transpose(1, 0, 2))
            _, ys = lax.scan(step, h0, xs)
            y = ys.transpose(1, 0, 2) + u * D_skip
            y = y * jax.nn.silu(z)
            return jnp.einsum('bte,de->btd', y, W_out)
        return _mamba_forward(x, W_in, conv_w, conv_b, W_xproj, W_dt, b_dt, A_log, D_skip, W_out)

    def _L0_ffn_ref(x, Wr, W1, W2, W3):
        import jax, jax.numpy as jnp
        import numpy as np
        DIM = 128
        NUM_EXPERTS = 8
        TOP_K = 2
        HIDDEN = int(DIM * 1.5)
        B, T, C = x.shape
        xf = x.reshape(-1, C)
        gate_logits = xf @ Wr
        w, idx = jax.lax.top_k(gate_logits, TOP_K)
        w = jax.nn.softmax(w, axis=-1)
        comb = jnp.sum(w[:, :, None] * jax.nn.one_hot(idx, NUM_EXPERTS, dtype=w.dtype), axis=1)
        h = jnp.einsum('nc,ech->neh', xf, W1)
        g = jnp.einsum('nc,ech->neh', xf, W3)
        y = jnp.einsum('neh,ehc->nec', jax.nn.silu(h) * g, W2)
        out = jnp.einsum('nec,ne->nc', y, comb)
        return out.reshape(B, T, C)

    def _L1_attn_ref(x, Wq, bq, Wk, bk, Wv, bv):
        import jax, jax.numpy as jnp
        import numpy as np
        EPS = 1e-08

        def unit_projection(x):
            f = jnp.fft.fft(x)
            f = f / (jnp.abs(f) + EPS)
            return jnp.fft.ifft(f).real

        def bind(a, b):
            return jnp.fft.ifft(jnp.fft.fft(a) * jnp.fft.fft(b)).real

        def unbind(s, a):
            return jnp.fft.ifft(jnp.fft.fft(s) * jnp.conj(jnp.fft.fft(a))).real
        query = unit_projection(jnp.einsum('bsd,ed->bse', x, Wq) + bq)
        keys = unit_projection(jnp.einsum('bsd,ed->bse', x, Wk) + bk)
        values = unit_projection(jnp.einsum('bsd,ed->bse', x, Wv) + bv)
        x_k = bind(keys, values)
        s = jnp.cumsum(x_k, axis=1)
        out = unbind(s, query)
        return out

    def _L1_ffn_ref(x, router_w, experts_bias, w1, w3, w2, sw1, sw3, sw2):
        import jax, jax.numpy as jnp
        import numpy as np
        D, H, E, K, S = (128, 256, 8, 2, 1)
        B, L = (4, 256)
        b, l, d = x.shape
        xf = x.reshape(-1, d)
        sg = jnp.einsum('td,sdh->tsh', xf, sw1)
        su = jnp.einsum('td,sdh->tsh', xf, sw3)
        shared_out = jnp.einsum('tsh,shd->td', jax.nn.silu(sg) * su, sw2)
        logits = xf @ router_w.T + experts_bias
        rw, sel = jax.lax.top_k(logits, K)
        rw = jax.nn.softmax(rw.astype(jnp.float32), axis=-1).astype(x.dtype)
        cw = (jax.nn.one_hot(sel, E, dtype=x.dtype) * rw[..., None]).sum(axis=1)
        g = jnp.einsum('td,edh->teh', xf, w1)
        u = jnp.einsum('td,edh->teh', xf, w3)
        eo = jax.nn.silu(g) * u
        moe_out = jnp.einsum('te,teh,ehd->td', cw, eo, w2)
        return (moe_out + shared_out).reshape(b, l, d)
    x = L0_attn_x
    x = x + 0.5 * _L0_ffn_ref(_layernorm(x, axis=-1), L0_ffn_Wr, L0_ffn_W1, L0_ffn_W2, L0_ffn_W3)
    x = x + _L0_attn_ref(_layernorm(x, axis=-1), L0_attn_W_in, L0_attn_conv_w, L0_attn_conv_b, L0_attn_W_xproj, L0_attn_W_dt, L0_attn_b_dt, L0_attn_A_log, L0_attn_D_skip, L0_attn_W_out)
    x = x + 0.5 * _L0_ffn_ref(_layernorm(x, axis=-1), L0_ffn_Wr, L0_ffn_W1, L0_ffn_W2, L0_ffn_W3)
    x = x + 0.5 * _L1_ffn_ref(_layernorm(x, axis=-1), L1_ffn_router_w, L1_ffn_experts_bias, L1_ffn_w1, L1_ffn_w3, L1_ffn_w2, L1_ffn_sw1, L1_ffn_sw3, L1_ffn_sw2)
    x = x + _L1_attn_ref(_layernorm(x, axis=-1), L1_attn_Wq, L1_attn_bq, L1_attn_Wk, L1_attn_bk, L1_attn_Wv, L1_attn_bv)
    x = x + 0.5 * _L1_ffn_ref(_layernorm(x, axis=-1), L1_ffn_router_w, L1_ffn_experts_bias, L1_ffn_w1, L1_ffn_w3, L1_ffn_w2, L1_ffn_sw1, L1_ffn_sw3, L1_ffn_sw2)
    return x

_drawn_inputs = setup_inputs


def setup_inputs(seed=0):
    import zlib

    import numpy as np

    out = dict(_drawn_inputs(seed))
    spreads = {'L0_attn_conv_b': (0.0, 0.8),
     'L0_attn_D_skip': (1.0, 0.6),
     'L1_ffn_experts_bias': (0.0, 0.773)}
    factors = {'L0_attn_W_in': 6.665,
     'L0_attn_conv_w': 8.0,
     'L0_attn_W_xproj': 8.0,
     'L0_attn_W_dt': 8.0,
     'L0_attn_b_dt': 8.0,
     'L0_attn_A_log': 8.0,
     'L0_attn_W_out': 5.389,
     'L1_ffn_router_w': 6.289,
     'L1_ffn_w1': 5.294,
     'L1_ffn_w3': 5.427,
     'L1_ffn_w2': 5.303,
     'L1_ffn_sw1': 3.96,
     'L1_ffn_sw3': 4.025,
     'L1_ffn_sw2': 3.897}
    for name, (base, spread) in spreads.items():
        noise = np.random.default_rng([zlib.crc32(name.encode()), seed]).standard_normal(out[name].shape)
        drawn = base * np.exp(spread * noise) if base else spread * noise
        out[name] = jnp.asarray(drawn.astype(out[name].dtype))
    for name, factor in factors.items():
        out[name] = (out[name] * factor).astype(out[name].dtype)
    return out
```

```python
import concourse.bass as bass
from concourse import mybir
from contextlib import ExitStack
import numpy as np

BATCH, SEQ, DIM = 8, 512, 128
P = 128
TILES = SEQ // P
INNER, HALVES, STATES, TAPS, RANK = 256, 2, 16, 4, 8
EXPERTS = 8
HID0, HID1 = 192, 256
BLOCKS0 = EXPERTS * HID0 // P
BLOCKS1 = (EXPERTS + 1) * HID1 // P
GATES = EXPERTS + 1
PARTS = 3
REAL, IMAG = DIM // 2 + 1, DIM // 2 - 1
LN_EPS, MAG_EPS = 1e-5, 1e-8

COL, _at = {}, 0
for _name, _w in (("r0", EXPERTS), ("r1", EXPERTS), ("up0", BLOCKS0 * P), ("gate0", BLOCKS0 * P),
                  ("down0", BLOCKS0 * P), ("in", 2 * INNER), ("up1", BLOCKS1 * P),
                  ("gate1", BLOCKS1 * P), ("down1", BLOCKS1 * P)):
    COL[_name], _at = _at, _at + _w
SPLIT_COLS = _at
CHUNKS = 8
CHUNK = SPLIT_COLS // CHUNKS

CALLS = {0: dict(layer=0, xin="xb", xout="xc", set=0), 1: dict(layer=1, xin="xe", xout="xe", set=1),
         2: dict(layer=1, xin="xc", xout="xc", set=0), 3: dict(layer=0, xin="xl", xout="xa", set=1)}
MIXER_SET = 2
BLOCKS = (BLOCKS0, BLOCKS1)
HG, RING, LAG = 2, 3, 2
UNITS = HALVES * STATES
DECAY_RING, SCAN_RING = 8, 5


def selector_at(layer, k):
    if layer == 1:
        return k // 2 * P
    pair, r = divmod(k, 3)
    return (2 * pair * P, 2 * pair * P + P // 2, (2 * pair + 1) * P)[r]




class Step:

    def __init__(self, kind, c=None, k=None, n=None, t=None, src=None, set=None, layer=None):
        self.kind, self.c, self.k, self.n, self.t = kind, c, k, n, t
        self.src, self.set, self.layer = src, set, layer
        self.x_misc = self.x_mb = 0


def prep_steps(c):
    about = dict(src=CALLS[c]["xin"], set=CALLS[c]["set"], layer=CALLS[c]["layer"])
    return [Step(k, **about) for k in ("ln_a", "ln_b", "ln_c", "rt_a", "rt_b", "rt_c")]


def mamba_steps():
    about = dict(src="xa", set=MIXER_SET)
    m = [Step(k, **about) for k in ("ln_a", "ln_b", "ln_c")]
    m += [Step(k) for k in ("m_in", "m_conv", "m_xp", "m_bc", "m_dt", "m_sp")]
    for n in range(STATES + 2):
        if n % 2 == 0 and n < STATES:
            m.append(Step("m_exp", n=n))
        m += [Step("m_even", n=n), Step("m_odd", n=n)]
    return m + [Step(k) for k in ("m_z", "m_gate", "m_out")]


def attn_steps():
    about = dict(src="xc", set=MIXER_SET)
    return [Step(k, **about) for k in ("ln_a", "ln_b", "ln_c")] + \
        [Step("a_f", t=t) for t in range(TILES)] + \
        [Step(k) for k in ("a_mag", "a_kv", "a_cum", "a_o", "a_t", "a_i")]


def segment_steps(calls, mamba, attn, prep_next):
    steps = []
    mixer = mamba_steps() if mamba else []
    late = (attn_steps() if attn else []) + (prep_steps(0) if prep_next else [])
    before_3 = sum(BLOCKS[CALLS[c]["layer"]] for c in calls if c != 3)
    mixer_slots = before_3 + 1 if before_3 else BLOCKS0
    slot, pending = 0, None
    if calls and calls[0] != 0:
        steps += prep_steps(calls[0])
    for j, c in enumerate(calls):
        layer = CALLS[c]["layer"]
        blocks = BLOCKS[layer]
        follow = calls[j + 1] if j + 1 < len(calls) else None
        waits = follow is not None and CALLS[follow]["xin"] == CALLS[c]["xout"]
        chain = prep_steps(follow) if follow is not None and not waits else []
        for k in range(blocks):
            steps.append(Step("up", c=c, k=k))
            steps.append(Step("cb", c=c, k=k))
            if k >= 1:
                steps.append(Step("ac", c=c, k=k - 1))
            if k >= LAG:
                steps.append(Step("down", c=c, k=k - LAG))
            if k == 1 and pending is not None:
                steps.append(Step("yt", c=pending))
                pending = None
            if chain and k >= 3:
                steps.append(chain.pop(0))
            if mixer:
                for _ in range(-(-len(mixer) // max(1, mixer_slots - slot))):
                    steps.append(mixer.pop(0))
            elif c == 3 and late and k >= 2:
                for _ in range(-(-len(late) // max(1, blocks - k))):
                    steps.append(late.pop(0))
            slot += 1
        steps.append(Step("ac", c=c, k=blocks - 1))
        steps += [Step("down", c=c, k=k) for k in range(blocks - LAG, blocks)]
        steps += chain
        steps.append(Step("ye", c=c))
        pending = c
        if waits:
            steps.append(Step("yt", c=c))
            pending = None
            steps += prep_steps(follow)
    if pending is not None:
        steps.append(Step("yt", c=pending))
    return number(steps + mixer + late, calls)


def number(steps, calls):
    misc = mb = mc = blocks = 0
    has_out = 1 in calls
    first, scaled, x_at, c_at, x_by = {}, {}, {}, {}, {}
    nos = {}
    for s in steps:
        s.misc, s.mb, s.mc, s.has_out = misc, mb, mc, has_out
        kind = s.kind
        s.no = nos.get(kind, 0)
        nos[kind] = s.no + 1
        if s.c is not None:
            s.layer, s.set = CALLS[s.c]["layer"], CALLS[s.c]["set"]
            s.nth = calls.index(s.c)
            if kind == "up" and s.k == 0:
                first[s.c] = blocks
            s.b = first[s.c] + (s.k if s.k is not None else BLOCKS[s.layer])
            blocks += kind == "up"
        if kind == "cb":
            scaled[s.b] = misc + 1
        if kind == "ac":
            s.scaled = scaled[s.b]
        if kind == "ln_a":
            assert nos["ln_a"] - nos.get("ln_c", 0) <= 2
            s.x_misc, s.x_mb = x_by.get(s.src, (0, 0))
        if kind in ("ln_b", "ln_c"):
            assert [t.src for t in steps if t.kind == kind][s.no] == \
                [t.src for t in steps if t.kind == "ln_a"][s.no]
        if kind == "ln_c":
            x_at[s.set] = misc + 1
        if kind == "rt_c":
            c_at[s.set] = misc + 1
        if kind in ("up", "rt_a"):
            s.x_at = x_at.get(s.set, 0)
        if kind in ("m_in", "m_z", "a_f"):
            s.x_at = x_at[MIXER_SET]
        if kind == "cb":
            s.c_at = c_at.get(s.set, 0)
        if kind == "yt":
            s.xin, s.xout = CALLS[s.c]["xin"], CALLS[s.c]["xout"]
            s.x_misc, s.x_mb = x_by.get(s.xin, (0, 0))
            x_by[s.xout] = (misc + 1, 0)
        if kind in ("m_out", "a_i"):
            s.xin, s.xout = ("xa", "xb") if kind == "m_out" else ("xc", "xe")
            s.x_misc, s.x_mb = x_by.get(s.xin, (0, 0))
            x_by[s.xout] = (0, mb + 1)
        misc += kind in ("ln_c", "rt_a", "rt_c", "cb", "yt")
        mb += kind in ("m_in", "m_z", "m_dt", "m_xp", "m_out", "a_cum", "a_i") or \
            (kind == "m_even" and s.n < STATES) or (kind == "a_f" and s.t % 2 == 0)
        mc += kind in ("m_in", "m_z", "m_dt", "a_t") or \
            (kind == "m_odd" and 1 <= s.n <= STATES) or (kind == "a_f" and s.t % 2 == 1)
    return steps


def macaron_kernel(nc, x_dram, split_dram, proj_dram, xproj_dram, wdt_dram, wout_dram, vec_dram,
                   bias_dram, const_dram, identb_dram, sel_dram, selbc_dram, out_dram):
    f32, r32, bf16, u32 = mybir.dt.float32, mybir.dt.float32r, mybir.dt.bfloat16, mybir.dt.uint32
    ALU, ACT = mybir.AluOpType, mybir.ActivationFunctionType

    ctx = ExitStack()
    with ctx:
        def sb(name, shape, dt=f32):
            return ctx.enter_context(nc.sbuf_tensor(name, shape, dt))

        def bank(name):
            return ctx.enter_context(nc.psum_tensor(name, [P, SEQ], f32))

        w_hi, w_lo = sb("w_hi", [P, SPLIT_COLS], r32), sb("w_lo", [P, SPLIT_COLS], r32)
        wf_hi, wf_lo = sb("wf_hi", [P, 3 * DIM], r32), sb("wf_lo", [P, 3 * DIM], r32)
        spec_bias = sb("spec_bias", [P, 3 * DIM])
        xproj = sb("xproj", [P, HALVES, P])
        wdt = sb("wdt", [RANK, INNER])
        wout = sb("wout", [P, HALVES, DIM])
        vec = sb("vec", [P, HALVES, TAPS + STATES + 3])
        conv_w, a_log = vec[:, :, 0:TAPS], vec[:, :, TAPS:TAPS + STATES]
        conv_b, b_dt, d_skip = (vec[:, :, TAPS + STATES + j:TAPS + STATES + j + 1] for j in range(3))
        a_neg = sb("a_neg", [P, HALVES, STATES])
        const = sb("const", [P, 4 * P + EXPERTS])
        ident, tri, idft, ones = (const[:, j * P:(j + 1) * P] for j in range(4))
        iota = const[:, 4 * P:4 * P + EXPERTS]
        identb = sb("identb", [P, P], bf16)
        sel = sb("sel", [PARTS * GATES, GATES * P], bf16)
        selbc = sb("selbc", [PARTS * 32, STATES * P], bf16)
        router_bias = sb("router_bias", [P, 2, EXPERTS])
        minus_half = sb("minus_half", [P, TILES])

        X = {n: sb(n, [P, TILES, DIM]) for n in ("xl", "xa", "xb", "xc", "xe")}

        stats = sb("stats", [P, TILES, 6])
        moments = sb("moments", [P, 2, TILES, 2])
        var_eps = sb("var_eps", [P, TILES])
        rstd = sb("rstd", [P, 2, TILES])
        xn = sb("xn", [P, 2, TILES, DIM])
        xt_hi, xt_lo = sb("xt_hi", [P, 3, SEQ], r32), sb("xt_lo", [P, 3, SEQ], r32)
        logits = sb("logits", [P, TILES, EXPERTS])
        top = sb("top", [P, TILES, 8])
        top_at = sb("top_at", [P, TILES, 8], u32)
        top_f = sb("top_f", [P, TILES, 2])
        gap, th = sb("gap", [P, TILES]), sb("th", [P, TILES])
        pair_w = sb("pair_w", [P, TILES, 2])
        hot = sb("hot", [P, TILES, 2, EXPERTS])
        comb = sb("comb", [P, TILES, GATES])
        rest = sb("rest", [P, TILES, GATES])
        comb3 = sb("comb3", [P, TILES, PARTS, GATES], bf16)
        comb_t = sb("comb_t", [PARTS * GATES, 2, SEQ], bf16)

        val = sb("val", [P, RING, SEQ])
        act_hi, act_lo = sb("act_hi", [P, RING, SEQ], r32), sb("act_lo", [P, RING, SEQ], r32)
        y_t = sb("y_t", [P, SEQ])

        u = sb("u", [P, HALVES, SEQ])
        dt = sb("dt", [P, HALVES, SEQ])
        dtu = sb("dtu", [P, HALVES, SEQ])
        decay = sb("decay", [P, DECAY_RING, SEQ])
        b_sb = sb("b_sb", [P, 2, SEQ])
        scan = sb("scan", [P, SCAN_RING, SEQ])
        bc3 = sb("bc3", [PARTS * 32, 2, SEQ], bf16)

        decay_flat = decay[:, :, :].rearrange("p a b -> p (a b)")
        scan_flat = scan[:, :, :].rearrange("p a b -> p (a b)")
        staging = decay_flat[:, 0:2 * CHUNK]
        proj = scan_flat[:, 0:4 * DIM + 3]
        dft = proj[:, 3 * DIM:4 * DIM]
        bias_cols = scan_flat[:, 5 * DIM:8 * DIM]
        wide = HALVES * SEQ
        x_in = decay_flat[:, 0:HALVES * (TAPS - 1 + SEQ)].rearrange("p (h t) -> p h t", h=HALVES)
        conv = [decay_flat[:, j * wide:(j + 1) * wide].rearrange("p (h t) -> p h t", h=HALVES)
                for j in (2, 3)]
        dt_pre, neg_abs, dt_exp = (decay_flat[:, j * wide:(j + 1) * wide]
                                   .rearrange("p (h t) -> p h t", h=HALVES) for j in (0, 1, 2))
        bc = scan_flat[0:STATES, 0:2 * SEQ].rearrange("p (j t) -> p j t", j=2)
        bc_rest = scan_flat[0:STATES, 2 * SEQ:4 * SEQ].rearrange("p (j t) -> p j t", j=2)
        bc_mid = scan_flat[0:STATES, 4 * SEQ:5 * SEQ].bitcast(bf16).rearrange("p (j t) -> p j t", j=2)
        dt_lo = b_sb[0:RANK, 0, :]

        def piece(flat, at, *dims):
            n = int(np.prod(dims))
            ap = flat[:, at:at + n]
            if len(dims) == 2:
                return ap.rearrange("p (a b) -> p a b", a=dims[0])
            return ap.rearrange("p (a b c) -> p a b c", a=dims[0], b=dims[1])

        spec = piece(scan_flat, 0, TILES, 3, DIM)
        kv = piece(scan_flat, 3 * SEQ, TILES, DIM)
        o_t = scan_flat[:, 4 * SEQ:5 * SEQ]
        power = piece(decay_flat, 0, TILES, 3, DIM)
        spec_out = piece(decay_flat, 0, TILES, DIM)
        prod = [piece(decay_flat, (3 + j) * SEQ // 1, TILES, IMAG) for j in range(2)]
        mag = piece(decay_flat, 5 * SEQ, TILES, 3, REAL)
        rq = piece(decay_flat, 5 * SEQ + 3 * TILES * REAL, TILES, REAL)
        rkv = piece(decay_flat, 5 * SEQ + 4 * TILES * REAL, TILES, REAL)

        h_ps = [bank(f"h_ps{j}") for j in range(HG)]
        g_ps = [bank(f"g_ps{j}") for j in range(HG)]
        y_ps, misc, m_b, m_c = bank("y_ps"), bank("misc"), bank("m_b"), bank("m_c")
        misc_bf = misc[:, :].bitcast(bf16)

        (h_full, g_full, silu_done, act_done, hi_done, lo_done, down_done, y_copied,
         misc_full, misc_free, mb_full, mb_free, mc_full, mc_free, ln_stats, ln_rstd, ln_xn,
         ln_hi, gap_ready, th_ready, comb_ready, xl_loaded, xe_final, out_stored,
         pad_zeroed, conv_done, u_ready, dtlo_ready, bc_copied, bc_hi, bc_rest_ready, bc_mid_ready,
         bc_ready, bc_parts, negabs_ready, log_ready, dt_ready, dtu_ready, y_started,
         decay_ready, drive_ready, scan_done, hc_even, y_added, yz_ready, sq_ready,
         power_ready, mag_ready, mags_ready, kv_ready, out_spec_ready, dve_chain, act_chain,
         pool_chain, arrived) = of_segment = [ctx.enter_context(nc.semaphore(name)) for name in (
            "h_full", "g_full", "silu_done", "act_done", "hi_done", "lo_done", "down_done",
            "y_copied", "misc_full", "misc_free", "mb_full", "mb_free", "mc_full",
            "mc_free", "ln_stats", "ln_rstd", "ln_xn", "ln_hi", "gap_ready", "th_ready",
            "comb_ready", "xl_loaded", "xe_final", "out_stored", "pad_zeroed", "conv_done",
            "u_ready", "dtlo_ready", "bc_copied", "bc_hi", "bc_rest_ready", "bc_mid_ready", "bc_ready",
            "bc_parts", "negabs_ready", "log_ready", "dt_ready", "dtu_ready", "y_started",
            "decay_ready", "drive_ready", "scan_done", "hc_even", "y_added", "yz_ready",
            "sq_ready", "power_ready", "mag_ready", "mags_ready", "kv_ready",
            "out_spec_ready", "dve_chain", "act_chain", "pool_chain", "arrived")]
        go_sync, go_act, go_dve, go_pe = go = [ctx.enter_context(nc.semaphore(f"go_{e}"))
                                               for e in ("sync", "act", "dve", "pe")]
        w_loaded = [ctx.enter_context(nc.semaphore(f"w_loaded{j}")) for j in range(2)]
        small_loaded = ctx.enter_context(nc.semaphore("small_loaded"))
        block = ctx.enter_context(nc.Block())

        class Count:

            def __init__(self):
                self.n = 0

            def up(self):
                self.n += 1
                return self.n

        def preloaded(i):
            return isinstance(i, int) and i == -1

        def steps_of(i):
            calls = [c for c, on in ((0, 1 <= i <= BATCH), (1, 2 <= i <= BATCH + 1),
                                     (2, 1 <= i <= BATCH), (3, -1 <= i <= BATCH - 2)) if on]
            mamba = 0 <= i < BATCH
            return segment_steps(calls, mamba, 1 <= i <= BATCH, mamba)

        LOOP_FROM, LOOP_TO = 2, BATCH - 1

        def run(e, segment):
            for i in (-1, 0, 1):
                segment(i, steps_of(i))
            full = steps_of(LOOP_FROM)
            with e.Fori(LOOP_FROM, LOOP_TO) as i:
                segment(i, full)
            for i in range(LOOP_TO, BATCH + 2):
                segment(i, steps_of(i))

        small = [(const[:, :], const_dram), (proj, proj_dram), (vec[:, :, :], vec_dram),
                 (wdt[:, :], wdt_dram), (xproj[:, :, :], xproj_dram), (wout[:, :, :], wout_dram),
                 (identb[:, :], identb_dram), (sel[:, :], sel_dram), (selbc[:, :], selbc_dram),
                 (router_bias[:, 1, :], bias_dram.partition_broadcast(P)),
                 (X["xl"][:, :, :], x_dram[0].rearrange("(t p) d -> p t d", p=P))]

        @block.sync
        def _(sp):
            for j in range(CHUNKS):
                if j >= 2:
                    sp.wait_ge(lo_done, j - 1)
                sp.dma_start(staging[:, (j % 2) * CHUNK:(j % 2 + 1) * CHUNK],
                             split_dram[:, j * CHUNK:(j + 1) * CHUNK]).then_inc(w_loaded[j % 2], 16)
                if j == 1:
                    for dst, src in small:
                        sp.dma_start(dst, src).then_inc(small_loaded, 16)
            sp.drain()
            sp.sem_inc(arrived, 1)
            sp.wait_ge(go_sync, 1)
            sp.sem_clear(go_sync)

            def segment(i, steps):
                kinds = {(s.kind, s.c) for s in steps}
                if ("up", 3) in kinds and not preloaded(i):
                    sp.dma_start(X["xl"][:, :, :],
                                 x_dram[i + 1].rearrange("(t p) d -> p t d", p=P)) \
                        .then_inc(xl_loaded, 16)
                    sp.wait_ge(xl_loaded, 16)
                if ("yt", 1) in kinds:
                    sp.wait_ge(xe_final, 1)
                    sp.dma_start(out_dram[i - 2].rearrange("(t p) d -> p t d", p=P),
                                 X["xe"][:, :, :]).then_inc(out_stored, 16)
                    sp.wait_ge(out_stored, 16)
                sp.drain()
                sp.sem_inc(arrived, 1)
                sp.wait_ge(go_sync, 1)
                sp.sem_clear(go_sync)
            run(sp, segment)

        @block.tensor
        def _(pe):
            def mm3(out, w, x, first, last):
                nc.tensor.matmul(out, w[0], x[0], start=first, stop=False)
                nc.tensor.matmul(out, w[0], x[1], start=False, stop=False)
                return nc.tensor.matmul(out, w[1], x[0], start=False, stop=last)

            def weights(name, k, width=P):
                c = COL[name] + k * width
                return w_hi[:, c:c + width], w_lo[:, c:c + width]

            pe.wait_ge(small_loaded, 16 * len(small))
            pe.wait_ge(bc_copied, 1)
            for j in range(3):
                nc.tensor.matmul(m_b[:, j * DIM:(j + 1) * DIM], proj[:, j * DIM:(j + 1) * DIM], dft,
                                 start=True, stop=True)
            for j in range(3):
                ins = nc.tensor.matmul(m_c[:, j * DIM:(j + 1) * DIM],
                                       bias_cols[:, j * DIM:(j + 1) * DIM], dft, start=True, stop=True)
            ins.then_inc(mb_full, 1)
            pe.drain()
            pe.sem_inc(arrived, 1)
            pe.wait_ge(go_pe, 1)
            pe.sem_clear(go_pe)

            def segment(i, steps):
                for s in steps:
                    k = s.kind
                    if k in ("ln_c", "rt_a", "rt_c", "cb", "yt"):
                        if k == "ln_c":
                            pe.wait_ge(ln_xn, s.no + 1)
                        if k == "rt_c":
                            pe.wait_ge(comb_ready, s.no + 1)
                        if k == "yt":
                            pe.wait_ge(y_copied, s.nth + 1)
                        if k == "rt_a":
                            if s.x_at > 0:
                                pe.wait_ge(misc_free, s.x_at)
                        if k == "cb":
                            if s.c_at > 0:
                                pe.wait_ge(misc_free, s.c_at)
                        if s.misc > 0:
                            pe.wait_ge(misc_free, s.misc)
                        tiles = [slice(t * P, (t + 1) * P) for t in range(TILES)]
                        if k == "ln_c":
                            for t in range(TILES):
                                ins = nc.tensor.transpose(misc[:, tiles[t]], xn[:, s.no % 2, t, :], ident)
                        elif k == "yt":
                            for t in range(TILES):
                                ins = nc.tensor.transpose(misc[:, tiles[t]], y_t[:, tiles[t]], ident)
                        elif k == "rt_a":
                            r = weights(f"r{s.layer}", 0, EXPERTS)
                            for t in range(TILES):
                                ins = mm3(misc[:, t * EXPERTS:(t + 1) * EXPERTS],
                                          (xt_hi[:, s.set, tiles[t]], xt_lo[:, s.set, tiles[t]]), r,
                                          True, True)
                        elif k == "rt_c":
                            for t in range(TILES):
                                ins = nc.tensor.transpose(misc_bf[0:PARTS * GATES, tiles[t]],
                                                          comb3[:, t].rearrange("p a b -> p (a b)"),
                                                          identb[:, :])
                        else:
                            at = selector_at(s.layer, s.k)
                            ins = nc.tensor.matmul(misc[:, :], sel[:, at:at + P], comb_t[:, s.set, :],
                                                   start=True, stop=True)
                        ins.then_inc(misc_full, 1)
                    elif k == "up":
                        xs = xt_hi[:, s.set, :], xt_lo[:, s.set, :]
                        if s.k == 0:
                            if s.x_at > 0:
                                pe.wait_ge(misc_free, s.x_at)
                        if s.b - HG + 1 > 0:
                            pe.wait_ge(silu_done, s.b - HG + 1)
                        mm3(h_ps[s.b % HG][:, :], weights(f"up{s.layer}", s.k), xs, True, True) \
                            .then_inc(h_full, 1)
                        if s.b - HG + 1 > 0:
                            pe.wait_ge(act_done, s.b - HG + 1)
                        mm3(g_ps[s.b % HG][:, :], weights(f"gate{s.layer}", s.k), xs, True, True) \
                            .then_inc(g_full, 1)
                    elif k == "down":
                        if s.k == 0:
                            if s.nth > 0:
                                pe.wait_ge(y_copied, s.nth)
                        pe.wait_ge(lo_done, s.b + 1)
                        mm3(y_ps[:, :], weights(f"down{s.layer}", s.k),
                            (act_hi[:, s.b % RING, :], act_lo[:, s.b % RING, :]),
                            s.k == 0, s.k == BLOCKS[s.layer] - 1).then_inc(down_done, 1)
                    elif k in ("m_in", "m_z"):
                        if s.x_at > 0:
                            pe.wait_ge(misc_free, s.x_at)
                        xs = xt_hi[:, MIXER_SET, :], xt_lo[:, MIXER_SET, :]
                        off = 0 if k == "m_in" else HALVES
                        if s.mb > 0:
                            pe.wait_ge(mb_free, s.mb)
                        mm3(m_b[:, :], weights("in", off), xs, True, True).then_inc(mb_full, 1)
                        if s.mc > 0:
                            pe.wait_ge(mc_free, s.mc)
                        mm3(m_c[:, :], weights("in", off + 1), xs, True, True).then_inc(mc_full, 1)
                    elif k == "m_xp":
                        pe.wait_ge(u_ready, HALVES)
                        if s.mb > 0:
                            pe.wait_ge(mb_free, s.mb)
                        for h in range(HALVES):
                            ins = nc.tensor.matmul(m_b[:, :], xproj[:, h, :], u[:, h, :],
                                                   start=h == 0, stop=h == HALVES - 1)
                        ins.then_inc(mb_full, 1)
                    elif k == "m_dt":
                        pe.wait_ge(dtlo_ready, 1)
                        if s.mb > 0:
                            pe.wait_ge(mb_free, s.mb)
                        nc.tensor.matmul(m_b[:, :], wdt[:, 0:P], dt_lo, start=True, stop=True) \
                            .then_inc(mb_full, 1)
                        if s.mc > 0:
                            pe.wait_ge(mc_free, s.mc)
                        nc.tensor.matmul(m_c[:, :], wdt[:, P:2 * P], dt_lo, start=True, stop=True) \
                            .then_inc(mc_full, 1)
                    elif k == "m_even" and s.n < STATES:
                        pe.wait_ge(bc_parts, 1)
                        pe.wait_ge(bc_ready, 1)
                        if s.mb > 0:
                            pe.wait_ge(mb_free, s.mb)
                        nc.tensor.matmul(m_b[:, :], selbc[:, s.n * P:(s.n + 1) * P], bc3[:, 0, :],
                                         start=True, stop=True).then_inc(mb_full, 1)
                    elif k == "m_odd" and 1 <= s.n <= STATES:
                        if s.mc > 0:
                            pe.wait_ge(mc_free, s.mc)
                        nc.tensor.matmul(m_c[:, :], selbc[:, (s.n - 1) * P:s.n * P], bc3[:, 1, :],
                                         start=True, stop=True).then_inc(mc_full, 1)
                    elif k == "m_out":
                        pe.wait_ge(yz_ready, 1)
                        if s.mb > 0:
                            pe.wait_ge(mb_free, s.mb)
                        for t in range(TILES):
                            for h in range(HALVES):
                                ins = nc.tensor.matmul(m_b[:, t * P:(t + 1) * P],
                                                       u[:, h, t * P:(t + 1) * P], wout[:, h, :],
                                                       start=h == 0, stop=h == HALVES - 1)
                        ins.then_inc(mb_full, 1)
                    elif k == "a_f":
                        if s.x_at > 0:
                            pe.wait_ge(misc_free, s.x_at)
                        ps, full, free, uses = (m_b, mb_full, mb_free, s.mb) if s.t % 2 == 0 \
                            else (m_c, mc_full, mc_free, s.mc)
                        if uses > 0:
                            pe.wait_ge(free, uses)
                        cols = slice(s.t * P, (s.t + 1) * P)
                        mm3(ps[:, 0:3 * DIM], (xt_hi[:, MIXER_SET, cols], xt_lo[:, MIXER_SET, cols]),
                            (wf_hi[:, :], wf_lo[:, :]), True, True).then_inc(full, 1)
                    elif k == "a_cum":
                        pe.wait_ge(kv_ready, 1)
                        if s.mb > 0:
                            pe.wait_ge(mb_free, s.mb)
                        for t in range(TILES):
                            for v in range(t + 1):
                                ins = nc.tensor.matmul(m_b[:, t * P:(t + 1) * P],
                                                       tri if v == t else ones, kv[:, v, :],
                                                       start=v == 0, stop=v == t)
                        ins.then_inc(mb_full, 1)
                    elif k == "a_t":
                        pe.wait_ge(out_spec_ready, 1)
                        if s.mc > 0:
                            pe.wait_ge(mc_free, s.mc)
                        for t in range(TILES):
                            ins = nc.tensor.transpose(m_c[:, t * P:(t + 1) * P], spec_out[:, t, :], ident)
                        ins.then_inc(mc_full, 1)
                    elif k == "a_i":
                        if s.mc > 0:
                            pe.wait_ge(mc_free, s.mc)
                        if s.mb > 0:
                            pe.wait_ge(mb_free, s.mb)
                        for t in range(TILES):
                            ins = nc.tensor.matmul(m_b[:, t * P:(t + 1) * P], o_t[:, t * P:(t + 1) * P],
                                                   idft, start=True, stop=True)
                        ins.then_inc(mb_full, 1)
                pe.drain()
                pe.sem_inc(arrived, 1)
                pe.wait_ge(go_pe, 1)
                pe.sem_clear(go_pe)
            run(pe, segment)

        @block.scalar
        def _(act):
            for j in range(CHUNKS):
                act.wait_ge(w_loaded[j % 2], 16 * (j // 2 + 1))
                nc.scalar.activation(w_hi[:, j * CHUNK:(j + 1) * CHUNK],
                                     staging[:, (j % 2) * CHUNK:(j % 2 + 1) * CHUNK],
                                     ACT.Copy).then_inc(hi_done, 1)
            act.wait_ge(small_loaded, 16 * len(small))
            nc.scalar.activation(a_neg[:, :, :], a_log, ACT.Exp).then_inc(act_chain, 1)
            act.wait_ge(mb_full, 1)
            nc.scalar.activation(wf_hi[:, :], m_b[:, 0:3 * DIM], ACT.Copy).then_inc(ln_hi, 1)
            nc.scalar.activation(spec_bias[:, :], m_c[:, 0:3 * DIM], ACT.Copy)
            act.drain()
            act.sem_inc(arrived, 1)
            act.wait_ge(go_act, 1)
            act.sem_clear(go_act)

            def segment(i, steps):
                for s in steps:
                    k = s.kind
                    if k == "ln_c":
                        act.wait_ge(misc_full, s.misc + 1)
                        nc.scalar.activation(xt_hi[:, s.set, :], misc[:, :], ACT.Copy) \
                            .then_inc(ln_hi, 1)
                    elif k == "rt_a":
                        act.wait_ge(gap_ready, s.no + 1)
                        nc.scalar.activation(th[:, :], gap[:, :], ACT.Tanh, scale=0.5) \
                            .then_inc(th_ready, 1)
                    elif k == "rt_c":
                        act.wait_ge(misc_full, s.misc + 1)
                        nc.scalar.activation(comb_t[:, s.set, :], misc_bf[0:PARTS * GATES, 0:SEQ],
                                             ACT.Copy).then_inc(misc_free, 1)
                    elif k == "up":
                        act.wait_ge(h_full, s.b + 1)
                        if s.b - RING + 1 > 0:
                            act.wait_ge(lo_done, s.b - RING + 1)
                        nc.scalar.activation(val[:, s.b % RING, :], h_ps[s.b % HG][:, :], ACT.Silu) \
                            .then_inc(silu_done, 1)
                    elif k == "ac":
                        act.wait_ge(act_done, s.b + 1)
                        if s.b - RING + 1 > 0:
                            act.wait_ge(down_done, s.b - RING + 1)
                        nc.scalar.activation(act_hi[:, s.b % RING, :], val[:, s.b % RING, :], ACT.Copy) \
                            .then_inc(hi_done, 1)
                    elif k == "ye":
                        if s.b > 0:
                            act.wait_ge(down_done, s.b)
                        nc.scalar.activation(y_t[:, :], y_ps[:, :], ACT.Copy).then_inc(y_copied, 1)
                    elif k in ("m_in", "m_z", "m_dt"):
                        for h, (ps, full, free, uses) in enumerate(((m_b, mb_full, mb_free, s.mb),
                                                                    (m_c, mc_full, mc_free, s.mc))):
                            act.wait_ge(full, uses + 1)
                            if k == "m_in":
                                ins = nc.scalar.activation(x_in[:, h, TAPS - 1:], ps[:, :], ACT.Copy)
                            elif k == "m_z":
                                ins = nc.scalar.activation(dt[:, h, :], ps[:, :], ACT.Silu)
                            else:
                                ins = nc.scalar.activation(dt_pre[:, h, :], ps[:, :], ACT.Identity,
                                                           bias=b_dt[:, h, :])
                            ins.then_inc(free, 1)
                    elif k == "m_conv":
                        for h in range(HALVES):
                            act.wait_ge(conv_done, h + 1)
                            nc.scalar.activation(u[:, h, :], conv[1][:, h, :], ACT.Silu,
                                                 bias=conv_b[:, h, :]).then_inc(u_ready, 1)
                    elif k == "m_xp":
                        act.wait_ge(mb_full, s.mb + 1)
                        nc.scalar.activation(dt_lo, m_b[0:RANK, :], ACT.Copy) \
                            .then_inc(dtlo_ready, 1)
                        nc.scalar.activation(bc[:, 0, :], m_b[32:32 + STATES, :], ACT.Copy) \
                            .then_inc(bc_copied, 1)
                        nc.scalar.activation(bc[:, 1, :], m_b[64:64 + STATES, :], ACT.Copy) \
                            .then_inc(mb_free, 1)
                    elif k == "m_bc":
                        act.wait_ge(bc_copied, 1)
                        if s.mb > 0:
                            act.wait_ge(mb_free, s.mb)
                        nc.scalar.activation(bc3[0:STATES, :, :], bc, ACT.Copy).then_inc(bc_hi, 1)
                        act.wait_ge(bc_rest_ready, 1)
                        nc.scalar.activation(bc_mid, bc_rest, ACT.Copy).then_inc(bc_mid_ready, 1)
                        act.wait_ge(bc_mid_ready, 1)
                        nc.scalar.activation(bc3[32:32 + STATES, :, :], bc_mid, ACT.Copy) \
                            .then_inc(bc_parts, 1)
                    elif k == "m_sp":
                        act.wait_ge(negabs_ready, 1)
                        nc.scalar.activation(dt_exp, neg_abs, ACT.Exp).then_inc(act_chain, 1)
                        act.wait_ge(act_chain, 1)
                        nc.scalar.activation(neg_abs, dt_exp, ACT.Ln, bias=1.0) \
                            .then_inc(log_ready, 1)
                        act.wait_ge(dtu_ready, 1)
                        for h in range(HALVES):
                            nc.scalar.activation(u[:, h, :], u[:, h, :], ACT.Copy,
                                                 scale=d_skip[:, h, :]).then_inc(y_started, 1)
                    elif k == "m_exp":
                        act.wait_ge(dt_ready, 1)
                        act.wait_ge(dtu_ready, 1)
                        for unit in range(2 * s.n, 2 * s.n + 2 * HALVES):
                            n, h = divmod(unit, HALVES)
                            if unit - DECAY_RING + 1 > 0:
                                act.wait_ge(scan_done, unit - DECAY_RING + 1)
                            nc.scalar.activation(decay[:, unit % DECAY_RING, 1:], dt[:, h, 1:], ACT.Exp,
                                                 scale=a_neg[:, h, n:n + 1]) \
                                .then_inc(decay_ready, 1)
                    elif k == "m_even" and s.n < STATES:
                        act.wait_ge(mb_full, s.mb + 1)
                        if 2 * s.n - 2 > 0:
                            act.wait_ge(drive_ready, 2 * s.n - 2)
                        nc.scalar.activation(b_sb[:, s.n % 2, :], m_b[:, :], ACT.Copy) \
                            .then_inc(mb_free, 1)
                    elif k == "a_mag":
                        if s.mb > 0:
                            act.wait_ge(mb_free, s.mb)
                        if s.mc > 0:
                            act.wait_ge(mc_free, s.mc)
                        nc.scalar.activation(power, spec, ACT.Square).then_inc(sq_ready, 1)
                        act.wait_ge(power_ready, 1)
                        nc.scalar.activation(mag, power[:, :, :, 0:REAL], ACT.Sqrt) \
                            .then_inc(mag_ready, 1)
                    elif k == "a_t":
                        act.wait_ge(mc_full, s.mc + 1)
                        nc.scalar.activation(o_t, m_c[:, :], ACT.Copy).then_inc(mc_free, 1)
                act.drain()
                act.sem_inc(arrived, 1)
                act.wait_ge(go_act, 1)
                act.sem_clear(go_act)
            run(act, segment)

        @block.vector
        def _(dve):
            tt, ts, stt = nc.vector.tensor_tensor, nc.vector.tensor_scalar, nc.vector.scalar_tensor_tensor

            nc.vector.memset(comb[:, :, :], 0.5)
            nc.vector.memset(router_bias[:, 0, :], 0.0)
            nc.vector.memset(bc3[:, :, :], 0.0)
            nc.vector.memset(minus_half[:, :], -0.5)
            for j in range(CHUNKS):
                cols = slice(j * CHUNK, (j + 1) * CHUNK)
                dve.wait_ge(hi_done, j + 1)
                tt(w_lo[:, cols], staging[:, (j % 2) * CHUNK:(j % 2 + 1) * CHUNK],
                   w_hi[:, cols].bitcast(f32), ALU.subtract).then_inc(lo_done, 1)
            dve.wait_ge(small_loaded, 16 * len(small))
            for j in range(3):
                ins = ts(bias_cols[:, j * DIM:(j + 1) * DIM], ones, proj[:, 4 * DIM + j:4 * DIM + j + 1],
                         None, ALU.mult)
            ins.then_inc(bc_copied, 1)
            dve.wait_ge(act_chain, 1)
            ts(a_neg[:, :, :], a_neg[:, :, :], -1.0, None, ALU.mult)
            dve.wait_ge(ln_hi, 1)
            tt(wf_lo[:, :], m_b[:, 0:3 * DIM], wf_hi[:, :].bitcast(f32), ALU.subtract)
            dve.drain()
            dve.sem_inc(arrived, 1)
            dve.wait_ge(go_dve, 1)
            dve.sem_clear(go_dve)

            re, im, re1 = slice(0, REAL), slice(REAL, DIM), slice(1, 1 + IMAG)

            def segment(i, steps):
                count = Count()

                for s in steps:
                    k = s.kind
                    if k == "ln_a":
                        if s.x_misc:
                            dve.wait_ge(misc_free, s.x_misc)
                        if s.x_mb:
                            dve.wait_ge(mb_free, s.x_mb)
                        if s.src == "xl" and not preloaded(i):
                            dve.wait_ge(xl_loaded, 16)
                        if s.no - 1 > 0:
                            dve.wait_ge(ln_rstd, s.no - 1)
                        for t in range(TILES):
                            ins = nc.vector.bn_stats(stats[:, t, :], X[s.src][:, t, :])
                        ins.then_inc(dve_chain, 1)
                        dve.wait_ge(dve_chain, count.up())
                        for t in range(TILES):
                            ins = nc.vector.bn_aggr(moments[:, s.no % 2, t, :], stats[:, t, :])
                        ins.then_inc(ln_stats, 1)
                    elif k == "ln_b":
                        dve.wait_ge(ln_rstd, s.no + 1)
                        for t in range(TILES):
                            ins = ts(xn[:, s.no % 2, t, :], X[s.src][:, t, :],
                                     moments[:, s.no % 2, t, 0:1], rstd[:, s.no % 2, t:t + 1],
                                     ALU.subtract, ALU.mult)
                        ins.then_inc(ln_xn, 1)
                    elif k == "ln_c":
                        dve.wait_ge(ln_hi, s.no + 1)
                        tt(xt_lo[:, s.set, :], misc[:, :], xt_hi[:, s.set, :].bitcast(f32), ALU.subtract) \
                            .then_inc(misc_free, 1)
                    elif k == "rt_a":
                        dve.wait_ge(misc_full, s.misc + 1)
                        bias = router_bias[:, s.layer, :].unsqueeze(1).to_broadcast([P, TILES, EXPERTS])
                        tt(logits[:, :, :], misc[:, 0:TILES * EXPERTS]
                           .rearrange("p (t e) -> p t e", t=TILES), bias, ALU.add) \
                            .then_inc(misc_free, 1)
                        dve.wait_ge(misc_free, s.misc + 1)
                        for t in range(TILES):
                            ins = nc.vector.max(top[:, t, :], logits[:, t, :])
                        ins.then_inc(dve_chain, 1)
                        dve.wait_ge(dve_chain, count.up())
                        tt(gap[:, :], top[:, :, 0], top[:, :, 1], ALU.subtract) \
                            .then_inc(gap_ready, 1)
                        for t in range(TILES):
                            ins = nc.vector.max_index(top_at[:, t, :], top[:, t, :], logits[:, t, :])
                        ins.then_inc(dve_chain, 1)
                        dve.wait_ge(dve_chain, count.up())
                        nc.vector.tensor_copy(top_f[:, :, :], top_at[:, :, 0:2]) \
                            .then_inc(dve_chain, 1)
                        count.up()
                    elif k == "rt_b":
                        dve.wait_ge(th_ready, s.no + 1)
                        ts(pair_w[:, :, 0], th[:, :], 0.25, 0.25, ALU.mult, ALU.add)
                        ts(pair_w[:, :, 1], th[:, :], -0.25, 0.25, ALU.mult, ALU.add) \
                            .then_inc(dve_chain, 1)
                        count.up()
                        dve.wait_ge(dve_chain, count.n - 1)
                        every = [P, TILES, 2, EXPERTS]
                        tt(hot[:, :, :, :], iota.unsqueeze(1).unsqueeze(1).to_broadcast(every),
                           top_f[:, :, :].unsqueeze(3).to_broadcast(every), ALU.is_equal) \
                               .then_inc(dve_chain, 1)
                        dve.wait_ge(dve_chain, count.up())
                        tt(hot[:, :, :, :], hot[:, :, :, :],
                           pair_w[:, :, :].unsqueeze(3).to_broadcast(every), ALU.mult) \
                               .then_inc(dve_chain, 1)
                        dve.wait_ge(dve_chain, count.up())
                        tt(comb[:, :, 0:EXPERTS], hot[:, :, 0, :], hot[:, :, 1, :], ALU.add) \
                            .then_inc(dve_chain, 1)
                        dve.wait_ge(dve_chain, count.up())
                        nc.vector.tensor_copy(comb3[:, :, 0, :], comb[:, :, :]) \
                            .then_inc(dve_chain, 1)
                        dve.wait_ge(dve_chain, count.up())
                        tt(rest[:, :, :], comb[:, :, :], comb3[:, :, 0, :], ALU.subtract) \
                            .then_inc(dve_chain, 1)
                        dve.wait_ge(dve_chain, count.up())
                        nc.vector.tensor_copy(comb3[:, :, 1, :], rest[:, :, :]) \
                            .then_inc(dve_chain, 1)
                        dve.wait_ge(dve_chain, count.up())
                        tt(comb3[:, :, 2, :], rest[:, :, :], comb3[:, :, 1, :], ALU.subtract) \
                            .then_inc(comb_ready, 1)
                    elif k == "cb":
                        dve.wait_ge(silu_done, s.b + 1)
                        dve.wait_ge(misc_full, s.misc + 1)
                        r = s.b % RING
                        tt(val[:, r, :], val[:, r, :], misc[:, :], ALU.mult).then_inc(misc_free, 1)
                    elif k == "ac":
                        if s.scaled > 0:
                            dve.wait_ge(misc_free, s.scaled)
                        dve.wait_ge(g_full, s.b + 1)
                        r = s.b % RING
                        tt(val[:, r, :], val[:, r, :], g_ps[s.b % HG][:, :], ALU.mult) \
                            .then_inc(act_done, 1)
                    elif k == "yt":
                        if s.x_misc:
                            dve.wait_ge(misc_free, s.x_misc)
                        if s.x_mb:
                            dve.wait_ge(mb_free, s.x_mb)
                        if s.xin == "xl" and not preloaded(i):
                            dve.wait_ge(xl_loaded, 16)
                        dve.wait_ge(misc_full, s.misc + 1)
                        tt(X[s.xout][:, :, :], X[s.xin][:, :, :],
                           misc[:, :].rearrange("p (t d) -> p t d", t=TILES), ALU.add) \
                            .then_inc(misc_free, 1)
                        if s.c == 1:
                            dve.wait_ge(misc_free, s.misc + 1)
                            dve.sem_inc(xe_final, 1)
                    elif k == "m_conv":
                        dve.wait_ge(pad_zeroed, 1)
                        if s.mb > 0:
                            dve.wait_ge(mb_free, s.mb)
                        if s.mc > 0:
                            dve.wait_ge(mc_free, s.mc)
                        for j in range(TAPS):
                            for h in range(HALVES):
                                src, dst = conv[(j + 1) % 2][:, h, :], conv[j % 2][:, h, :]
                                if j == 0:
                                    ts(dst, x_in[:, h, j:j + SEQ], conv_w[:, h, j:j + 1], None,
                                       ALU.mult).then_inc(dve_chain, 1)
                                    count.up()
                                    continue
                                if count.n - (1 if j < TAPS - 1 or h == 0 else 0) > 0:
                                    dve.wait_ge(dve_chain, count.n - (1 if j < TAPS - 1 or h == 0 else 0))
                                ins = stt(dst, x_in[:, h, j:j + SEQ], conv_w[:, h, j:j + 1], src,
                                          ALU.mult, ALU.add)
                                if j < TAPS - 1:
                                    ins.then_inc(dve_chain, 1)
                                    count.up()
                                else:
                                    ins.then_inc(conv_done, 1)
                    elif k == "m_bc":
                        dve.wait_ge(bc_hi, 1)
                        tt(bc_rest, bc, bc3[0:STATES, :, :], ALU.subtract) \
                            .then_inc(bc_rest_ready, 1)
                        dve.wait_ge(bc_mid_ready, 1)
                        dve.wait_ge(bc_rest_ready, 1)
                        tt(bc3[64:64 + STATES, :, :], bc_rest, bc_mid, ALU.subtract) \
                            .then_inc(bc_ready, 1)
                    elif k == "m_sp":
                        if s.mb > 0:
                            dve.wait_ge(mb_free, s.mb)
                        if s.mc > 0:
                            dve.wait_ge(mc_free, s.mc)
                        stt(neg_abs, dt_pre, -1.0, dt_pre, ALU.mult, ALU.min) \
                            .then_inc(negabs_ready, 1)
                        dve.wait_ge(log_ready, 1)
                        stt(dt[:, :, :], dt_pre, 0.0, neg_abs, ALU.max, ALU.add) \
                            .then_inc(dt_ready, 1)
                    elif k in ("m_even", "m_odd"):
                        unit = 2 * s.n - (2 if k == "m_even" else 1)
                        if 0 <= unit < UNITS:
                            dve.wait_ge(decay_ready, unit + 1)
                            dve.wait_ge(drive_ready, unit + 1)
                            r = unit % SCAN_RING
                            nc.vector.tensor_tensor_scan(scan[:, r, :], decay[:, unit % DECAY_RING, :],
                                                         scan[:, r, :], 0.0, ALU.mult, ALU.add) \
                                .then_inc(scan_done, 1)
                        if 0 <= unit - 1 < UNITS:
                            done = unit - 1
                            if s.mc + (k == "m_odd") > 0:
                                dve.wait_ge(mc_full, s.mc + (k == "m_odd"))
                            dve.wait_ge(scan_done, done + 1)
                            r = done % SCAN_RING
                            ins = tt(scan[:, r, :], scan[:, r, :], m_c[:, :], ALU.mult)
                            ins.then_inc(mc_free if done % 2 else hc_even, 1)
                    elif k in ("m_out", "a_i"):
                        if s.x_misc:
                            dve.wait_ge(misc_free, s.x_misc)
                        if s.x_mb:
                            dve.wait_ge(mb_free, s.x_mb)
                        if k == "a_i" and s.has_out:
                            dve.wait_ge(out_stored, 16)
                        dve.wait_ge(mb_full, s.mb + 1)
                        tt(X[s.xout][:, :, :], X[s.xin][:, :, :],
                           m_b[:, :].rearrange("p (t d) -> p t d", t=TILES), ALU.add) \
                            .then_inc(mb_free, 1)
                    elif k == "a_f":
                        ps, full, free, uses = (m_b, mb_full, mb_free, s.mb) if s.t % 2 == 0 \
                            else (m_c, mc_full, mc_free, s.mc)
                        dve.wait_ge(full, uses + 1)
                        tt(spec[:, s.t].rearrange("p n d -> p (n d)"), ps[:, 0:3 * DIM], spec_bias[:, :],
                           ALU.add).then_inc(free, 1)
                    elif k == "a_mag":
                        dve.wait_ge(mags_ready, 1)
                        nc.vector.reciprocal(rkv, rkv)
                        nc.vector.reciprocal(rq, mag[:, :, 0, :]).then_inc(dve_chain, 1)
                        count.up()
                        if count.n > 0:
                            dve.wait_ge(dve_chain, count.n)
                    elif k == "a_kv":
                        q, ky, vl = (spec[:, :, j, :] for j in range(3))
                        tt(kv[:, :, re], ky[:, :, re], vl[:, :, re], ALU.mult)
                        tt(kv[:, :, im], ky[:, :, im], vl[:, :, re1], ALU.mult)
                        tt(prod[0], ky[:, :, im], vl[:, :, im], ALU.mult)
                        tt(prod[1], ky[:, :, re1], vl[:, :, im], ALU.mult).then_inc(dve_chain, 1)
                        dve.wait_ge(dve_chain, count.up())
                        tt(kv[:, :, re1], kv[:, :, re1], prod[0], ALU.subtract)
                        tt(kv[:, :, im], kv[:, :, im], prod[1], ALU.add).then_inc(dve_chain, 1)
                        dve.wait_ge(dve_chain, count.up())
                        tt(kv[:, :, re], kv[:, :, re], rkv, ALU.mult)
                        tt(kv[:, :, im], kv[:, :, im], rkv[:, :, re1], ALU.mult) \
                            .then_inc(kv_ready, 1)
                        tt(q[:, :, re], q[:, :, re], rq, ALU.mult)
                        tt(q[:, :, im], q[:, :, im], rq[:, :, re1], ALU.mult).then_inc(dve_chain, 1)
                        dve.wait_ge(dve_chain, count.up())
                    elif k == "a_o":
                        q = spec[:, :, 0, :]
                        sums = m_b[:, :].rearrange("p (t d) -> p t d", t=TILES)
                        if s.mb > 0:
                            dve.wait_ge(mb_full, s.mb)
                        tt(spec_out[:, :, re], sums[:, :, re], q[:, :, re], ALU.mult)
                        tt(spec_out[:, :, im], sums[:, :, im], q[:, :, re1], ALU.mult)
                        tt(prod[0], sums[:, :, im], q[:, :, im], ALU.mult)
                        tt(prod[1], sums[:, :, re1], q[:, :, im], ALU.mult).then_inc(mb_free, 1)
                        if s.mb > 0:
                            dve.wait_ge(mb_free, s.mb)
                        tt(spec_out[:, :, re1], spec_out[:, :, re1], prod[0], ALU.add)
                        tt(spec_out[:, :, im], spec_out[:, :, im], prod[1], ALU.subtract) \
                            .then_inc(out_spec_ready, 1)
                dve.drain()
                dve.sem_inc(arrived, 1)
                dve.wait_ge(go_dve, 1)
                dve.sem_clear(go_dve)
            run(dve, segment)

        @block.gpsimd
        def _(pool):
            tt = nc.gpsimd.tensor_tensor

            def meet_all():
                pool.drain()
                pool.wait_ge(arrived, len(go))
                for sem in of_segment:
                    pool.sem_clear(sem)
                for sem in go:
                    pool.sem_inc(sem, 1)

            meet_all()

            def segment(i, steps):
                count = Count()

                def drive(s, unit):
                    n, h = divmod(unit, HALVES)
                    if s.mb + (s.kind == "m_even") > 0:
                        pool.wait_ge(mb_free, s.mb + (s.kind == "m_even"))
                    if unit - SCAN_RING + 1 > 0:
                        pool.wait_ge(y_added, unit - SCAN_RING + 1)
                    tt(scan[:, unit % SCAN_RING, :], dtu[:, h, :], b_sb[:, n % 2, :], ALU.mult) \
                        .then_inc(drive_ready, 1)

                for s in steps:
                    k = s.kind
                    if k == "ln_a":
                        pool.wait_ge(ln_stats, s.no + 1)
                        nc.gpsimd.tensor_scalar(var_eps[:, :], moments[:, s.no % 2, :, 1], LN_EPS,
                                                None, ALU.add).then_inc(pool_chain, 1)
                        pool.wait_ge(pool_chain, count.up())
                        tt(rstd[:, s.no % 2, :], var_eps[:, :], minus_half[:, :], ALU.pow) \
                            .then_inc(ln_rstd, 1)
                    elif k == "ac":
                        pool.wait_ge(hi_done, s.b + 1)
                        r = s.b % RING
                        tt(act_lo[:, r, :], val[:, r, :], act_hi[:, r, :].bitcast(f32), ALU.subtract) \
                            .then_inc(lo_done, 1)
                    elif k == "m_in":
                        nc.gpsimd.memset(x_in[:, :, 0:TAPS - 1], 0.0).then_inc(pad_zeroed, 1)
                    elif k == "m_sp":
                        pool.wait_ge(dt_ready, 1)
                        nc.gpsimd.memset(decay[:, :, 0:1], 0.0)
                        tt(dtu[:, :, :], dt[:, :, :], u[:, :, :], ALU.mult).then_inc(dtu_ready, 1)
                    elif k == "m_even" and s.n < STATES:
                        if s.n == 0:
                            pool.wait_ge(dtu_ready, 1)
                        drive(s, 2 * s.n)
                    elif k == "m_odd":
                        for unit in (2 * s.n - 4, 2 * s.n - 3):
                            if unit < 0:
                                continue
                            h, r = unit % HALVES, unit % SCAN_RING
                            pool.wait_ge(y_started, HALVES)
                            if h == 0:
                                pool.wait_ge(hc_even, unit // 2 + 1)
                            else:
                                if s.mc > 0:
                                    pool.wait_ge(mc_free, s.mc)
                            if unit - 1 > 0:
                                pool.wait_ge(y_added, unit - 1)
                            tt(u[:, h, :], u[:, h, :], scan[:, r, :], ALU.add) \
                                .then_inc(y_added, 1)
                        if s.n < STATES:
                            drive(s, 2 * s.n + 1)
                    elif k == "m_gate":
                        if s.mb > 0:
                            pool.wait_ge(mb_free, s.mb)
                        if s.mc > 0:
                            pool.wait_ge(mc_free, s.mc)
                        pool.wait_ge(y_added, UNITS)
                        tt(u[:, :, :], u[:, :, :], dt[:, :, :], ALU.mult).then_inc(yz_ready, 1)
                    elif k == "a_mag":
                        pool.wait_ge(sq_ready, 1)
                        pairs = power[:, :, :, 1:1 + IMAG]
                        tt(pairs, pairs, power[:, :, :, REAL:DIM], ALU.add) \
                            .then_inc(power_ready, 1)
                        pool.wait_ge(mag_ready, 1)
                        nc.gpsimd.tensor_scalar(mag, mag, MAG_EPS, None, ALU.add) \
                            .then_inc(pool_chain, 1)
                        pool.wait_ge(pool_chain, count.up())
                        tt(rkv, mag[:, :, 1, :], mag[:, :, 2, :], ALU.mult) \
                            .then_inc(mags_ready, 1)
                meet_all()
            run(pool, segment)


def kernel(**inputs):
    import numpy as _np
    import concourse.bacc as _bacc
    from concourse.bass_utils import run_bass_kernel_spmd as _run

    a = {name: _np.asarray(v) for name, v in inputs.items()}

    def rows(w):
        n = w.shape[0] // P
        return w.reshape(n, P, -1).transpose(1, 0, 2).reshape(P, -1)

    def halves(v):
        return v.reshape(HALVES, P, -1).transpose(1, 0, 2)

    def ups(w):
        return w.transpose(1, 0, 2).reshape(DIM, -1)

    def with_shared(w, sw):
        return _np.concatenate([a["L1_ffn_" + w], a["L1_ffn_" + sw]], axis=0)

    split = _np.concatenate([
        a["L0_ffn_Wr"], a["L1_ffn_router_w"].T, ups(a["L0_ffn_W1"]), ups(a["L0_ffn_W3"]),
        rows(a["L0_ffn_W2"].reshape(-1, DIM)), a["L0_attn_W_in"].T, ups(with_shared("w1", "sw1")),
        ups(with_shared("w3", "sw3")), rows(with_shared("w2", "sw2").reshape(-1, DIM))], axis=1)

    angle = 2 * _np.pi * _np.outer(_np.arange(DIM), _np.arange(REAL)) / DIM
    cos, sin = _np.cos(angle), _np.sin(angle)[:, 1:REAL - 1]
    dft = _np.concatenate([cos, -sin], axis=1).astype(_np.float32)
    weight = _np.where(_np.isin(_np.arange(REAL), (0, REAL - 1)), 1.0, 2.0) / DIM
    idft = _np.concatenate([cos * weight, -sin * 2.0 / DIM], axis=1).T.astype(_np.float32)

    proj = _np.concatenate([a["L1_attn_W" + n] for n in "qkv"] + [dft] +
                           [a["L1_attn_b" + n][:, None] for n in "qkv"], axis=1)
    xp = halves(a["L0_attn_W_xproj"].T)
    xproj = _np.zeros((P, HALVES, P), _np.float32)
    xproj[:, :, 0:RANK] = xp[:, :, 0:RANK]
    xproj[:, :, 32:32 + STATES] = xp[:, :, RANK:RANK + STATES]
    xproj[:, :, 64:64 + STATES] = xp[:, :, RANK + STATES:]
    vec = halves(_np.concatenate([a["L0_attn_conv_w"], a["L0_attn_A_log"]] +
                                 [a["L0_attn_" + n][:, None] for n in ("conv_b", "b_dt", "D_skip")],
                                 axis=1))
    const = _np.concatenate([_np.eye(P), _np.triu(_np.ones((P, P))), idft, _np.ones((P, P)),
                             _np.tile(_np.arange(EXPERTS), (P, 1))], axis=1).astype(_np.float32)
    bf16 = mybir.dt.np(mybir.dt.bfloat16)
    sel = _np.zeros((PARTS * GATES, GATES * P))
    selbc = _np.zeros((PARTS * 32, STATES * P))
    for part in range(PARTS):
        for e in range(GATES):
            sel[part * GATES + e, e * P:(e + 1) * P] = 1
        for n in range(STATES):
            selbc[part * 32 + n, n * P:(n + 1) * P] = 1

    arrays = {
        "x_dram": a["L0_attn_x"], "split_dram": split, "proj_dram": proj, "xproj_dram": xproj,
        "wdt_dram": a["L0_attn_W_dt"].T, "wout_dram": halves(a["L0_attn_W_out"].T), "vec_dram": vec,
        "bias_dram": a["L1_ffn_experts_bias"], "const_dram": const,
        "identb_dram": _np.eye(P).astype(bf16), "sel_dram": sel.astype(bf16),
        "selbc_dram": selbc.astype(bf16)}
    arrays = {name: _np.ascontiguousarray(v) for name, v in arrays.items()}

    nc = _bacc.Bacc("TRN2", target_bir_lowering=False, num_devices=1)
    args = [nc.dram_tensor(name, v.shape, mybir.dt.from_np(v.dtype), kind="ExternalInput").ap()
            for name, v in arrays.items()]
    out = nc.dram_tensor("out_dram", (BATCH, SEQ, DIM), mybir.dt.float32, kind="ExternalOutput").ap()
    macaron_kernel(nc, *args, out)
    r = _run(nc, [arrays], core_ids=[0])
    return r.results[0]["out_dram"]
```

```python
import concourse.bass as bass
from concourse import mybir
from contextlib import ExitStack
import numpy as np

BATCH, SEQ, DIM = 8, 512, 128
P = 128
TILES = SEQ // P
INNER, HALVES, STATES, TAPS, RANK = 256, 2, 16, 4, 8
EXPERTS = 8
HID0, HID1 = 192, 256
BLOCKS0 = EXPERTS * HID0 // P
BLOCKS1 = (EXPERTS + 1) * HID1 // P
GATES = EXPERTS + 1
PARTS = 3
REAL, IMAG = DIM // 2 + 1, DIM // 2 - 1
LN_EPS, MAG_EPS = 1e-5, 1e-8

COL, _at = {}, 0
for _name, _w in (("r0", EXPERTS), ("r1", EXPERTS), ("up0", BLOCKS0 * P), ("gate0", BLOCKS0 * P),
                  ("down0", BLOCKS0 * P), ("in", 2 * INNER), ("up1", BLOCKS1 * P),
                  ("gate1", BLOCKS1 * P), ("down1", BLOCKS1 * P)):
    COL[_name], _at = _at, _at + _w
SPLIT_COLS = _at
CHUNKS = 8
CHUNK = SPLIT_COLS // CHUNKS

CALLS = {0: dict(layer=0, xin="xb", xout="xc", set=0), 1: dict(layer=1, xin="xe", xout="xe", set=1),
         2: dict(layer=1, xin="xc", xout="xc", set=0), 3: dict(layer=0, xin="xl", xout="xl", set=1)}
MIXER_SET = 2
BLOCKS = (BLOCKS0, BLOCKS1)
HG, RING, LAG = 2, 3, 2
EXP_STATES = 2
MIXER_EXTRA = 2
UNITS = HALVES * STATES
DECAY_RING, SCAN_RING = 8, 5


def selector_at(layer, k):
    if layer == 1:
        return k // 2 * P
    pair, r = divmod(k, 3)
    return (2 * pair * P, 2 * pair * P + P // 2, (2 * pair + 1) * P)[r]




class Step:

    def __init__(self, kind, c=None, k=None, n=None, t=None, b=None, src=None,
                 set=None, layer=None):
        self.kind, self.c, self.k, self.n, self.t, self.b = kind, c, k, n, t, b
        self.src, self.set, self.layer = src, set, layer
        self.x_misc = self.x_mb = 0


def prep_steps(c):
    about = dict(src=CALLS[c]["xin"], set=CALLS[c]["set"], layer=CALLS[c]["layer"])
    return [Step(k, **about) for k in ("ln_a", "ln_b", "ln_c", "rt_a", "rt_b", "rt_c")]


def mamba_steps():
    about = dict(src="xa", set=MIXER_SET)
    m = [Step(k, **about) for k in ("ln_a", "ln_b", "ln_c")] + [Step("m_in")]
    m += [Step("m_conv", t=t) for t in range(TAPS)]
    m += [Step(k) for k in ("m_xp", "m_bc", "m_bc2", "m_dt", "m_sp", "m_sp2", "m_sp3")]
    for n in range(STATES + 2):
        if n % EXP_STATES == 0 and n < STATES:
            m.append(Step("m_exp", n=n))
        m += [Step("m_even", n=n), Step("m_odd", n=n)]
    return m + [Step(k) for k in ("m_z", "m_gate", "m_out")]


def attn_steps():
    about = dict(src="xc", set=MIXER_SET)
    return [Step(k, **about) for k in ("ln_a", "ln_b", "ln_c")] + \
        [Step("a_f", t=t) for t in range(TILES)] + \
        [Step(k) for k in ("a_pow", "a_mag", "a_rec", "a_kv", "a_cum", "a_o", "a_t", "a_i")]


def segment_steps(calls, mamba, attn, next_xa):
    blocks = [(c, k) for c in calls for k in range(BLOCKS[CALLS[c]["layer"]])]
    steps, due = [], []
    mixer = mamba_steps() if mamba else []
    late = (prep_steps(0) if mamba else []) + (attn_steps() if attn else [])
    last = 1 if len(calls) > 1 and 1 in calls else None
    mixer_slots = sum(c != last for c, _ in blocks) + MIXER_EXTRA * (last == 1)
    steps += [Step("x_e")] if calls[0] == 1 else []
    steps += prep_steps(calls[0]) if calls[0] != 0 else []
    chain, opened = [], set()

    def follows(j):
        at = calls.index(blocks[j][0]) + 1
        if at == len(calls) or CALLS[calls[at]]["xin"] == CALLS[blocks[j][0]]["xout"]:
            return None
        return calls[at]

    def step(kind, j):
        c, k = blocks[j]
        return Step(kind, c=c, k=k, b=j)

    def tail(j):
        if j - 2 >= done[0]:
            done[0] = j - 1
            steps.append(step("down", j - 2))
            c, k = blocks[j - 2]
            if k == BLOCKS[CALLS[c]["layer"]] - 1:
                due.append(Step("ye", c=c, b=j - 1))
                due.append(Step("yt", c=c, b=j - 1))

    done = [0]
    for j, (c, k) in enumerate(blocks):
        if due:
            steps.append(due.pop(0))
        if j >= 1 and (j - 1) not in opened:
            steps.append(step("ac", j - 1))
        if ("uh", j) not in opened:
            steps.append(step("uh", j))
        ahead = j + 1 < len(blocks) and (blocks[j + 1][0] == c or follows(j) is not None)
        if ahead:
            if blocks[j + 1][0] != c:
                steps += chain
                chain = []
            steps.append(step("uh", j + 1))
            opened.add(("uh", j + 1))
        steps.append(step("ug", j))
        steps.append(step("cb", j))
        if j >= 1 and (j - 1) not in opened:
            steps.append(step("lo", j - 1))
        tail(j)
        if k == 0:
            chain = prep_steps(follows(j)) if follows(j) is not None else []
        if j == 4 and 1 in calls[1:]:
            steps.append(Step("x_e"))
        if chain and k >= 4:
            steps.append(chain.pop(0))
        if mixer:
            for _ in range(-(-len(mixer) // max(1, mixer_slots - j))):
                steps.append(mixer.pop(0))
        elif c == last and late and k >= 4:
            for _ in range(-(-len(late) // max(1, BLOCKS[CALLS[c]["layer"]] - k))):
                steps.append(late.pop(0))
        if not ahead:
            opened.add(j)
            steps += [step("ac", j), step("lo", j)]
            tail(j + 1)
            tail(j + 2)
            steps += due
            due = []
            if j + 1 < len(blocks):
                steps += prep_steps(blocks[j + 1][0])
    steps += mixer + late
    if next_xa:
        steps.append(Step("x_a"))
    return number(steps, calls)


def lo_on_dve(b):
    return b % 3 == 2


def number(steps, calls):
    misc = mb = mc = 0
    los, lo_at, scaled, x_at, c_at, x_by = [0, 0], {}, {}, {}, {}, {}
    nos = {}
    for s in steps:
        s.misc, s.mb, s.mc = misc, mb, mc
        kind = s.kind
        s.no = nos.get(kind, 0)
        nos[kind] = s.no + 1
        if s.c is not None:
            s.layer, s.set = CALLS[s.c]["layer"], CALLS[s.c]["set"]
            s.nth = calls.index(s.c)
        if kind == "lo":
            by_dve = lo_on_dve(s.b)
            los[by_dve] += 1
            lo_at[s.b] = by_dve, los[by_dve]
        if kind == "down":
            s.lo_dve, s.lo_at = lo_at[s.b]
        if kind == "uh" and s.b >= RING:
            s.lo_dve, s.lo_at = lo_at[s.b - RING]
        if kind == "cb":
            scaled[s.b] = misc + 1
        if kind == "ac":
            s.scaled = scaled[s.b]
        if kind == "ln_a":
            assert nos["ln_a"] - nos.get("ln_c", 0) <= 2
            s.x_misc, s.x_mb = x_by.get(s.src, (0, 0))
        if kind in ("ln_b", "ln_c"):
            assert [t.src for t in steps if t.kind == kind][s.no] == \
                [t.src for t in steps if t.kind == "ln_a"][s.no]
        if kind == "ln_c":
            x_at[s.set] = misc + 1
        if kind == "rt_c":
            c_at[s.set] = misc + 1
        if kind in ("uh", "ug", "rt_a"):
            s.x_at = x_at.get(s.set, 0)
        if kind in ("m_in", "m_z", "a_f"):
            s.x_at = x_at[MIXER_SET]
        if kind == "cb":
            s.c_at = c_at.get(s.set, 0)
        if kind == "x_a":
            s.x_misc, s.x_mb = x_by["xl"]
        if kind == "yt":
            s.xin, s.xout = CALLS[s.c]["xin"], CALLS[s.c]["xout"]
            s.x_misc, s.x_mb = x_by.get(s.xin, (0, 0))
            x_by[s.xout] = (misc + 1, 0)
        if kind in ("m_out", "a_i"):
            s.xin, s.xout = ("xa", "xb") if kind == "m_out" else ("xc", "xc")
            s.x_misc, s.x_mb = x_by.get(s.xin, (0, 0))
            x_by[s.xout] = (0, mb + 1)
        misc += kind in ("ln_c", "rt_a", "rt_c", "cb", "yt")
        mb += kind in ("m_in", "m_z", "m_dt", "m_xp", "m_out", "a_cum", "a_i") or \
            (kind == "m_even" and s.n < STATES) or (kind == "a_f" and s.t % 2 == 0)
        mc += kind in ("m_in", "m_z", "m_dt", "a_t") or \
            (kind == "m_odd" and 1 <= s.n <= STATES) or (kind == "a_f" and s.t % 2 == 1)
    return steps


def macaron_kernel(nc, x_dram, split_dram, proj_dram, xproj_dram, wdt_dram, wout_dram, vec_dram,
                   bias_dram, const_dram, identb_dram, sel_dram, selbc_dram, out_dram):
    f32, r32, bf16, u32 = mybir.dt.float32, mybir.dt.float32r, mybir.dt.bfloat16, mybir.dt.uint32
    ALU, ACT = mybir.AluOpType, mybir.ActivationFunctionType

    ctx = ExitStack()
    with ctx:
        def sb(name, shape, dt=f32):
            return ctx.enter_context(nc.sbuf_tensor(name, shape, dt))

        def bank(name):
            return ctx.enter_context(nc.psum_tensor(name, [P, SEQ], f32))

        w_hi, w_lo = sb("w_hi", [P, SPLIT_COLS], r32), sb("w_lo", [P, SPLIT_COLS], r32)
        wf_hi, wf_lo = sb("wf_hi", [P, 3 * DIM], r32), sb("wf_lo", [P, 3 * DIM], r32)
        spec_bias = sb("spec_bias", [P, 3 * DIM])
        xproj = sb("xproj", [P, HALVES, P])
        wdt = sb("wdt", [RANK, INNER])
        wout = sb("wout", [P, HALVES, DIM])
        vec = sb("vec", [P, HALVES, TAPS + STATES + 3])
        conv_w, a_log = vec[:, :, 0:TAPS], vec[:, :, TAPS:TAPS + STATES]
        conv_b, b_dt, d_skip = (vec[:, :, TAPS + STATES + j:TAPS + STATES + j + 1] for j in range(3))
        a_neg = sb("a_neg", [P, HALVES, STATES])
        const = sb("const", [P, 4 * P + EXPERTS])
        ident, tri, idft, ones = (const[:, j * P:(j + 1) * P] for j in range(4))
        iota = const[:, 4 * P:4 * P + EXPERTS]
        identb = sb("identb", [P, P], bf16)
        sel = sb("sel", [PARTS * GATES, GATES * P], bf16)
        selbc = sb("selbc", [PARTS * 32, STATES * P], bf16)
        router_bias = sb("router_bias", [P, 2, EXPERTS])
        minus_half = sb("minus_half", [P, TILES])

        X = {n: sb(n, [P, TILES, DIM]) for n in ("xl", "xa", "xb", "xc", "xe")}

        stats = sb("stats", [P, TILES, 6])
        moments = sb("moments", [P, 2, TILES, 2])
        var_eps = sb("var_eps", [P, TILES])
        rstd = sb("rstd", [P, 2, TILES])
        xn = sb("xn", [P, 2, TILES, DIM])
        xt_hi, xt_lo = sb("xt_hi", [P, 3, SEQ], r32), sb("xt_lo", [P, 3, SEQ], r32)
        logits = sb("logits", [P, TILES, EXPERTS])
        top = sb("top", [P, TILES, 8])
        top_at = sb("top_at", [P, TILES, 8], u32)
        top_f = sb("top_f", [P, TILES, 2])
        gap, th = sb("gap", [P, TILES]), sb("th", [P, TILES])
        pair_w = sb("pair_w", [P, TILES, 2])
        hot = sb("hot", [P, TILES, 2, EXPERTS])
        comb = sb("comb", [P, TILES, GATES])
        rest = sb("rest", [P, TILES, GATES])
        comb3 = sb("comb3", [P, TILES, PARTS, GATES], bf16)
        comb_t = sb("comb_t", [PARTS * GATES, 2, SEQ], bf16)

        val = sb("val", [P, RING, SEQ])
        act_hi, act_lo = sb("act_hi", [P, RING, SEQ], r32), sb("act_lo", [P, RING, SEQ], r32)
        y_t = sb("y_t", [P, SEQ])

        u = sb("u", [P, HALVES, SEQ])
        dt = sb("dt", [P, HALVES, SEQ])
        dtu = sb("dtu", [P, HALVES, SEQ])
        decay = sb("decay", [P, DECAY_RING, SEQ])
        b_sb = sb("b_sb", [P, 2, SEQ])
        scan = sb("scan", [P, SCAN_RING, SEQ])
        bc3 = sb("bc3", [PARTS * 32, 2, SEQ], bf16)

        decay_flat = decay[:, :, :].rearrange("p a b -> p (a b)")
        scan_flat = scan[:, :, :].rearrange("p a b -> p (a b)")
        staging = decay_flat[:, 0:2 * CHUNK]
        proj = scan_flat[:, 0:4 * DIM + 3]
        dft = proj[:, 3 * DIM:4 * DIM]
        bias_cols = scan_flat[:, 5 * DIM:8 * DIM]
        wide = HALVES * SEQ
        x_in = decay_flat[:, 0:HALVES * (TAPS - 1 + SEQ)].rearrange("p (h t) -> p h t", h=HALVES)
        conv = [decay_flat[:, j * wide:(j + 1) * wide].rearrange("p (h t) -> p h t", h=HALVES)
                for j in (2, 3)]
        dt_pre, neg_abs, dt_exp = (decay_flat[:, j * wide:(j + 1) * wide]
                                   .rearrange("p (h t) -> p h t", h=HALVES) for j in (0, 1, 2))
        bc = scan_flat[0:STATES, 0:2 * SEQ].rearrange("p (j t) -> p j t", j=2)
        bc_rest = scan_flat[0:STATES, 2 * SEQ:4 * SEQ].rearrange("p (j t) -> p j t", j=2)
        bc_mid = scan_flat[0:STATES, 4 * SEQ:5 * SEQ].bitcast(bf16).rearrange("p (j t) -> p j t", j=2)
        dt_lo = b_sb[0:RANK, 0, :]

        def piece(flat, at, *dims):
            n = int(np.prod(dims))
            ap = flat[:, at:at + n]
            if len(dims) == 2:
                return ap.rearrange("p (a b) -> p a b", a=dims[0])
            return ap.rearrange("p (a b c) -> p a b c", a=dims[0], b=dims[1])

        spec = piece(scan_flat, 0, TILES, 3, DIM)
        kv = piece(scan_flat, 3 * SEQ, TILES, DIM)
        o_t = scan_flat[:, 4 * SEQ:5 * SEQ]
        power = piece(decay_flat, 0, TILES, 3, DIM)
        spec_out = piece(decay_flat, 0, TILES, DIM)
        prod = [piece(decay_flat, (3 + j) * SEQ // 1, TILES, IMAG) for j in range(2)]
        mag = piece(decay_flat, 5 * SEQ, TILES, 3, REAL)
        rq = piece(decay_flat, 5 * SEQ + 3 * TILES * REAL, TILES, REAL)
        rkv = piece(decay_flat, 5 * SEQ + 4 * TILES * REAL, TILES, REAL)

        h_ps = [bank(f"h_ps{j}") for j in range(HG)]
        g_ps = [bank(f"g_ps{j}") for j in range(HG)]
        y_ps, misc, m_b, m_c = bank("y_ps"), bank("misc"), bank("m_b"), bank("m_c")
        misc_bf = misc[:, :].bitcast(bf16)

        (h_full, g_full, silu_done, act_done, hi_done, lo_done, lo_by_dve, lo_by_pool, down_done, y_copied,
         misc_full, misc_free, mb_full, mb_free, mc_full, mc_free, ln_stats, ln_rstd, ln_xn,
         ln_hi, gap_ready, th_ready, comb_ready, xl_loaded, xe_final, xe_ready, out_stored,
         pad_zeroed, tap_done, u_ready, dtlo_ready, bc_copied, bc_hi, bc_rest_ready, bc_mid_ready,
         bc_ready, bc_parts, negabs_ready, log_ready, dt_ready, dtu_ready, y_started,
         decay_ready, drive_ready, scan_done, hc_even, y_added, yz_ready, sq_ready,
         power_ready, mag_ready, mags_ready, kv_ready, out_spec_ready, dve_chain, act_chain,
         pool_chain, arrived) = of_segment = [ctx.enter_context(nc.semaphore(name)) for name in (
            "h_full", "g_full", "silu_done", "act_done", "hi_done", "lo_done", "lo_by_dve", "lo_by_pool", "down_done",
            "y_copied", "misc_full", "misc_free", "mb_full", "mb_free", "mc_full",
            "mc_free", "ln_stats", "ln_rstd", "ln_xn", "ln_hi", "gap_ready", "th_ready",
            "comb_ready", "xl_loaded", "xe_final", "xe_ready", "out_stored", "pad_zeroed", "tap_done",
            "u_ready", "dtlo_ready", "bc_copied", "bc_hi", "bc_rest_ready", "bc_mid_ready", "bc_ready",
            "bc_parts", "negabs_ready", "log_ready", "dt_ready", "dtu_ready", "y_started",
            "decay_ready", "drive_ready", "scan_done", "hc_even", "y_added", "yz_ready",
            "sq_ready", "power_ready", "mag_ready", "mags_ready", "kv_ready",
            "out_spec_ready", "dve_chain", "act_chain", "pool_chain", "arrived")]
        go_sync, go_act, go_dve, go_pe = go = [ctx.enter_context(nc.semaphore(f"go_{e}"))
                                               for e in ("sync", "act", "dve", "pe")]
        w_loaded = [ctx.enter_context(nc.semaphore(f"w_loaded{j}")) for j in range(2)]
        small_loaded = ctx.enter_context(nc.semaphore("small_loaded"))
        block = ctx.enter_context(nc.Block())

        class Count:

            def __init__(self):
                self.n = 0

            def up(self):
                self.n += 1
                return self.n

        def preloaded(i):
            return isinstance(i, int) and i == -1

        def steps_of(i):
            calls = [c for c, on in ((0, 1 <= i <= BATCH), (3, -1 <= i <= BATCH - 2),
                                     (2, 1 <= i <= BATCH), (1, 2 <= i <= BATCH + 1)) if on]
            return segment_steps(calls, 0 <= i < BATCH, 1 <= i <= BATCH, 3 in calls)

        LOOP_FROM, LOOP_TO = 3, BATCH - 1

        def run(e, segment):
            for i in range(-1, LOOP_FROM):
                segment(i, steps_of(i))
            full = steps_of(LOOP_FROM)
            with e.Fori(LOOP_FROM, LOOP_TO) as i:
                segment(i, full)
            for i in range(LOOP_TO, BATCH + 2):
                segment(i, steps_of(i))

        small = [(const[:, :], const_dram), (proj, proj_dram), (vec[:, :, :], vec_dram),
                 (wdt[:, :], wdt_dram), (xproj[:, :, :], xproj_dram), (wout[:, :, :], wout_dram),
                 (identb[:, :], identb_dram), (sel[:, :], sel_dram), (selbc[:, :], selbc_dram),
                 (router_bias[:, 1, :], bias_dram.partition_broadcast(P)),
                 (X["xl"][:, :, :], x_dram[0].rearrange("(t p) d -> p t d", p=P))]

        @block.sync
        def _(sp):
            for j in range(CHUNKS):
                if j >= 2:
                    sp.wait_ge(lo_done, j - 1)
                sp.dma_start(staging[:, (j % 2) * CHUNK:(j % 2 + 1) * CHUNK],
                             split_dram[:, j * CHUNK:(j + 1) * CHUNK]).then_inc(w_loaded[j % 2], 16)
                if j == 1:
                    for dst, src in small:
                        sp.dma_start(dst, src).then_inc(small_loaded, 16)
            sp.drain()
            sp.sem_inc(arrived, 1)
            sp.wait_ge(go_sync, 1)
            sp.sem_clear(go_sync)

            def segment(i, steps):
                kinds = {(s.kind, s.c) for s in steps}
                if ("ug", 3) in kinds and not preloaded(i):
                    sp.dma_start(X["xl"][:, :, :],
                                 x_dram[i + 1].rearrange("(t p) d -> p t d", p=P)) \
                        .then_inc(xl_loaded, 16)
                if not isinstance(i, int) or i >= 3:
                    sp.dma_start(out_dram[i - 3].rearrange("(t p) d -> p t d", p=P),
                                 X["xe"][:, :, :]).then_inc(out_stored, 16)
                    sp.wait_ge(out_stored, 16)
                if ("ug", 3) in kinds and not preloaded(i):
                    sp.wait_ge(xl_loaded, 16)
                if isinstance(i, int) and i == BATCH + 1:
                    sp.wait_ge(xe_final, 1)
                    sp.dma_start(out_dram[BATCH - 1].rearrange("(t p) d -> p t d", p=P),
                                 X["xe"][:, :, :]).then_inc(out_stored, 16)
                    sp.wait_ge(out_stored, 32)
                sp.drain()
                sp.sem_inc(arrived, 1)
                sp.wait_ge(go_sync, 1)
                sp.sem_clear(go_sync)
            run(sp, segment)

        @block.tensor
        def _(pe):
            def mm3(out, w, x, first, last):
                nc.tensor.matmul(out, w[0], x[0], start=first, stop=False)
                nc.tensor.matmul(out, w[0], x[1], start=False, stop=False)
                return nc.tensor.matmul(out, w[1], x[0], start=False, stop=last)

            def weights(name, k, width=P):
                c = COL[name] + k * width
                return w_hi[:, c:c + width], w_lo[:, c:c + width]

            pe.wait_ge(small_loaded, 16 * len(small))
            pe.wait_ge(bc_copied, 1)
            for j in range(3):
                nc.tensor.matmul(m_b[:, j * DIM:(j + 1) * DIM], proj[:, j * DIM:(j + 1) * DIM], dft,
                                 start=True, stop=True)
            for j in range(3):
                ins = nc.tensor.matmul(m_c[:, j * DIM:(j + 1) * DIM],
                                       bias_cols[:, j * DIM:(j + 1) * DIM], dft, start=True, stop=True)
            ins.then_inc(mb_full, 1)
            pe.drain()
            pe.sem_inc(arrived, 1)
            pe.wait_ge(go_pe, 1)
            pe.sem_clear(go_pe)

            def segment(i, steps):
                for s in steps:
                    k = s.kind
                    if k in ("ln_c", "rt_a", "rt_c", "cb", "yt"):
                        if k == "ln_c":
                            pe.wait_ge(ln_xn, s.no + 1)
                        if k == "rt_c":
                            pe.wait_ge(comb_ready, s.no + 1)
                        if k == "yt":
                            pe.wait_ge(y_copied, s.nth + 1)
                        if k == "rt_a":
                            if s.x_at > 0:
                                pe.wait_ge(misc_free, s.x_at)
                        if k == "cb":
                            if s.c_at > 0:
                                pe.wait_ge(misc_free, s.c_at)
                        if s.misc > 0:
                            pe.wait_ge(misc_free, s.misc)
                        tiles = [slice(t * P, (t + 1) * P) for t in range(TILES)]
                        if k == "ln_c":
                            for t in range(TILES):
                                ins = nc.tensor.transpose(misc[:, tiles[t]], xn[:, s.no % 2, t, :], ident)
                        elif k == "yt":
                            for t in range(TILES):
                                ins = nc.tensor.transpose(misc[:, tiles[t]], y_t[:, tiles[t]], ident)
                        elif k == "rt_a":
                            r = weights(f"r{s.layer}", 0, EXPERTS)
                            for t in range(TILES):
                                ins = mm3(misc[:, t * EXPERTS:(t + 1) * EXPERTS],
                                          (xt_hi[:, s.set, tiles[t]], xt_lo[:, s.set, tiles[t]]), r,
                                          True, True)
                        elif k == "rt_c":
                            for t in range(TILES):
                                ins = nc.tensor.transpose(misc_bf[0:PARTS * GATES, tiles[t]],
                                                          comb3[:, t].rearrange("p a b -> p (a b)"),
                                                          identb[:, :])
                        else:
                            at = selector_at(s.layer, s.k)
                            ins = nc.tensor.matmul(misc[:, :], sel[:, at:at + P], comb_t[:, s.set, :],
                                                   start=True, stop=True)
                        ins.then_inc(misc_full, 1)
                    elif k == "uh":
                        if s.k == 0 and s.x_at > 0:
                            pe.wait_ge(misc_free, s.x_at)
                        if s.b >= HG:
                            pe.wait_ge(silu_done, s.b - HG + 1)
                        mm3(h_ps[s.b % HG][:, :], weights(f"up{s.layer}", s.k),
                            (xt_hi[:, s.set, :], xt_lo[:, s.set, :]), True, True).then_inc(h_full, 1)
                    elif k == "ug":
                        if s.b >= HG:
                            pe.wait_ge(act_done, s.b - HG + 1)
                        mm3(g_ps[s.b % HG][:, :], weights(f"gate{s.layer}", s.k),
                            (xt_hi[:, s.set, :], xt_lo[:, s.set, :]), True, True).then_inc(g_full, 1)
                    elif k == "down":
                        if s.k == 0 and s.nth > 0:
                            pe.wait_ge(y_copied, s.nth)
                        if s.lo_dve:
                            pe.wait_ge(lo_by_dve, s.lo_at)
                        else:
                            pe.wait_ge(lo_by_pool, s.lo_at)
                        mm3(y_ps[:, :], weights(f"down{s.layer}", s.k),
                            (act_hi[:, s.b % RING, :], act_lo[:, s.b % RING, :]),
                            s.k == 0, s.k == BLOCKS[s.layer] - 1).then_inc(down_done, 1)
                    elif k in ("m_in", "m_z"):
                        if s.x_at > 0:
                            pe.wait_ge(misc_free, s.x_at)
                        xs = xt_hi[:, MIXER_SET, :], xt_lo[:, MIXER_SET, :]
                        off = 0 if k == "m_in" else HALVES
                        if s.mb > 0:
                            pe.wait_ge(mb_free, s.mb)
                        mm3(m_b[:, :], weights("in", off), xs, True, True).then_inc(mb_full, 1)
                        if s.mc > 0:
                            pe.wait_ge(mc_free, s.mc)
                        mm3(m_c[:, :], weights("in", off + 1), xs, True, True).then_inc(mc_full, 1)
                    elif k == "m_xp":
                        pe.wait_ge(u_ready, HALVES)
                        if s.mb > 0:
                            pe.wait_ge(mb_free, s.mb)
                        for h in range(HALVES):
                            ins = nc.tensor.matmul(m_b[:, :], xproj[:, h, :], u[:, h, :],
                                                   start=h == 0, stop=h == HALVES - 1)
                        ins.then_inc(mb_full, 1)
                    elif k == "m_dt":
                        pe.wait_ge(dtlo_ready, 1)
                        if s.mb > 0:
                            pe.wait_ge(mb_free, s.mb)
                        nc.tensor.matmul(m_b[:, :], wdt[:, 0:P], dt_lo, start=True, stop=True) \
                            .then_inc(mb_full, 1)
                        if s.mc > 0:
                            pe.wait_ge(mc_free, s.mc)
                        nc.tensor.matmul(m_c[:, :], wdt[:, P:2 * P], dt_lo, start=True, stop=True) \
                            .then_inc(mc_full, 1)
                    elif k == "m_even" and s.n < STATES:
                        pe.wait_ge(bc_parts, 1)
                        pe.wait_ge(bc_ready, 1)
                        if s.mb > 0:
                            pe.wait_ge(mb_free, s.mb)
                        nc.tensor.matmul(m_b[:, :], selbc[:, s.n * P:(s.n + 1) * P], bc3[:, 0, :],
                                         start=True, stop=True).then_inc(mb_full, 1)
                    elif k == "m_odd" and 1 <= s.n <= STATES:
                        if s.mc > 0:
                            pe.wait_ge(mc_free, s.mc)
                        nc.tensor.matmul(m_c[:, :], selbc[:, (s.n - 1) * P:s.n * P], bc3[:, 1, :],
                                         start=True, stop=True).then_inc(mc_full, 1)
                    elif k == "m_out":
                        pe.wait_ge(yz_ready, 1)
                        if s.mb > 0:
                            pe.wait_ge(mb_free, s.mb)
                        for t in range(TILES):
                            for h in range(HALVES):
                                ins = nc.tensor.matmul(m_b[:, t * P:(t + 1) * P],
                                                       u[:, h, t * P:(t + 1) * P], wout[:, h, :],
                                                       start=h == 0, stop=h == HALVES - 1)
                        ins.then_inc(mb_full, 1)
                    elif k == "a_f":
                        if s.x_at > 0:
                            pe.wait_ge(misc_free, s.x_at)
                        ps, full, free, uses = (m_b, mb_full, mb_free, s.mb) if s.t % 2 == 0 \
                            else (m_c, mc_full, mc_free, s.mc)
                        if uses > 0:
                            pe.wait_ge(free, uses)
                        cols = slice(s.t * P, (s.t + 1) * P)
                        mm3(ps[:, 0:3 * DIM], (xt_hi[:, MIXER_SET, cols], xt_lo[:, MIXER_SET, cols]),
                            (wf_hi[:, :], wf_lo[:, :]), True, True).then_inc(full, 1)
                    elif k == "a_cum":
                        pe.wait_ge(kv_ready, 1)
                        if s.mb > 0:
                            pe.wait_ge(mb_free, s.mb)
                        for t in range(TILES):
                            for v in range(t + 1):
                                ins = nc.tensor.matmul(m_b[:, t * P:(t + 1) * P],
                                                       tri if v == t else ones, kv[:, v, :],
                                                       start=v == 0, stop=v == t)
                        ins.then_inc(mb_full, 1)
                    elif k == "a_t":
                        pe.wait_ge(out_spec_ready, 1)
                        if s.mc > 0:
                            pe.wait_ge(mc_free, s.mc)
                        for t in range(TILES):
                            ins = nc.tensor.transpose(m_c[:, t * P:(t + 1) * P], spec_out[:, t, :], ident)
                        ins.then_inc(mc_full, 1)
                    elif k == "a_i":
                        if s.mc > 0:
                            pe.wait_ge(mc_free, s.mc)
                        if s.mb > 0:
                            pe.wait_ge(mb_free, s.mb)
                        for t in range(TILES):
                            ins = nc.tensor.matmul(m_b[:, t * P:(t + 1) * P], o_t[:, t * P:(t + 1) * P],
                                                   idft, start=True, stop=True)
                        ins.then_inc(mb_full, 1)
                pe.drain()
                pe.sem_inc(arrived, 1)
                pe.wait_ge(go_pe, 1)
                pe.sem_clear(go_pe)
            run(pe, segment)

        @block.scalar
        def _(act):
            for j in range(CHUNKS):
                act.wait_ge(w_loaded[j % 2], 16 * (j // 2 + 1))
                nc.scalar.activation(w_hi[:, j * CHUNK:(j + 1) * CHUNK],
                                     staging[:, (j % 2) * CHUNK:(j % 2 + 1) * CHUNK],
                                     ACT.Copy).then_inc(hi_done, 1)
            act.wait_ge(small_loaded, 16 * len(small))
            nc.scalar.activation(a_neg[:, :, :], a_log, ACT.Exp).then_inc(act_chain, 1)
            act.wait_ge(mb_full, 1)
            nc.scalar.activation(wf_hi[:, :], m_b[:, 0:3 * DIM], ACT.Copy).then_inc(ln_hi, 1)
            nc.scalar.activation(spec_bias[:, :], m_c[:, 0:3 * DIM], ACT.Copy)
            act.drain()
            act.sem_inc(arrived, 1)
            act.wait_ge(go_act, 1)
            act.sem_clear(go_act)

            def segment(i, steps):
                for s in steps:
                    k = s.kind
                    if k == "ln_c":
                        act.wait_ge(misc_full, s.misc + 1)
                        nc.scalar.activation(xt_hi[:, s.set, :], misc[:, :], ACT.Copy) \
                            .then_inc(ln_hi, 1)
                    elif k == "rt_a":
                        act.wait_ge(gap_ready, s.no + 1)
                        nc.scalar.activation(th[:, :], gap[:, :], ACT.Tanh, scale=0.5) \
                            .then_inc(th_ready, 1)
                    elif k == "rt_c":
                        act.wait_ge(misc_full, s.misc + 1)
                        nc.scalar.activation(comb_t[:, s.set, :], misc_bf[0:PARTS * GATES, 0:SEQ],
                                             ACT.Copy).then_inc(misc_free, 1)
                    elif k == "uh":
                        act.wait_ge(h_full, s.b + 1)
                        if s.b >= RING:
                            if s.lo_dve:
                                act.wait_ge(lo_by_dve, s.lo_at)
                            else:
                                act.wait_ge(lo_by_pool, s.lo_at)
                        nc.scalar.activation(val[:, s.b % RING, :], h_ps[s.b % HG][:, :], ACT.Silu) \
                            .then_inc(silu_done, 1)
                    elif k == "ac":
                        act.wait_ge(act_done, s.b + 1)
                        if s.b - RING + 1 > 0:
                            act.wait_ge(down_done, s.b - RING + 1)
                        nc.scalar.activation(act_hi[:, s.b % RING, :], val[:, s.b % RING, :], ACT.Copy) \
                            .then_inc(hi_done, 1)
                    elif k == "ye":
                        if s.b > 0:
                            act.wait_ge(down_done, s.b)
                        nc.scalar.activation(y_t[:, :], y_ps[:, :], ACT.Copy).then_inc(y_copied, 1)
                    elif k in ("m_in", "m_z", "m_dt"):
                        for h, (ps, full, free, uses) in enumerate(((m_b, mb_full, mb_free, s.mb),
                                                                    (m_c, mc_full, mc_free, s.mc))):
                            act.wait_ge(full, uses + 1)
                            if k == "m_in":
                                ins = nc.scalar.activation(x_in[:, h, TAPS - 1:], ps[:, :], ACT.Copy)
                            elif k == "m_z":
                                ins = nc.scalar.activation(dt[:, h, :], ps[:, :], ACT.Silu)
                            else:
                                ins = nc.scalar.activation(dt_pre[:, h, :], ps[:, :], ACT.Identity,
                                                           bias=b_dt[:, h, :])
                            ins.then_inc(free, 1)
                    elif k == "m_conv" and s.t == TAPS - 1:
                        for h in range(HALVES):
                            act.wait_ge(tap_done, HALVES * s.t + h + 1)
                            nc.scalar.activation(u[:, h, :], conv[1][:, h, :], ACT.Silu,
                                                 bias=conv_b[:, h, :]).then_inc(u_ready, 1)
                    elif k == "m_xp":
                        act.wait_ge(mb_full, s.mb + 1)
                        nc.scalar.activation(dt_lo, m_b[0:RANK, :], ACT.Copy) \
                            .then_inc(dtlo_ready, 1)
                        nc.scalar.activation(bc[:, 0, :], m_b[32:32 + STATES, :], ACT.Copy) \
                            .then_inc(bc_copied, 1)
                        nc.scalar.activation(bc[:, 1, :], m_b[64:64 + STATES, :], ACT.Copy) \
                            .then_inc(mb_free, 1)
                    elif k == "m_bc":
                        act.wait_ge(bc_copied, 1)
                        if s.mb > 0:
                            act.wait_ge(mb_free, s.mb)
                        nc.scalar.activation(bc3[0:STATES, :, :], bc, ACT.Copy).then_inc(bc_hi, 1)
                    elif k == "m_bc2":
                        act.wait_ge(bc_rest_ready, 1)
                        nc.scalar.activation(bc_mid, bc_rest, ACT.Copy).then_inc(bc_mid_ready, 1)
                        act.wait_ge(bc_mid_ready, 1)
                        nc.scalar.activation(bc3[32:32 + STATES, :, :], bc_mid, ACT.Copy) \
                            .then_inc(bc_parts, 1)
                    elif k == "m_sp":
                        act.wait_ge(negabs_ready, 1)
                        nc.scalar.activation(dt_exp, neg_abs, ACT.Exp).then_inc(act_chain, 1)
                        act.wait_ge(act_chain, 1)
                        nc.scalar.activation(neg_abs, dt_exp, ACT.Ln, bias=1.0) \
                            .then_inc(log_ready, 1)
                    elif k == "m_sp3":
                        act.wait_ge(dtu_ready, 1)
                        for h in range(HALVES):
                            nc.scalar.activation(u[:, h, :], u[:, h, :], ACT.Copy,
                                                 scale=d_skip[:, h, :]).then_inc(y_started, 1)
                    elif k == "m_exp":
                        act.wait_ge(dt_ready, 1)
                        act.wait_ge(dtu_ready, 1)
                        for unit in range(HALVES * s.n, HALVES * (s.n + EXP_STATES)):
                            n, h = divmod(unit, HALVES)
                            if unit - DECAY_RING + 1 > 0:
                                act.wait_ge(scan_done, unit - DECAY_RING + 1)
                            nc.scalar.activation(decay[:, unit % DECAY_RING, 1:], dt[:, h, 1:], ACT.Exp,
                                                 scale=a_neg[:, h, n:n + 1]) \
                                .then_inc(decay_ready, 1)
                    elif k == "m_even" and s.n < STATES:
                        act.wait_ge(mb_full, s.mb + 1)
                        if 2 * s.n - 2 > 0:
                            act.wait_ge(drive_ready, 2 * s.n - 2)
                        nc.scalar.activation(b_sb[:, s.n % 2, :], m_b[:, :], ACT.Copy) \
                            .then_inc(mb_free, 1)
                    elif k == "a_pow":
                        if s.mb > 0:
                            act.wait_ge(mb_free, s.mb)
                        if s.mc > 0:
                            act.wait_ge(mc_free, s.mc)
                        nc.scalar.activation(power, spec, ACT.Square).then_inc(sq_ready, 1)
                    elif k == "a_mag":
                        act.wait_ge(power_ready, 1)
                        nc.scalar.activation(mag, power[:, :, :, 0:REAL], ACT.Sqrt) \
                            .then_inc(mag_ready, 1)
                    elif k == "a_t":
                        act.wait_ge(mc_full, s.mc + 1)
                        nc.scalar.activation(o_t, m_c[:, :], ACT.Copy).then_inc(mc_free, 1)
                act.drain()
                act.sem_inc(arrived, 1)
                act.wait_ge(go_act, 1)
                act.sem_clear(go_act)
            run(act, segment)

        @block.vector
        def _(dve):
            tt, ts, stt = nc.vector.tensor_tensor, nc.vector.tensor_scalar, nc.vector.scalar_tensor_tensor

            nc.vector.memset(comb[:, :, :], 0.5)
            nc.vector.memset(router_bias[:, 0, :], 0.0)
            nc.vector.memset(bc3[:, :, :], 0.0)
            nc.vector.memset(minus_half[:, :], -0.5)
            for j in range(CHUNKS):
                cols = slice(j * CHUNK, (j + 1) * CHUNK)
                dve.wait_ge(hi_done, j + 1)
                tt(w_lo[:, cols], staging[:, (j % 2) * CHUNK:(j % 2 + 1) * CHUNK],
                   w_hi[:, cols].bitcast(f32), ALU.subtract).then_inc(lo_done, 1)
            dve.wait_ge(small_loaded, 16 * len(small))
            for j in range(3):
                ins = ts(bias_cols[:, j * DIM:(j + 1) * DIM], ones, proj[:, 4 * DIM + j:4 * DIM + j + 1],
                         None, ALU.mult)
            ins.then_inc(bc_copied, 1)
            dve.wait_ge(act_chain, 1)
            ts(a_neg[:, :, :], a_neg[:, :, :], -1.0, None, ALU.mult)
            dve.wait_ge(ln_hi, 1)
            tt(wf_lo[:, :], m_b[:, 0:3 * DIM], wf_hi[:, :].bitcast(f32), ALU.subtract)
            dve.drain()
            dve.sem_inc(arrived, 1)
            dve.wait_ge(go_dve, 1)
            dve.sem_clear(go_dve)

            re, im, re1 = slice(0, REAL), slice(REAL, DIM), slice(1, 1 + IMAG)

            def segment(i, steps):
                count = Count()

                for s in steps:
                    k = s.kind
                    if k == "ln_a":
                        if s.x_misc:
                            dve.wait_ge(misc_free, s.x_misc)
                        if s.x_mb:
                            dve.wait_ge(mb_free, s.x_mb)
                        if s.src == "xl" and not preloaded(i):
                            dve.wait_ge(xl_loaded, 16)
                        if s.src == "xe":
                            dve.wait_ge(xe_ready, 1)
                        if s.no - 1 > 0:
                            dve.wait_ge(ln_rstd, s.no - 1)
                        for t in range(TILES):
                            ins = nc.vector.bn_stats(stats[:, t, :], X[s.src][:, t, :])
                        ins.then_inc(dve_chain, 1)
                        dve.wait_ge(dve_chain, count.up())
                        for t in range(TILES):
                            ins = nc.vector.bn_aggr(moments[:, s.no % 2, t, :], stats[:, t, :])
                        ins.then_inc(ln_stats, 1)
                    elif k == "ln_b":
                        dve.wait_ge(ln_rstd, s.no + 1)
                        for t in range(TILES):
                            ins = ts(xn[:, s.no % 2, t, :], X[s.src][:, t, :],
                                     moments[:, s.no % 2, t, 0:1], rstd[:, s.no % 2, t:t + 1],
                                     ALU.subtract, ALU.mult)
                        ins.then_inc(ln_xn, 1)
                    elif k == "ln_c":
                        dve.wait_ge(ln_hi, s.no + 1)
                        tt(xt_lo[:, s.set, :], misc[:, :], xt_hi[:, s.set, :].bitcast(f32), ALU.subtract) \
                            .then_inc(misc_free, 1)
                    elif k == "rt_a":
                        dve.wait_ge(misc_full, s.misc + 1)
                        bias = router_bias[:, s.layer, :].unsqueeze(1).to_broadcast([P, TILES, EXPERTS])
                        tt(logits[:, :, :], misc[:, 0:TILES * EXPERTS]
                           .rearrange("p (t e) -> p t e", t=TILES), bias, ALU.add) \
                            .then_inc(misc_free, 1)
                        dve.wait_ge(misc_free, s.misc + 1)
                        for t in range(TILES):
                            ins = nc.vector.max(top[:, t, :], logits[:, t, :])
                        ins.then_inc(dve_chain, 1)
                        dve.wait_ge(dve_chain, count.up())
                        tt(gap[:, :], top[:, :, 0], top[:, :, 1], ALU.subtract) \
                            .then_inc(gap_ready, 1)
                        for t in range(TILES):
                            ins = nc.vector.max_index(top_at[:, t, :], top[:, t, :], logits[:, t, :])
                        ins.then_inc(dve_chain, 1)
                        dve.wait_ge(dve_chain, count.up())
                        nc.vector.tensor_copy(top_f[:, :, :], top_at[:, :, 0:2]) \
                            .then_inc(dve_chain, 1)
                        count.up()
                    elif k == "rt_b":
                        dve.wait_ge(th_ready, s.no + 1)
                        ts(pair_w[:, :, 0], th[:, :], 0.25, 0.25, ALU.mult, ALU.add)
                        ts(pair_w[:, :, 1], th[:, :], -0.25, 0.25, ALU.mult, ALU.add) \
                            .then_inc(dve_chain, 1)
                        count.up()
                        dve.wait_ge(dve_chain, count.n - 1)
                        every = [P, TILES, 2, EXPERTS]
                        tt(hot[:, :, :, :], iota.unsqueeze(1).unsqueeze(1).to_broadcast(every),
                           top_f[:, :, :].unsqueeze(3).to_broadcast(every), ALU.is_equal) \
                               .then_inc(dve_chain, 1)
                        dve.wait_ge(dve_chain, count.up())
                        tt(hot[:, :, :, :], hot[:, :, :, :],
                           pair_w[:, :, :].unsqueeze(3).to_broadcast(every), ALU.mult) \
                               .then_inc(dve_chain, 1)
                        dve.wait_ge(dve_chain, count.up())
                        tt(comb[:, :, 0:EXPERTS], hot[:, :, 0, :], hot[:, :, 1, :], ALU.add) \
                            .then_inc(dve_chain, 1)
                        dve.wait_ge(dve_chain, count.up())
                        nc.vector.tensor_copy(comb3[:, :, 0, :], comb[:, :, :]) \
                            .then_inc(dve_chain, 1)
                        dve.wait_ge(dve_chain, count.up())
                        tt(rest[:, :, :], comb[:, :, :], comb3[:, :, 0, :], ALU.subtract) \
                            .then_inc(dve_chain, 1)
                        dve.wait_ge(dve_chain, count.up())
                        nc.vector.tensor_copy(comb3[:, :, 1, :], rest[:, :, :]) \
                            .then_inc(dve_chain, 1)
                        dve.wait_ge(dve_chain, count.up())
                        tt(comb3[:, :, 2, :], rest[:, :, :], comb3[:, :, 1, :], ALU.subtract) \
                            .then_inc(comb_ready, 1)
                    elif k == "cb":
                        dve.wait_ge(silu_done, s.b + 1)
                        dve.wait_ge(misc_full, s.misc + 1)
                        r = s.b % RING
                        tt(val[:, r, :], val[:, r, :], misc[:, :], ALU.mult).then_inc(misc_free, 1)
                    elif k == "ac":
                        if s.scaled > 0:
                            dve.wait_ge(misc_free, s.scaled)
                        dve.wait_ge(g_full, s.b + 1)
                        r = s.b % RING
                        tt(val[:, r, :], val[:, r, :], g_ps[s.b % HG][:, :], ALU.mult) \
                            .then_inc(act_done, 1)
                    elif k == "lo" and lo_on_dve(s.b):
                        dve.wait_ge(hi_done, s.b + 1)
                        r = s.b % RING
                        tt(act_lo[:, r, :], val[:, r, :], act_hi[:, r, :].bitcast(f32), ALU.subtract) \
                            .then_inc(lo_by_dve, 1)
                    elif k == "yt":
                        if s.x_misc:
                            dve.wait_ge(misc_free, s.x_misc)
                        if s.x_mb:
                            dve.wait_ge(mb_free, s.x_mb)
                        if s.xin == "xl" and not preloaded(i):
                            dve.wait_ge(xl_loaded, 16)
                        if s.xin == "xe":
                            dve.wait_ge(xe_ready, 1)
                        dve.wait_ge(misc_full, s.misc + 1)
                        tt(X[s.xout][:, :, :], X[s.xin][:, :, :],
                           misc[:, :].rearrange("p (t d) -> p t d", t=TILES), ALU.add) \
                            .then_inc(misc_free, 1)
                        if s.c == 1 and isinstance(i, int) and i == BATCH + 1:
                            dve.wait_ge(misc_free, s.misc + 1)
                            dve.sem_inc(xe_final, 1)
                    elif k == "x_e":
                        if not isinstance(i, int) or i >= 3:
                            dve.wait_ge(out_stored, 16)
                        nc.vector.tensor_copy(X["xe"][:, :, :], X["xc"][:, :, :]) \
                            .then_inc(xe_ready, 1)
                    elif k == "x_a":
                        if s.x_misc:
                            dve.wait_ge(misc_free, s.x_misc)
                        nc.vector.tensor_copy(X["xa"][:, :, :], X["xl"][:, :, :])
                    elif k == "m_conv":
                        j = s.t
                        if j == 0:
                            dve.wait_ge(pad_zeroed, 1)
                            dve.wait_ge(mb_free, s.mb)
                            dve.wait_ge(mc_free, s.mc)
                        for h in range(HALVES):
                            src, dst = conv[(j + 1) % 2][:, h, :], conv[j % 2][:, h, :]
                            taken = x_in[:, h, j:j + SEQ], conv_w[:, h, j:j + 1]
                            if j == 0:
                                ts(dst, *taken, None, ALU.mult).then_inc(tap_done, 1)
                            else:
                                dve.wait_ge(tap_done, HALVES * (j - 1) + h + 1)
                                stt(dst, *taken, src, ALU.mult, ALU.add).then_inc(tap_done, 1)
                    elif k == "m_bc":
                        dve.wait_ge(bc_hi, 1)
                        tt(bc_rest, bc, bc3[0:STATES, :, :], ALU.subtract) \
                            .then_inc(bc_rest_ready, 1)
                    elif k == "m_bc2":
                        dve.wait_ge(bc_mid_ready, 1)
                        dve.wait_ge(bc_rest_ready, 1)
                        tt(bc3[64:64 + STATES, :, :], bc_rest, bc_mid, ALU.subtract) \
                            .then_inc(bc_ready, 1)
                    elif k == "m_sp":
                        if s.mb > 0:
                            dve.wait_ge(mb_free, s.mb)
                        if s.mc > 0:
                            dve.wait_ge(mc_free, s.mc)
                        stt(neg_abs, dt_pre, -1.0, dt_pre, ALU.mult, ALU.min) \
                            .then_inc(negabs_ready, 1)
                    elif k == "m_sp2":
                        dve.wait_ge(log_ready, 1)
                        stt(dt[:, :, :], dt_pre, 0.0, neg_abs, ALU.max, ALU.add) \
                            .then_inc(dt_ready, 1)
                    elif k in ("m_even", "m_odd"):
                        unit = 2 * s.n - (2 if k == "m_even" else 1)
                        if 0 <= unit < UNITS:
                            dve.wait_ge(decay_ready, unit + 1)
                            dve.wait_ge(drive_ready, unit + 1)
                            r = unit % SCAN_RING
                            nc.vector.tensor_tensor_scan(scan[:, r, :], decay[:, unit % DECAY_RING, :],
                                                         scan[:, r, :], 0.0, ALU.mult, ALU.add) \
                                .then_inc(scan_done, 1)
                        if 0 <= unit - 1 < UNITS:
                            done = unit - 1
                            if s.mc + (k == "m_odd") > 0:
                                dve.wait_ge(mc_full, s.mc + (k == "m_odd"))
                            dve.wait_ge(scan_done, done + 1)
                            r = done % SCAN_RING
                            ins = tt(scan[:, r, :], scan[:, r, :], m_c[:, :], ALU.mult)
                            ins.then_inc(mc_free if done % 2 else hc_even, 1)
                    elif k in ("m_out", "a_i"):
                        if s.x_misc:
                            dve.wait_ge(misc_free, s.x_misc)
                        if s.x_mb:
                            dve.wait_ge(mb_free, s.x_mb)
                        dve.wait_ge(mb_full, s.mb + 1)
                        tt(X[s.xout][:, :, :], X[s.xin][:, :, :],
                           m_b[:, :].rearrange("p (t d) -> p t d", t=TILES), ALU.add) \
                            .then_inc(mb_free, 1)
                    elif k == "a_f":
                        ps, full, free, uses = (m_b, mb_full, mb_free, s.mb) if s.t % 2 == 0 \
                            else (m_c, mc_full, mc_free, s.mc)
                        dve.wait_ge(full, uses + 1)
                        tt(spec[:, s.t].rearrange("p n d -> p (n d)"), ps[:, 0:3 * DIM], spec_bias[:, :],
                           ALU.add).then_inc(free, 1)
                    elif k == "a_rec":
                        dve.wait_ge(mags_ready, 1)
                        nc.vector.reciprocal(rkv, rkv)
                        nc.vector.reciprocal(rq, mag[:, :, 0, :]).then_inc(dve_chain, 1)
                        count.up()
                        if count.n > 0:
                            dve.wait_ge(dve_chain, count.n)
                    elif k == "a_kv":
                        q, ky, vl = (spec[:, :, j, :] for j in range(3))
                        tt(kv[:, :, re], ky[:, :, re], vl[:, :, re], ALU.mult)
                        tt(kv[:, :, im], ky[:, :, im], vl[:, :, re1], ALU.mult)
                        tt(prod[0], ky[:, :, im], vl[:, :, im], ALU.mult)
                        tt(prod[1], ky[:, :, re1], vl[:, :, im], ALU.mult).then_inc(dve_chain, 1)
                        dve.wait_ge(dve_chain, count.up())
                        tt(kv[:, :, re1], kv[:, :, re1], prod[0], ALU.subtract)
                        tt(kv[:, :, im], kv[:, :, im], prod[1], ALU.add).then_inc(dve_chain, 1)
                        dve.wait_ge(dve_chain, count.up())
                        tt(kv[:, :, re], kv[:, :, re], rkv, ALU.mult)
                        tt(kv[:, :, im], kv[:, :, im], rkv[:, :, re1], ALU.mult) \
                            .then_inc(kv_ready, 1)
                        tt(q[:, :, re], q[:, :, re], rq, ALU.mult)
                        tt(q[:, :, im], q[:, :, im], rq[:, :, re1], ALU.mult).then_inc(dve_chain, 1)
                        dve.wait_ge(dve_chain, count.up())
                    elif k == "a_o":
                        q = spec[:, :, 0, :]
                        sums = m_b[:, :].rearrange("p (t d) -> p t d", t=TILES)
                        if s.mb > 0:
                            dve.wait_ge(mb_full, s.mb)
                        tt(spec_out[:, :, re], sums[:, :, re], q[:, :, re], ALU.mult)
                        tt(spec_out[:, :, im], sums[:, :, im], q[:, :, re1], ALU.mult)
                        tt(prod[0], sums[:, :, im], q[:, :, im], ALU.mult)
                        tt(prod[1], sums[:, :, re1], q[:, :, im], ALU.mult).then_inc(mb_free, 1)
                        if s.mb > 0:
                            dve.wait_ge(mb_free, s.mb)
                        tt(spec_out[:, :, re1], spec_out[:, :, re1], prod[0], ALU.add)
                        tt(spec_out[:, :, im], spec_out[:, :, im], prod[1], ALU.subtract) \
                            .then_inc(out_spec_ready, 1)
                dve.drain()
                dve.sem_inc(arrived, 1)
                dve.wait_ge(go_dve, 1)
                dve.sem_clear(go_dve)
            run(dve, segment)

        @block.gpsimd
        def _(pool):
            tt = nc.gpsimd.tensor_tensor

            def meet_all():
                pool.drain()
                pool.wait_ge(arrived, len(go))
                pool.sem_clear(range(of_segment[0].num, of_segment[-1].num + 1))
                for sem in go:
                    pool.sem_inc(sem, 1)

            meet_all()

            def segment(i, steps):
                count = Count()

                def drive(s, unit):
                    n, h = divmod(unit, HALVES)
                    if s.mb + (s.kind == "m_even") > 0:
                        pool.wait_ge(mb_free, s.mb + (s.kind == "m_even"))
                    if unit - SCAN_RING + 1 > 0:
                        pool.wait_ge(y_added, unit - SCAN_RING + 1)
                    tt(scan[:, unit % SCAN_RING, :], dtu[:, h, :], b_sb[:, n % 2, :], ALU.mult) \
                        .then_inc(drive_ready, 1)

                for s in steps:
                    k = s.kind
                    if k == "ln_a":
                        pool.wait_ge(ln_stats, s.no + 1)
                        nc.gpsimd.tensor_scalar(var_eps[:, :], moments[:, s.no % 2, :, 1], LN_EPS,
                                                None, ALU.add).then_inc(pool_chain, 1)
                        pool.wait_ge(pool_chain, count.up())
                        tt(rstd[:, s.no % 2, :], var_eps[:, :], minus_half[:, :], ALU.pow) \
                            .then_inc(ln_rstd, 1)
                    elif k == "lo" and not lo_on_dve(s.b):
                        pool.wait_ge(hi_done, s.b + 1)
                        r = s.b % RING
                        tt(act_lo[:, r, :], val[:, r, :], act_hi[:, r, :].bitcast(f32), ALU.subtract) \
                            .then_inc(lo_by_pool, 1)
                    elif k == "m_in":
                        nc.gpsimd.memset(x_in[:, :, 0:TAPS - 1], 0.0).then_inc(pad_zeroed, 1)
                    elif k == "m_sp2":
                        pool.wait_ge(dt_ready, 1)
                        nc.gpsimd.memset(decay[:, :, 0:1], 0.0)
                        tt(dtu[:, :, :], dt[:, :, :], u[:, :, :], ALU.mult).then_inc(dtu_ready, 1)
                    elif k == "m_even" and s.n < STATES:
                        if s.n == 0:
                            pool.wait_ge(dtu_ready, 1)
                        drive(s, 2 * s.n)
                    elif k == "m_odd":
                        for unit in (2 * s.n - 4, 2 * s.n - 3):
                            if unit < 0:
                                continue
                            h, r = unit % HALVES, unit % SCAN_RING
                            pool.wait_ge(y_started, HALVES)
                            if h == 0:
                                pool.wait_ge(hc_even, unit // 2 + 1)
                            else:
                                if s.mc > 0:
                                    pool.wait_ge(mc_free, s.mc)
                            if unit - 1 > 0:
                                pool.wait_ge(y_added, unit - 1)
                            tt(u[:, h, :], u[:, h, :], scan[:, r, :], ALU.add) \
                                .then_inc(y_added, 1)
                        if s.n < STATES:
                            drive(s, 2 * s.n + 1)
                    elif k == "m_gate":
                        if s.mb > 0:
                            pool.wait_ge(mb_free, s.mb)
                        if s.mc > 0:
                            pool.wait_ge(mc_free, s.mc)
                        pool.wait_ge(y_added, UNITS)
                        tt(u[:, :, :], u[:, :, :], dt[:, :, :], ALU.mult).then_inc(yz_ready, 1)
                    elif k == "a_pow":
                        pool.wait_ge(sq_ready, 1)
                        pairs = power[:, :, :, 1:1 + IMAG]
                        tt(pairs, pairs, power[:, :, :, REAL:DIM], ALU.add) \
                            .then_inc(power_ready, 1)
                    elif k == "a_mag":
                        pool.wait_ge(mag_ready, 1)
                        nc.gpsimd.tensor_scalar(mag, mag, MAG_EPS, None, ALU.add) \
                            .then_inc(pool_chain, 1)
                        pool.wait_ge(pool_chain, count.up())
                        tt(rkv, mag[:, :, 1, :], mag[:, :, 2, :], ALU.mult) \
                            .then_inc(mags_ready, 1)
                meet_all()
            run(pool, segment)


def kernel(**inputs):
    import numpy as _np
    import concourse.bacc as _bacc
    from concourse.bass_utils import run_bass_kernel_spmd as _run

    a = {name: _np.asarray(v) for name, v in inputs.items()}

    def rows(w):
        n = w.shape[0] // P
        return w.reshape(n, P, -1).transpose(1, 0, 2).reshape(P, -1)

    def halves(v):
        return v.reshape(HALVES, P, -1).transpose(1, 0, 2)

    def ups(w):
        return w.transpose(1, 0, 2).reshape(DIM, -1)

    def with_shared(w, sw):
        return _np.concatenate([a["L1_ffn_" + w], a["L1_ffn_" + sw]], axis=0)

    split = _np.concatenate([
        a["L0_ffn_Wr"], a["L1_ffn_router_w"].T, ups(a["L0_ffn_W1"]), ups(a["L0_ffn_W3"]),
        rows(a["L0_ffn_W2"].reshape(-1, DIM)), a["L0_attn_W_in"].T, ups(with_shared("w1", "sw1")),
        ups(with_shared("w3", "sw3")), rows(with_shared("w2", "sw2").reshape(-1, DIM))], axis=1)

    angle = 2 * _np.pi * _np.outer(_np.arange(DIM), _np.arange(REAL)) / DIM
    cos, sin = _np.cos(angle), _np.sin(angle)[:, 1:REAL - 1]
    dft = _np.concatenate([cos, -sin], axis=1).astype(_np.float32)
    weight = _np.where(_np.isin(_np.arange(REAL), (0, REAL - 1)), 1.0, 2.0) / DIM
    idft = _np.concatenate([cos * weight, -sin * 2.0 / DIM], axis=1).T.astype(_np.float32)

    proj = _np.concatenate([a["L1_attn_W" + n] for n in "qkv"] + [dft] +
                           [a["L1_attn_b" + n][:, None] for n in "qkv"], axis=1)
    xp = halves(a["L0_attn_W_xproj"].T)
    xproj = _np.zeros((P, HALVES, P), _np.float32)
    xproj[:, :, 0:RANK] = xp[:, :, 0:RANK]
    xproj[:, :, 32:32 + STATES] = xp[:, :, RANK:RANK + STATES]
    xproj[:, :, 64:64 + STATES] = xp[:, :, RANK + STATES:]
    vec = halves(_np.concatenate([a["L0_attn_conv_w"], a["L0_attn_A_log"]] +
                                 [a["L0_attn_" + n][:, None] for n in ("conv_b", "b_dt", "D_skip")],
                                 axis=1))
    const = _np.concatenate([_np.eye(P), _np.triu(_np.ones((P, P))), idft, _np.ones((P, P)),
                             _np.tile(_np.arange(EXPERTS), (P, 1))], axis=1).astype(_np.float32)
    bf16 = mybir.dt.np(mybir.dt.bfloat16)
    sel = _np.zeros((PARTS * GATES, GATES * P))
    selbc = _np.zeros((PARTS * 32, STATES * P))
    for part in range(PARTS):
        for e in range(GATES):
            sel[part * GATES + e, e * P:(e + 1) * P] = 1
        for n in range(STATES):
            selbc[part * 32 + n, n * P:(n + 1) * P] = 1

    arrays = {
        "x_dram": a["L0_attn_x"], "split_dram": split, "proj_dram": proj, "xproj_dram": xproj,
        "wdt_dram": a["L0_attn_W_dt"].T, "wout_dram": halves(a["L0_attn_W_out"].T), "vec_dram": vec,
        "bias_dram": a["L1_ffn_experts_bias"], "const_dram": const,
        "identb_dram": _np.eye(P).astype(bf16), "sel_dram": sel.astype(bf16),
        "selbc_dram": selbc.astype(bf16)}
    arrays = {name: _np.ascontiguousarray(v) for name, v in arrays.items()}

    nc = _bacc.Bacc("TRN2", target_bir_lowering=False, num_devices=1)
    args = [nc.dram_tensor(name, v.shape, mybir.dt.from_np(v.dtype), kind="ExternalInput").ap()
            for name, v in arrays.items()]
    out = nc.dram_tensor("out_dram", (BATCH, SEQ, DIM), mybir.dt.float32, kind="ExternalOutput").ap()
    macaron_kernel(nc, *args, out)
    r = _run(nc, [arrays], core_ids=[0])
    return r.results[0]["out_dram"]
```

```python
import concourse.bass as bass
from concourse import mybir
from contextlib import ExitStack
import numpy as np

BATCH, SEQ, DIM = 8, 512, 128
P = 128
TILES = SEQ // P
INNER, HALVES, STATES, TAPS, RANK = 256, 2, 16, 4, 8
EXPERTS = 8
HID0, HID1 = 192, 256
BLOCKS0 = EXPERTS * HID0 // P
BLOCKS1 = (EXPERTS + 1) * HID1 // P
PARTS = 3
REAL, IMAG = DIM // 2 + 1, DIM // 2 - 1
LN_EPS, MAG_EPS = 1e-5, 1e-8

COL, _at = {}, 0
for _name, _w in (("r0", EXPERTS), ("r1", EXPERTS), ("up0", BLOCKS0 * P), ("gate0", BLOCKS0 * P),
                  ("in", 2 * INNER), ("up1", BLOCKS1 * P), ("gate1", BLOCKS1 * P)):
    COL[_name], _at = _at, _at + _w
SPLIT_COLS = _at
CHUNKS = 8
CHUNK = SPLIT_COLS // CHUNKS
SETUP_CHUNKS = -(-COL["in"] // CHUNK)

CALLS = {0: dict(layer=0, xin="xb", xout="xc", set=0), 1: dict(layer=1, xin="xe", xout="xe", set=1),
         2: dict(layer=1, xin="xc", xout="xc", set=0), 3: dict(layer=0, xin="xl", xout="xl", set=1)}
MIXER_SET = 2
BLOCKS = (BLOCKS0, BLOCKS1)
HG, LAG = 2, 2
RING = 5
EXP_STATES = 4
PLACES = {
    (0, 3, 2, 1, True): dict(
        prep3=(2, 15, 24, 29, 39, 39, 44),
        prep2=(63, 66, 71, 78, 86, 88, 92),
        prep1=(99, 103, 116, 134, 143, 148, 158),
        mamba=(0, 0, 3, 7, 9, 12, 14, 14, 20, 20, 28, 28, 31, 34, 41, 48, 48, 54, 56, 63, 69, 72,
            72, 73, 74, 77, 78, 90, 91, 97, 97, 99, 106, 108, 108, 111, 113, 116, 123, 125, 125,
            130, 131, 132, 137, 139, 148, 154, 154, 159, 165, 173, 173, 173, 178, 178, 178, 183),
        next=(190, 201, 203, 207, 211, 222, 231),
        attn=(181, 185, 190, 194, 196, 198, 198, 200, 210, 217, 226, 233, 233, 239, 240),
        x_e=(46,),
        cb_pool=(0, 2, 3, 4, 5, 6, 7, 8, 9, 10, 15, 16, 26, 38, 43, 45, 46, 47, 50, 54, 56, 59)),
    (0, 3, 2, True): dict(
        prep3=(3, 22, 27, 32, 37, 44, 44),
        prep2=(63, 68, 73, 82, 89, 89, 91),
        mamba=(0, 0, 2, 9, 11, 12, 15, 19, 23, 24, 30, 30, 33, 41, 41, 43, 44, 46, 47, 49, 50, 54,
            55, 58, 59, 59, 63, 68, 68, 74, 77, 77, 79, 79, 85, 90, 90, 97, 97, 102, 102, 105,
            105, 108, 110, 115, 116, 124, 128, 133, 138, 142, 142, 145, 149, 149, 153, 155),
        next=(159, 161, 166, 168, 168, 168, 168),
        attn=(168, 168, 168, 168, 168, 168, 168, 168, 168, 168, 168, 168, 168, 168, 168),
        cb_pool=(2, 3, 4, 6, 7, 8, 10, 14, 39, 40, 41)),
    (0, 2, 1, True): dict(
        prep1=(48, 64, 68, 80, 83, 101, 109),
        mamba=(1, 1, 3, 7, 10, 14, 15, 15, 19, 19, 24, 24, 30, 34, 38, 42, 42, 44, 48, 48, 49, 56,
            56, 58, 59, 59, 65, 67, 69, 71, 75, 77, 79, 79, 80, 82, 86, 89, 94, 97, 97, 101, 103,
            103, 107, 111, 113, 116, 120, 130, 130, 135, 135, 138, 138, 141, 145, 151),
        next=(161, 165, 176, 181, 185, 187, 191),
        attn=(139, 144, 151, 154, 154, 154, 154, 154, 164, 168, 180, 185, 187, 191, 192),
        x_e=(18,),
        cb_pool=(1, 3, 5, 6, 7, 28, 37, 38, 42, 44, 45, 46, 47)),
    (3, True): dict(
        mamba=(0, 0, 0, 0, 2, 2, 2, 5, 12, 12, 17, 17, 21, 21, 22, 22, 22, 23, 24, 24, 24, 24, 24,
            24, 24, 24, 24, 24, 24, 24, 24, 24, 24, 24, 25, 25, 25, 25, 25, 26, 26, 26, 26, 26,
            26, 26, 26, 26, 26, 26, 27, 27, 27, 27, 27, 30, 32, 36),
        next=(38, 42, 42, 45, 46, 47, 47),
        cb_pool=(0, 1, 2, 4, 5, 6, 8, 9, 10)),
    (0, 2, 1, False): dict(
        prep1=(48, 49, 49, 50, 56, 81, 102),
        attn=(132, 137, 142, 145, 145, 146, 146, 147, 153, 170, 176, 185, 185, 191, 192),
        x_e=(3,),
        cb_pool=(0, 3, 6, 8, 9, 10, 11, 13, 15, 18, 19, 21, 24, 25, 26, 27, 28, 29, 32, 35, 36,
            41, 42, 43, 45)),
}
DECAY_RING, SCAN_RING = 6, 4
SPREAD_RING = 4


def experts_of(layer, k):
    if layer == 1:
        return [(slice(0, P), k // 2)]
    pair, r = divmod(k, 3)
    both = [(slice(0, P // 2), 2 * pair), (slice(P // 2, P), 2 * pair + 1)]
    return ([(slice(0, P), 2 * pair)], both, [(slice(0, P), 2 * pair + 1)])[r]


def is_shared(layer, k):
    return layer == 1 and k * P >= EXPERTS * HID1


class Step:

    def __init__(self, kind, c=None, k=None, n=None, t=None, b=None, src=None,
                 set=None, layer=None):
        self.kind, self.c, self.k, self.n, self.t, self.b = kind, c, k, n, t, b
        self.src, self.set, self.layer = src, set, layer
        self.x_misc = self.x_mb = 0


def prep_steps(c):
    about = dict(src=CALLS[c]["xin"], set=CALLS[c]["set"], layer=CALLS[c]["layer"])
    return [Step(k, **about) for k in ("ln_a", "ln_b", "ln_c", "rt_l", "rt_a", "rt_b", "rt_c")]


def mamba_steps():
    about = dict(src="xa", set=MIXER_SET)
    m = [Step(k, **about) for k in ("ln_a", "ln_b", "ln_c")] + [Step("m_in")]
    m += [Step("m_conv", t=t) for t in range(TAPS)]
    m += [Step(k) for k in ("m_xp", "m_bc", "m_bc2", "m_dt", "m_sp", "m_sp2", "m_sp3")]
    for n in range(STATES + 2):
        if n % EXP_STATES == 0 and n < STATES:
            m.append(Step("m_exp", n=n))
        m += [Step("m_even", n=n), Step("m_odd", n=n)]
    return m + [Step(k) for k in ("m_z", "m_gate", "m_out")]


def attn_steps():
    about = dict(src="xc", set=MIXER_SET)
    return [Step(k, **about) for k in ("ln_a", "ln_b", "ln_c")] + \
        [Step("a_f", t=t) for t in range(TILES)] + \
        [Step(k) for k in ("a_pow", "a_mag", "a_rec", "a_kv", "a_cum", "a_o", "a_t", "a_i")]


def spread(steps, first, last):
    n = max(1, len(steps) - 1)
    return [first + (last - first) * i // n for i in range(len(steps))]


def segment_steps(calls, mamba, attn, next_xa, first=False):
    blocks = [(c, k) for c in calls for k in range(BLOCKS[CALLS[c]["layer"]])]
    start = {c: blocks.index((c, 0)) for c in calls}
    places = PLACES.get(tuple(calls) + (mamba,), {})
    alone = [j for j in range(1, len(blocks)) if blocks[j][1] == 0 and
             CALLS[blocks[j][0]]["xin"] == CALLS[blocks[j - 1][0]]["xout"]]
    extra, end = [], 4 * len(blocks)

    def place(steps, name, first, last):
        at = places.get(name) or spread(steps, first, last)
        extra.extend((q, len(extra) + i, s) for i, (q, s) in enumerate(zip(at, steps)))

    for before, c in zip(calls, calls[1:]):
        if start[c] not in alone:
            place(prep_steps(c), f"prep{c}", 4 * start[before] + 18, 4 * start[c] - 6)
    if mamba:
        place(mamba_steps(), "mamba", 0, 4 * start[1] + 8 if 1 in calls else end - 1)
        place(prep_steps(0), "next", end, end)
    if attn:
        place(attn_steps(), "attn", *((4 * start[1] + 14, end - 1) if 1 in calls else (end, end)))
    if 1 in calls:
        place([Step("x_e")], "x_e", *((19, 19) if calls[0] != 1 else (-1, -1)))
    if first:
        place([Step("w_split", t=j) for j in range(SETUP_CHUNKS, CHUNKS)], "split", 16, 40)
    extra.sort(key=lambda e: e[:2])
    steps = []

    def others(quarter):
        while extra and extra[0][0] <= quarter:
            steps.append(extra.pop(0)[2])

    def add(kind, j):
        if 0 <= j < len(blocks):
            c, k = blocks[j]
            if kind == "cb" and is_shared(CALLS[c]["layer"], k):
                return
            steps.append(Step(kind, c=c, k=k, b=j))
            if kind == "down" and k == BLOCKS[CALLS[c]["layer"]] - 1:
                due.extend(Step(kind, c=c, b=j + 1) for kind in ("ye", "yt"))

    due, flushed = [], 0
    others(-1)
    if calls[0] != 0:
        steps += prep_steps(calls[0])
    add("uh", 0)
    for j in range(len(blocks)):
        if due:
            steps.append(due.pop(0))
        if j > flushed:
            add("ac", j - 1)
        others(4 * j)
        if j + 1 not in alone:
            add("uh", j + 1)
        others(4 * j + 1)
        add("ug", j)
        add("cb", j)
        others(4 * j + 2)
        if j - LAG >= flushed:
            add("down", j - LAG)
        others(4 * j + 3)
        if j + 1 == len(blocks) or j + 1 in alone:
            add("ac", j)
            for older in range(max(flushed, j - LAG + 1), j + 1):
                add("down", older)
            steps += due
            due, flushed = [], j + 1
            if j + 1 in alone:
                steps += prep_steps(blocks[j + 1][0])
                add("uh", j + 1)
    others(end)
    if next_xa:
        steps.append(Step("x_a"))

    at = 0
    for j, (c, k) in enumerate(blocks):
        layer = CALLS[c]["layer"]
        if is_shared(layer, k) or (layer == 1 and k % 2):
            continue
        up = [i for i, s in enumerate(steps) if s.kind == "uh" and s.b in (j - 1, j)]
        ready = [i + 1 for i, s in enumerate(steps[:up[-1]]) if s.kind == "rt_c" and
                 (s.src, s.set) == (CALLS[c]["xin"], CALLS[c]["set"])]
        at = max([at, up[0]] + ready)
        steps.insert(at, Step("spread", c=c, k=k, b=j))
        at += 1
    return number(steps, calls, places.get("cb_pool", ()))


def number(steps, calls, cb_pool):
    misc = mb = mc = 0
    x_at, x_by = {}, {}
    scaled, cbs = {}, [0, 0]
    uses, filled, blocks_of = {}, [0] * SPREAD_RING, {}
    nos = {}
    for s in steps:
        s.misc, s.mb, s.mc = misc, mb, mc
        kind = s.kind
        s.no = nos.get(kind, 0)
        nos[kind] = s.no + 1
        if s.c is not None:
            s.layer, s.set = CALLS[s.c]["layer"], CALLS[s.c]["set"]
            s.nth = calls.index(s.c)
        s.cbs = tuple(cbs)
        s.dve_adds = len(calls) == 1
        if kind == "spread":
            use = s.no
            s.buf = use % SPREAD_RING
            s.experts = experts_of(s.layer, s.k)
            filled[s.buf] += 16 * len(s.experts)
            s.freed = [scaled[b] for b in blocks_of.get(use - SPREAD_RING, ())]
            blocks_of[use] = (s.b, s.b + 1)[:1 + (s.layer == 1)]
            for b in blocks_of[use]:
                uses[b] = s.buf, filled[s.buf]
        if kind == "cb":
            s.by_pool = s.b in cb_pool
            cbs[s.by_pool] += 1
            scaled[s.b] = s.by_pool, cbs[s.by_pool]
            s.buf, s.filled = uses[s.b]
        if kind == "ac":
            s.shared = is_shared(s.layer, s.k)
            s.scaled = scaled.get(s.b)
        if kind == "ln_a":
            assert nos["ln_a"] - nos.get("ln_c", 0) <= 2
            s.x_misc, s.x_mb = x_by.get(s.src, (0, 0))
        if kind in ("ln_b", "ln_c"):
            assert [t.src for t in steps if t.kind == kind][s.no] == \
                [t.src for t in steps if t.kind == "ln_a"][s.no]
        if kind == "ln_c":
            x_at[s.set] = misc + 1
        if kind in ("uh", "ug", "rt_l"):
            s.x_at = x_at.get(s.set, 0)
        if kind in ("m_in", "m_z", "a_f"):
            s.x_at = x_at[MIXER_SET]
        if kind == "x_a":
            s.x_misc, s.x_mb = x_by["xl"]
        if kind == "yt":
            s.xin, s.xout = CALLS[s.c]["xin"], CALLS[s.c]["xout"]
            s.x_misc, s.x_mb = x_by.get(s.xin, (0, 0))
            x_by[s.xout] = (misc + 1, 0)
        if kind in ("m_out", "a_i"):
            s.xin, s.xout = ("xa", "xb") if kind == "m_out" else ("xc", "xc")
            s.x_misc, s.x_mb = x_by.get(s.xin, (0, 0))
            x_by[s.xout] = (0, mb + 1)
        misc += kind in ("ln_c", "rt_l", "rt_a", "rt_c", "yt")
        mb += kind in ("m_in", "m_z", "m_dt", "m_xp", "m_out", "a_cum", "a_i") or \
            (kind == "m_even" and s.n < STATES) or (kind == "a_f" and s.t % 2 == 0)
        mc += kind in ("m_in", "m_z", "m_dt", "a_t") or \
            (kind == "m_odd" and 1 <= s.n <= STATES) or (kind == "a_f" and s.t % 2 == 1)
    return steps


def macaron_kernel(nc, x_dram, split_dram, down_dram, proj_dram, xproj_dram, wdt_dram, wout_dram,
                   vec_dram, bias_dram, const_dram, selbc_dram, comb_dram, out_dram):
    f32, r32, bf16, u32 = mybir.dt.float32, mybir.dt.float32r, mybir.dt.bfloat16, mybir.dt.uint32
    ALU, ACT = mybir.AluOpType, mybir.ActivationFunctionType

    ctx = ExitStack()
    with ctx:
        def sb(name, shape, dt=f32):
            return ctx.enter_context(nc.sbuf_tensor(name, shape, dt))

        def bank(name):
            return ctx.enter_context(nc.psum_tensor(name, [P, SEQ], f32))

        w_hi, w_lo = sb("w_hi", [P, SPLIT_COLS], r32), sb("w_lo", [P, SPLIT_COLS], r32)
        w_down = sb("w_down", [P, (BLOCKS0 + BLOCKS1) * P])
        wf_hi, wf_lo = sb("wf_hi", [P, 3 * DIM], r32), sb("wf_lo", [P, 3 * DIM], r32)
        spec_bias = sb("spec_bias", [P, 3 * DIM])
        xproj = sb("xproj", [P, HALVES, P])
        wdt = sb("wdt", [RANK, INNER])
        wout = sb("wout", [P, HALVES, DIM])
        vec = sb("vec", [P, HALVES, TAPS + STATES + 3])
        conv_w, a_log = vec[:, :, 0:TAPS], vec[:, :, TAPS:TAPS + STATES]
        conv_b, b_dt, d_skip = (vec[:, :, TAPS + STATES + j:TAPS + STATES + j + 1] for j in range(3))
        a_neg = sb("a_neg", [P, HALVES, STATES])
        const = sb("const", [P, 4 * P + EXPERTS])
        ident, tri, idft, ones = (const[:, j * P:(j + 1) * P] for j in range(4))
        iota = const[:, 4 * P:4 * P + EXPERTS]
        selbc = sb("selbc", [PARTS * 32, STATES * P], bf16)
        router_bias = sb("router_bias", [P, 2, EXPERTS])
        minus_half = sb("minus_half", [P, TILES])

        X = {n: sb(n, [P, TILES, DIM]) for n in ("xl", "xa", "xb", "xc", "xe")}

        stats = sb("stats", [P, TILES, 6])
        moments = sb("moments", [P, 2, TILES, 2])
        var_eps = sb("var_eps", [P, TILES])
        rstd = sb("rstd", [P, 2, TILES])
        xn = sb("xn", [P, 2, TILES, DIM])
        xt_hi, xt_lo = sb("xt_hi", [P, 3, SEQ], r32), sb("xt_lo", [P, 3, SEQ], r32)
        top_at = sb("top_at", [P, TILES, 8], u32)
        top_f = sb("top_f", [P, TILES, 2])
        gap, th = sb("gap", [P, TILES]), sb("th", [P, TILES])
        pair_w = sb("pair_w", [P, TILES, 2])
        hot = sb("hot", [P, TILES, 2, EXPERTS])
        logits, top = hot[:, :, 0, :], hot[:, :, 1, :]
        comb = sb("comb", [P, TILES, EXPERTS])
        both_t = sb("both_t", [32 + EXPERTS, SEQ])
        comb_t = both_t[0:EXPERTS, :]
        spread_w = sb("spread_w", [P, SPREAD_RING, SEQ])
        logits_t = both_t[32:32 + EXPERTS, :]
        ident_logits = ident[32:32 + EXPERTS, 32:32 + EXPERTS]

        val = sb("val", [P, RING, SEQ])
        y_t = sb("y_t", [P, SEQ])

        u = sb("u", [P, HALVES, SEQ])
        dt = sb("dt", [P, HALVES, SEQ])
        dtu = sb("dtu", [P, HALVES, SEQ])
        decay = sb("decay", [P, DECAY_RING, HALVES, SEQ])
        b_sb = sb("b_sb", [P, 2, SEQ])
        scan = sb("scan", [P, SCAN_RING, HALVES, SEQ])
        bc3 = sb("bc3", [PARTS * 32, 2, SEQ], bf16)

        decay_flat = decay[:, :, :, :].rearrange("p a b c -> p (a b c)")
        scan_flat = scan[:, :, :, :].rearrange("p a b c -> p (a b c)")
        staging = decay_flat[:, 0:2 * CHUNK]
        proj = scan_flat[:, 0:4 * DIM + 3]
        dft = proj[:, 3 * DIM:4 * DIM]
        bias_cols = scan_flat[:, 5 * DIM:8 * DIM]
        wide = HALVES * SEQ
        x_in = decay_flat[:, 0:HALVES * (TAPS - 1 + SEQ)].rearrange("p (h t) -> p h t", h=HALVES)
        conv = [decay_flat[:, j * wide:(j + 1) * wide].rearrange("p (h t) -> p h t", h=HALVES)
                for j in (2, 3)]
        dt_pre, neg_abs, dt_exp = (decay_flat[:, j * wide:(j + 1) * wide]
                                   .rearrange("p (h t) -> p h t", h=HALVES) for j in (0, 1, 2))
        bc = scan_flat[0:STATES, 0:2 * SEQ].rearrange("p (j t) -> p j t", j=2)
        bc_rest = scan_flat[0:STATES, 2 * SEQ:4 * SEQ].rearrange("p (j t) -> p j t", j=2)
        bc_mid = scan_flat[0:STATES, 4 * SEQ:5 * SEQ].bitcast(bf16).rearrange("p (j t) -> p j t", j=2)
        dt_lo = b_sb[0:RANK, 0, :]

        def piece(flat, at, *dims):
            n = int(np.prod(dims))
            ap = flat[:, at:at + n]
            if len(dims) == 2:
                return ap.rearrange("p (a b) -> p a b", a=dims[0])
            return ap.rearrange("p (a b c) -> p a b c", a=dims[0], b=dims[1])

        spec = piece(scan_flat, 0, TILES, 3, DIM)
        kv = piece(scan_flat, 3 * SEQ, TILES, DIM)
        o_t = scan_flat[:, 4 * SEQ:5 * SEQ]
        power = piece(decay_flat, 0, TILES, 3, DIM)
        spec_out = piece(decay_flat, 0, TILES, DIM)
        prod = [piece(decay_flat, (3 + j) * SEQ // 1, TILES, IMAG) for j in range(2)]
        mag = piece(decay_flat, 5 * SEQ, TILES, 3, REAL)
        rq = piece(decay_flat, 5 * SEQ + 3 * TILES * REAL, TILES, REAL)
        rkv = piece(decay_flat, 5 * SEQ + 4 * TILES * REAL, TILES, REAL)

        h_ps = [bank(f"h_ps{j}") for j in range(HG)]
        g_ps = [bank(f"g_ps{j}") for j in range(HG)]
        y_ps, misc, m_b, m_c = bank("y_ps"), bank("misc"), bank("m_b"), bank("m_c")

        (h_full, g_full, silu_done, act_done, hi_done, lo_done, w_hi_done, down_done, y_copied,
         misc_full, misc_free, mb_full, mb_free, mc_full, mc_free, ln_stats, ln_rstd, ln_xn,
         ln_hi, gap_ready, th_ready, comb_ready, comb_copied, comb_stored, cb_dve, cb_pool,
         spread_0, spread_1, spread_2, spread_3, xl_loaded, xe_final, xe_ready, out_stored,
         pad_zeroed, tap_done, u_ready, dtlo_ready, bc_copied, bc_hi, bc_rest_ready, bc_mid_ready,
         bc_ready, bc_parts, negabs_ready, log_ready, dt_ready, dtu_ready, y_started,
         decay_ready, drive_ready, scan_done, y_added, yz_ready, sq_ready,
         power_ready, mag_ready, mags_ready, kv_ready, out_spec_ready, dve_chain, act_chain,
         pool_chain, arrived) = of_segment = [ctx.enter_context(nc.semaphore(name)) for name in (
            "h_full", "g_full", "silu_done", "act_done", "hi_done", "lo_done", "w_hi_done", "down_done",
            "y_copied", "misc_full", "misc_free", "mb_full", "mb_free", "mc_full",
            "mc_free", "ln_stats", "ln_rstd", "ln_xn", "ln_hi", "gap_ready", "th_ready",
            "comb_ready", "comb_copied", "comb_stored", "cb_dve", "cb_pool",
            "spread_0", "spread_1", "spread_2", "spread_3", "xl_loaded", "xe_final", "xe_ready",
            "out_stored", "pad_zeroed", "tap_done",
            "u_ready", "dtlo_ready", "bc_copied", "bc_hi", "bc_rest_ready", "bc_mid_ready", "bc_ready",
            "bc_parts", "negabs_ready", "log_ready", "dt_ready", "dtu_ready", "y_started",
            "decay_ready", "drive_ready", "scan_done", "y_added", "yz_ready",
            "sq_ready", "power_ready", "mag_ready", "mags_ready", "kv_ready",
            "out_spec_ready", "dve_chain", "act_chain", "pool_chain", "arrived")]
        go_sync, go_act, go_dve, go_pe = go = [ctx.enter_context(nc.semaphore(f"go_{e}"))
                                               for e in ("sync", "act", "dve", "pe")]
        spread_full = (spread_0, spread_1, spread_2, spread_3)
        w_loaded = [ctx.enter_context(nc.semaphore(f"w_loaded{j}")) for j in range(2)]
        down_loaded = ctx.enter_context(nc.semaphore("down_loaded"))
        small_loaded = ctx.enter_context(nc.semaphore("small_loaded"))
        block = ctx.enter_context(nc.Block())

        class Count:

            def __init__(self):
                self.n = 0

            def up(self):
                self.n += 1
                return self.n

        def preloaded(i):
            return isinstance(i, int) and i == -1

        def steps_of(i):
            calls = [c for c, on in ((0, 1 <= i <= BATCH), (3, -1 <= i <= BATCH - 2),
                                     (2, 1 <= i <= BATCH), (1, 2 <= i <= BATCH + 1)) if on]
            return segment_steps(calls, 0 <= i < BATCH, 1 <= i <= BATCH, 3 in calls, i == -1)

        LOOP_FROM, LOOP_TO = 3, BATCH - 1

        def run(e, segment):
            for i in range(-1, LOOP_FROM):
                segment(i, steps_of(i))
            full = steps_of(LOOP_FROM)
            with e.Fori(LOOP_FROM, LOOP_TO) as i:
                segment(i, full)
            for i in range(LOOP_TO, BATCH + 2):
                segment(i, steps_of(i))

        small = [(const[:, :], const_dram), (proj, proj_dram), (vec[:, :, :], vec_dram),
                 (wdt[:, :], wdt_dram), (xproj[:, :, :], xproj_dram), (wout[:, :, :], wout_dram),
                 (selbc[:, :], selbc_dram),
                 (router_bias[:, 1, :], bias_dram.partition_broadcast(P)),
                 (w_down[:, 0:BLOCKS0 * P], down_dram[:, 0:BLOCKS0 * P]),
                 (X["xl"][:, :, :], x_dram[0].rearrange("(t p) d -> p t d", p=P))]

        @block.sync
        def _(sp):
            for j in range(SETUP_CHUNKS):
                if j >= 2:
                    sp.wait_ge(lo_done, j - 1)
                sp.dma_start(staging[:, (j % 2) * CHUNK:(j % 2 + 1) * CHUNK],
                             split_dram[:, j * CHUNK:(j + 1) * CHUNK]).then_inc(w_loaded[j % 2], 16)
                if j == 1:
                    for dst, src in small:
                        sp.dma_start(dst, src).then_inc(small_loaded, 16)
            sp.drain()
            sp.sem_inc(arrived, 1)
            sp.wait_ge(go_sync, 1)
            sp.sem_clear(go_sync)

            def segment(i, steps):
                kinds = {(s.kind, s.c) for s in steps}
                if preloaded(i):
                    for j in range(SETUP_CHUNKS, SETUP_CHUNKS + 2):
                        sp.dma_start(staging[:, (j % 2) * CHUNK:(j % 2 + 1) * CHUNK],
                                     split_dram[:, j * CHUNK:(j + 1) * CHUNK]) \
                            .then_inc(w_loaded[j % 2], 16)
                    sp.dma_start(w_down[:, BLOCKS0 * P:], down_dram[:, BLOCKS0 * P:]) \
                        .then_inc(down_loaded, 16)

                def load_and_store():
                    if ("ug", 3) in kinds and not preloaded(i):
                        sp.dma_start(X["xl"][:, :, :],
                                     x_dram[i + 1].rearrange("(t p) d -> p t d", p=P)) \
                            .then_inc(xl_loaded, 16)
                    if not isinstance(i, int) or i >= 3:
                        sp.dma_start(out_dram[i - 3].rearrange("(t p) d -> p t d", p=P),
                                     X["xe"][:, :, :]).then_inc(out_stored, 16)

                at_once = ("ug", 0) in kinds
                if not at_once:
                    load_and_store()
                for s in steps:
                    if s.kind == "w_split" and s.t + 2 < CHUNKS:
                        j = s.t + 2
                        sp.wait_ge(lo_done, s.t - SETUP_CHUNKS + 1)
                        sp.dma_start(staging[:, (j % 2) * CHUNK:(j % 2 + 1) * CHUNK],
                                     split_dram[:, j * CHUNK:(j + 1) * CHUNK]) \
                            .then_inc(w_loaded[j % 2], 16)
                    elif s.kind == "rt_c":
                        sp.wait_ge(comb_copied, s.no + 1)
                        if s.cbs[0]:
                            sp.wait_ge(cb_dve, s.cbs[0])
                        if s.cbs[1]:
                            sp.wait_ge(cb_pool, s.cbs[1])
                        sp.dma_start(comb_dram[s.set], comb_t).then_inc(comb_stored, 16)
                        sp.wait_ge(comb_stored, 16 * (s.no + 1))
                    elif s.kind == "spread":
                        for by_pool, number in s.freed:
                            if by_pool:
                                sp.wait_ge(cb_pool, number)
                            else:
                                sp.wait_ge(cb_dve, number)
                        for rows, e in s.experts:
                            sp.dma_start(spread_w[rows, s.buf, :],
                                         comb_dram[s.set, e].partition_broadcast(rows.stop - rows.start)) \
                                .then_inc(spread_full[s.buf], 16)
                        if at_once and s.no == 1:
                            load_and_store()
                if not isinstance(i, int) or i >= 3:
                    sp.wait_ge(out_stored, 16)
                if ("ug", 3) in kinds and not preloaded(i):
                    sp.wait_ge(xl_loaded, 16)
                if preloaded(i):
                    sp.wait_ge(down_loaded, 16)
                if isinstance(i, int) and i == BATCH + 1:
                    sp.wait_ge(xe_final, 1)
                    sp.dma_start(out_dram[BATCH - 1].rearrange("(t p) d -> p t d", p=P),
                                 X["xe"][:, :, :]).then_inc(out_stored, 16)
                    sp.wait_ge(out_stored, 32)
                sp.drain()
                sp.sem_inc(arrived, 1)
                sp.wait_ge(go_sync, 1)
                sp.sem_clear(go_sync)
            run(sp, segment)

        @block.tensor
        def _(pe):
            def mm3(out, w, x, first, last):
                nc.tensor.matmul(out, w[0], x[0], start=first, stop=False)
                nc.tensor.matmul(out, w[0], x[1], start=False, stop=False)
                return nc.tensor.matmul(out, w[1], x[0], start=False, stop=last)

            def weights(name, k, width=P):
                c = COL[name] + k * width
                return w_hi[:, c:c + width], w_lo[:, c:c + width]

            pe.wait_ge(small_loaded, 16 * len(small))
            pe.wait_ge(bc_copied, 1)
            for j in range(3):
                nc.tensor.matmul(m_b[:, j * DIM:(j + 1) * DIM], proj[:, j * DIM:(j + 1) * DIM], dft,
                                 start=True, stop=True)
            for j in range(3):
                ins = nc.tensor.matmul(m_c[:, j * DIM:(j + 1) * DIM],
                                       bias_cols[:, j * DIM:(j + 1) * DIM], dft, start=True, stop=True)
            ins.then_inc(mb_full, 1)
            pe.drain()
            pe.sem_inc(arrived, 1)
            pe.wait_ge(go_pe, 1)
            pe.sem_clear(go_pe)

            def segment(i, steps):
                for s in steps:
                    k = s.kind
                    if k in ("ln_c", "rt_l", "rt_a", "rt_c", "yt"):
                        if k == "ln_c":
                            pe.wait_ge(ln_xn, s.no + 1)
                        if k == "rt_c":
                            pe.wait_ge(comb_ready, s.no + 1)
                        if k == "yt":
                            pe.wait_ge(y_copied, s.nth + 1)
                        if k == "rt_l":
                            if s.x_at > 0:
                                pe.wait_ge(misc_free, s.x_at)
                        if s.misc > 0:
                            pe.wait_ge(misc_free, s.misc)
                        tiles = [slice(t * P, (t + 1) * P) for t in range(TILES)]
                        if k == "ln_c":
                            for t in range(TILES):
                                ins = nc.tensor.transpose(misc[:, tiles[t]], xn[:, s.no % 2, t, :], ident)
                        elif k == "yt":
                            for t in range(TILES):
                                ins = nc.tensor.transpose(misc[:, tiles[t]], y_t[:, tiles[t]], ident)
                        elif k == "rt_l":
                            ins = mm3(misc[:, :], weights(f"r{s.layer}", 0),
                                      (xt_hi[:, s.set, :], xt_lo[:, s.set, :]), True, True)
                        elif k == "rt_a":
                            for t in range(TILES):
                                ins = nc.tensor.transpose(misc[:, t * EXPERTS:(t + 1) * EXPERTS],
                                                          logits_t[:, tiles[t]], ident_logits)
                        elif k == "rt_c":
                            for t in range(TILES):
                                ins = nc.tensor.transpose(misc[0:EXPERTS, tiles[t]], comb[:, t, :],
                                                          ident)
                        ins.then_inc(misc_full, 1)
                    elif k == "uh":
                        if s.k == 0 and s.x_at > 0:
                            pe.wait_ge(misc_free, s.x_at)
                        if s.b >= HG:
                            pe.wait_ge(silu_done, s.b - HG + 1)
                        mm3(h_ps[s.b % HG][:, :], weights(f"up{s.layer}", s.k),
                            (xt_hi[:, s.set, :], xt_lo[:, s.set, :]), True, True).then_inc(h_full, 1)
                    elif k == "ug":
                        if s.b >= HG:
                            pe.wait_ge(act_done, s.b - HG + 1)
                        mm3(g_ps[s.b % HG][:, :], weights(f"gate{s.layer}", s.k),
                            (xt_hi[:, s.set, :], xt_lo[:, s.set, :]), True, True).then_inc(g_full, 1)
                    elif k == "down":
                        if s.k == 0 and s.nth > 0:
                            pe.wait_ge(y_copied, s.nth)
                        pe.wait_ge(act_done, s.b + 1)
                        at = (s.layer * BLOCKS0 + s.k) * P
                        nc.tensor.matmul(y_ps[:, :], w_down[:, at:at + P], val[:, s.b % RING, :],
                                         start=s.k == 0, stop=s.k == BLOCKS[s.layer] - 1) \
                            .then_inc(down_done, 1)
                    elif k in ("m_in", "m_z"):
                        if s.x_at > 0:
                            pe.wait_ge(misc_free, s.x_at)
                        xs = xt_hi[:, MIXER_SET, :], xt_lo[:, MIXER_SET, :]
                        off = 0 if k == "m_in" else HALVES
                        if s.mb > 0:
                            pe.wait_ge(mb_free, s.mb)
                        mm3(m_b[:, :], weights("in", off), xs, True, True).then_inc(mb_full, 1)
                        if s.mc > 0:
                            pe.wait_ge(mc_free, s.mc)
                        mm3(m_c[:, :], weights("in", off + 1), xs, True, True).then_inc(mc_full, 1)
                    elif k == "m_xp":
                        pe.wait_ge(u_ready, HALVES)
                        if s.mb > 0:
                            pe.wait_ge(mb_free, s.mb)
                        for h in range(HALVES):
                            ins = nc.tensor.matmul(m_b[:, :], xproj[:, h, :], u[:, h, :],
                                                   start=h == 0, stop=h == HALVES - 1)
                        ins.then_inc(mb_full, 1)
                    elif k == "m_dt":
                        pe.wait_ge(dtlo_ready, 1)
                        if s.mb > 0:
                            pe.wait_ge(mb_free, s.mb)
                        nc.tensor.matmul(m_b[:, :], wdt[:, 0:P], dt_lo, start=True, stop=True) \
                            .then_inc(mb_full, 1)
                        if s.mc > 0:
                            pe.wait_ge(mc_free, s.mc)
                        nc.tensor.matmul(m_c[:, :], wdt[:, P:2 * P], dt_lo, start=True, stop=True) \
                            .then_inc(mc_full, 1)
                    elif k == "m_even" and s.n < STATES:
                        pe.wait_ge(bc_parts, 1)
                        pe.wait_ge(bc_ready, 1)
                        if s.mb > 0:
                            pe.wait_ge(mb_free, s.mb)
                        nc.tensor.matmul(m_b[:, :], selbc[:, s.n * P:(s.n + 1) * P], bc3[:, 0, :],
                                         start=True, stop=True).then_inc(mb_full, 1)
                    elif k == "m_odd" and 1 <= s.n <= STATES:
                        if s.mc > 0:
                            pe.wait_ge(mc_free, s.mc)
                        nc.tensor.matmul(m_c[:, :], selbc[:, (s.n - 1) * P:s.n * P], bc3[:, 1, :],
                                         start=True, stop=True).then_inc(mc_full, 1)
                    elif k == "m_out":
                        pe.wait_ge(yz_ready, 1)
                        if s.mb > 0:
                            pe.wait_ge(mb_free, s.mb)
                        for t in range(TILES):
                            for h in range(HALVES):
                                ins = nc.tensor.matmul(m_b[:, t * P:(t + 1) * P],
                                                       u[:, h, t * P:(t + 1) * P], wout[:, h, :],
                                                       start=h == 0, stop=h == HALVES - 1)
                        ins.then_inc(mb_full, 1)
                    elif k == "a_f":
                        if s.x_at > 0:
                            pe.wait_ge(misc_free, s.x_at)
                        ps, full, free, uses = (m_b, mb_full, mb_free, s.mb) if s.t % 2 == 0 \
                            else (m_c, mc_full, mc_free, s.mc)
                        if uses > 0:
                            pe.wait_ge(free, uses)
                        cols = slice(s.t * P, (s.t + 1) * P)
                        mm3(ps[:, 0:3 * DIM], (xt_hi[:, MIXER_SET, cols], xt_lo[:, MIXER_SET, cols]),
                            (wf_hi[:, :], wf_lo[:, :]), True, True).then_inc(full, 1)
                    elif k == "a_cum":
                        pe.wait_ge(kv_ready, 1)
                        if s.mb > 0:
                            pe.wait_ge(mb_free, s.mb)
                        for t in range(TILES):
                            for v in range(t + 1):
                                ins = nc.tensor.matmul(m_b[:, t * P:(t + 1) * P],
                                                       tri if v == t else ones, kv[:, v, :],
                                                       start=v == 0, stop=v == t)
                        ins.then_inc(mb_full, 1)
                    elif k == "a_t":
                        pe.wait_ge(out_spec_ready, 1)
                        if s.mc > 0:
                            pe.wait_ge(mc_free, s.mc)
                        for t in range(TILES):
                            ins = nc.tensor.transpose(m_c[:, t * P:(t + 1) * P], spec_out[:, t, :], ident)
                        ins.then_inc(mc_full, 1)
                    elif k == "a_i":
                        if s.mc > 0:
                            pe.wait_ge(mc_free, s.mc)
                        if s.mb > 0:
                            pe.wait_ge(mb_free, s.mb)
                        for t in range(TILES):
                            ins = nc.tensor.matmul(m_b[:, t * P:(t + 1) * P], o_t[:, t * P:(t + 1) * P],
                                                   idft, start=True, stop=True)
                        ins.then_inc(mb_full, 1)
                pe.drain()
                pe.sem_inc(arrived, 1)
                pe.wait_ge(go_pe, 1)
                pe.sem_clear(go_pe)
            run(pe, segment)

        @block.scalar
        def _(act):
            for j in range(SETUP_CHUNKS):
                act.wait_ge(w_loaded[j % 2], 16 * (j // 2 + 1))
                nc.scalar.activation(w_hi[:, j * CHUNK:(j + 1) * CHUNK],
                                     staging[:, (j % 2) * CHUNK:(j % 2 + 1) * CHUNK],
                                     ACT.Copy).then_inc(hi_done, 1)
            act.wait_ge(small_loaded, 16 * len(small))
            nc.scalar.activation(a_neg[:, :, :], a_log, ACT.Exp).then_inc(act_chain, 1)
            act.wait_ge(mb_full, 1)
            nc.scalar.activation(wf_hi[:, :], m_b[:, 0:3 * DIM], ACT.Copy).then_inc(ln_hi, 1)
            nc.scalar.activation(spec_bias[:, :], m_c[:, 0:3 * DIM], ACT.Copy)
            act.drain()
            act.sem_inc(arrived, 1)
            act.wait_ge(go_act, 1)
            act.sem_clear(go_act)

            def segment(i, steps):
                for s in steps:
                    k = s.kind
                    if k == "ln_c":
                        act.wait_ge(misc_full, s.misc + 1)
                        nc.scalar.activation(xt_hi[:, s.set, :], misc[:, :], ACT.Copy) \
                            .then_inc(ln_hi, 1)
                    elif k == "w_split":
                        j = s.t
                        act.wait_ge(w_loaded[j % 2], 16 * (j // 2 + 1))
                        nc.scalar.activation(w_hi[:, j * CHUNK:(j + 1) * CHUNK],
                                             staging[:, (j % 2) * CHUNK:(j % 2 + 1) * CHUNK],
                                             ACT.Copy).then_inc(w_hi_done, 1)
                    elif k == "rt_l":
                        act.wait_ge(misc_full, s.misc + 1)
                        nc.scalar.activation(logits_t, misc[0:EXPERTS, :], ACT.Copy) \
                            .then_inc(misc_free, 1)
                    elif k == "rt_a":
                        act.wait_ge(gap_ready, s.no + 1)
                        nc.scalar.activation(th[:, :], gap[:, :], ACT.Tanh, scale=0.5) \
                            .then_inc(th_ready, 1)
                    elif k == "rt_c":
                        act.wait_ge(misc_full, s.misc + 1)
                        if s.no:
                            act.wait_ge(comb_stored, 16 * s.no)
                        nc.scalar.activation(comb_t, misc[0:EXPERTS, :], ACT.Copy) \
                            .then_inc(misc_free, 1)
                        act.wait_ge(misc_free, s.misc + 1)
                        act.sem_inc(comb_copied, 1)
                    elif k == "uh":
                        act.wait_ge(h_full, s.b + 1)
                        if s.b >= RING:
                            act.wait_ge(down_done, s.b - RING + 1)
                        nc.scalar.activation(val[:, s.b % RING, :], h_ps[s.b % HG][:, :], ACT.Silu) \
                            .then_inc(silu_done, 1)
                    elif k == "ye":
                        if s.b > 0:
                            act.wait_ge(down_done, s.b)
                        nc.scalar.activation(y_t[:, :], y_ps[:, :], ACT.Copy).then_inc(y_copied, 1)
                    elif k in ("m_in", "m_z", "m_dt"):
                        for h, (ps, full, free, uses) in enumerate(((m_b, mb_full, mb_free, s.mb),
                                                                    (m_c, mc_full, mc_free, s.mc))):
                            act.wait_ge(full, uses + 1)
                            if k == "m_in":
                                ins = nc.scalar.activation(x_in[:, h, TAPS - 1:], ps[:, :], ACT.Copy)
                            elif k == "m_z":
                                ins = nc.scalar.activation(dt[:, h, :], ps[:, :], ACT.Silu)
                            else:
                                ins = nc.scalar.activation(dt_pre[:, h, :], ps[:, :], ACT.Identity,
                                                           bias=b_dt[:, h, :])
                            ins.then_inc(free, 1)
                    elif k == "m_conv" and s.t == TAPS - 1:
                        for h in range(HALVES):
                            act.wait_ge(tap_done, HALVES * s.t + h + 1)
                            nc.scalar.activation(u[:, h, :], conv[1][:, h, :], ACT.Silu,
                                                 bias=conv_b[:, h, :]).then_inc(u_ready, 1)
                    elif k == "m_xp":
                        act.wait_ge(mb_full, s.mb + 1)
                        nc.scalar.activation(dt_lo, m_b[0:RANK, :], ACT.Copy) \
                            .then_inc(dtlo_ready, 1)
                        nc.scalar.activation(bc[:, 0, :], m_b[32:32 + STATES, :], ACT.Copy) \
                            .then_inc(bc_copied, 1)
                        nc.scalar.activation(bc[:, 1, :], m_b[64:64 + STATES, :], ACT.Copy) \
                            .then_inc(mb_free, 1)
                    elif k == "m_bc":
                        act.wait_ge(bc_copied, 1)
                        if s.mb > 0:
                            act.wait_ge(mb_free, s.mb)
                        nc.scalar.activation(bc3[0:STATES, :, :], bc, ACT.Copy).then_inc(bc_hi, 1)
                    elif k == "m_bc2":
                        act.wait_ge(bc_rest_ready, 1)
                        nc.scalar.activation(bc_mid, bc_rest, ACT.Copy).then_inc(bc_mid_ready, 1)
                        act.wait_ge(bc_mid_ready, 1)
                        nc.scalar.activation(bc3[32:32 + STATES, :, :], bc_mid, ACT.Copy) \
                            .then_inc(bc_parts, 1)
                    elif k == "m_sp":
                        act.wait_ge(negabs_ready, 1)
                        nc.scalar.activation(dt_exp, neg_abs, ACT.Exp).then_inc(act_chain, 1)
                        act.wait_ge(act_chain, 1)
                        nc.scalar.activation(neg_abs, dt_exp, ACT.Ln, bias=1.0) \
                            .then_inc(log_ready, 1)
                    elif k == "m_sp3":
                        act.wait_ge(dtu_ready, 1)
                        for h in range(HALVES):
                            nc.scalar.activation(u[:, h, :], u[:, h, :], ACT.Copy,
                                                 scale=d_skip[:, h, :]).then_inc(y_started, 1)
                    elif k == "m_exp":
                        act.wait_ge(dt_ready, 1)
                        act.wait_ge(dtu_ready, 1)
                        for n in range(s.n, s.n + EXP_STATES):
                            if n >= DECAY_RING:
                                act.wait_ge(scan_done, n - DECAY_RING + 1)
                            for h in range(HALVES):
                                nc.scalar.activation(decay[:, n % DECAY_RING, h, 1:], dt[:, h, 1:],
                                                     ACT.Exp, scale=a_neg[:, h, n:n + 1]) \
                                    .then_inc(decay_ready, 1)
                    elif k == "m_even" and s.n < STATES:
                        act.wait_ge(mb_full, s.mb + 1)
                        if s.n >= 2:
                            act.wait_ge(drive_ready, s.n - 1)
                        nc.scalar.activation(b_sb[:, s.n % 2, :], m_b[:, :], ACT.Copy) \
                            .then_inc(mb_free, 1)
                    elif k == "a_pow":
                        if s.mb > 0:
                            act.wait_ge(mb_free, s.mb)
                        if s.mc > 0:
                            act.wait_ge(mc_free, s.mc)
                        nc.scalar.activation(power, spec, ACT.Square).then_inc(sq_ready, 1)
                    elif k == "a_mag":
                        act.wait_ge(power_ready, 1)
                        nc.scalar.activation(mag, power[:, :, :, 0:REAL], ACT.Sqrt) \
                            .then_inc(mag_ready, 1)
                    elif k == "a_t":
                        act.wait_ge(mc_full, s.mc + 1)
                        nc.scalar.activation(o_t, m_c[:, :], ACT.Copy).then_inc(mc_free, 1)
                act.drain()
                act.sem_inc(arrived, 1)
                act.wait_ge(go_act, 1)
                act.sem_clear(go_act)
            run(act, segment)

        @block.vector
        def _(dve):
            tt, ts, stt = nc.vector.tensor_tensor, nc.vector.tensor_scalar, nc.vector.scalar_tensor_tensor

            nc.vector.memset(router_bias[:, 0, :], 0.0)
            nc.vector.memset(bc3[:, :, :], 0.0)
            nc.vector.memset(minus_half[:, :], -0.5)
            for j in range(SETUP_CHUNKS):
                cols = slice(j * CHUNK, (j + 1) * CHUNK)
                dve.wait_ge(hi_done, j + 1)
                tt(w_lo[:, cols], staging[:, (j % 2) * CHUNK:(j % 2 + 1) * CHUNK],
                   w_hi[:, cols].bitcast(f32), ALU.subtract).then_inc(lo_done, 1)
            dve.wait_ge(small_loaded, 16 * len(small))
            for j in range(3):
                ins = ts(bias_cols[:, j * DIM:(j + 1) * DIM], ones, proj[:, 4 * DIM + j:4 * DIM + j + 1],
                         None, ALU.mult)
            ins.then_inc(bc_copied, 1)
            dve.wait_ge(act_chain, 1)
            ts(a_neg[:, :, :], a_neg[:, :, :], -1.0, None, ALU.mult)
            dve.wait_ge(ln_hi, 1)
            tt(wf_lo[:, :], m_b[:, 0:3 * DIM], wf_hi[:, :].bitcast(f32), ALU.subtract)
            dve.drain()
            dve.sem_inc(arrived, 1)
            dve.wait_ge(go_dve, 1)
            dve.sem_clear(go_dve)

            re, im, re1 = slice(0, REAL), slice(REAL, DIM), slice(1, 1 + IMAG)

            def segment(i, steps):
                count = Count()

                for s in steps:
                    k = s.kind
                    if k == "ln_a":
                        if s.x_misc:
                            dve.wait_ge(misc_free, s.x_misc)
                        if s.x_mb:
                            dve.wait_ge(mb_free, s.x_mb)
                        if s.src == "xl" and not preloaded(i):
                            dve.wait_ge(xl_loaded, 16)
                        if s.src == "xe":
                            dve.wait_ge(xe_ready, 1)
                        if s.no > 0:
                            dve.wait_ge(ln_stats, s.no)
                        if s.no - 1 > 0:
                            dve.wait_ge(ln_rstd, s.no - 1)
                        for t in range(TILES):
                            ins = nc.vector.bn_stats(stats[:, t, :], X[s.src][:, t, :])
                        ins.then_inc(dve_chain, 1)
                        dve.wait_ge(dve_chain, count.up())
                        for t in range(TILES):
                            ins = nc.vector.bn_aggr(moments[:, s.no % 2, t, :], stats[:, t, :])
                        ins.then_inc(ln_stats, 1)
                    elif k == "ln_b":
                        dve.wait_ge(ln_rstd, s.no + 1)
                        for t in range(TILES):
                            ins = ts(xn[:, s.no % 2, t, :], X[s.src][:, t, :],
                                     moments[:, s.no % 2, t, 0:1], rstd[:, s.no % 2, t:t + 1],
                                     ALU.subtract, ALU.mult)
                        ins.then_inc(ln_xn, 1)
                    elif k == "ln_c":
                        dve.wait_ge(ln_hi, s.no + 1)
                        tt(xt_lo[:, s.set, :], misc[:, :], xt_hi[:, s.set, :].bitcast(f32), ALU.subtract) \
                            .then_inc(misc_free, 1)
                    elif k == "w_split":
                        j = s.t
                        cols = slice(j * CHUNK, (j + 1) * CHUNK)
                        dve.wait_ge(w_hi_done, j - SETUP_CHUNKS + 1)
                        tt(w_lo[:, cols], staging[:, (j % 2) * CHUNK:(j % 2 + 1) * CHUNK],
                           w_hi[:, cols].bitcast(f32), ALU.subtract).then_inc(lo_done, 1)
                    elif k == "rt_a":
                        dve.wait_ge(misc_full, s.misc + 1)
                        bias = router_bias[:, s.layer, :].unsqueeze(1).to_broadcast([P, TILES, EXPERTS])
                        tt(logits, misc[:, 0:TILES * EXPERTS]
                           .rearrange("p (t e) -> p t e", t=TILES), bias, ALU.add) \
                            .then_inc(misc_free, 1)
                        dve.wait_ge(misc_free, s.misc + 1)
                        for t in range(TILES):
                            ins = nc.vector.max(top[:, t, :], logits[:, t, :])
                        ins.then_inc(dve_chain, 1)
                        dve.wait_ge(dve_chain, count.up())
                        tt(gap[:, :], top[:, :, 0], top[:, :, 1], ALU.subtract) \
                            .then_inc(gap_ready, 1)
                        for t in range(TILES):
                            ins = nc.vector.max_index(top_at[:, t, :], top[:, t, :], logits[:, t, :])
                        ins.then_inc(dve_chain, 1)
                        dve.wait_ge(dve_chain, count.up())
                        nc.vector.tensor_copy(top_f[:, :, :], top_at[:, :, 0:2]) \
                            .then_inc(dve_chain, 1)
                        count.up()
                    elif k == "rt_b":
                        dve.wait_ge(th_ready, s.no + 1)
                        ts(pair_w[:, :, 0], th[:, :], 0.25, 0.25, ALU.mult, ALU.add)
                        ts(pair_w[:, :, 1], th[:, :], -0.25, 0.25, ALU.mult, ALU.add) \
                            .then_inc(dve_chain, 1)
                        count.up()
                        dve.wait_ge(dve_chain, count.n - 1)
                        every = [P, TILES, 2, EXPERTS]
                        tt(hot[:, :, :, :], iota.unsqueeze(1).unsqueeze(1).to_broadcast(every),
                           top_f[:, :, :].unsqueeze(3).to_broadcast(every), ALU.is_equal) \
                               .then_inc(dve_chain, 1)
                        dve.wait_ge(dve_chain, count.up())
                        tt(hot[:, :, :, :], hot[:, :, :, :],
                           pair_w[:, :, :].unsqueeze(3).to_broadcast(every), ALU.mult) \
                               .then_inc(dve_chain, 1)
                        dve.wait_ge(dve_chain, count.up())
                        tt(comb[:, :, :], hot[:, :, 0, :], hot[:, :, 1, :], ALU.add) \
                            .then_inc(comb_ready, 1)
                    elif k == "cb" and not s.by_pool:
                        dve.wait_ge(silu_done, s.b + 1)
                        dve.wait_ge(spread_full[s.buf], s.filled)
                        v = s.b % RING
                        tt(val[:, v, :], val[:, v, :], spread_w[:, s.buf, :], ALU.mult) \
                            .then_inc(cb_dve, 1)
                    elif k == "ac":
                        v = s.b % RING
                        if s.shared:
                            dve.wait_ge(silu_done, s.b + 1)
                            dve.wait_ge(g_full, s.b + 1)
                            stt(val[:, v, :], val[:, v, :], 0.5, g_ps[s.b % HG][:, :], ALU.mult,
                                ALU.mult).then_inc(act_done, 1)
                        else:
                            if s.scaled[0]:
                                dve.wait_ge(cb_pool, s.scaled[1])
                            else:
                                dve.wait_ge(cb_dve, s.scaled[1])
                            dve.wait_ge(g_full, s.b + 1)
                            tt(val[:, v, :], val[:, v, :], g_ps[s.b % HG][:, :], ALU.mult) \
                                .then_inc(act_done, 1)
                    elif k == "yt":
                        if s.x_misc:
                            dve.wait_ge(misc_free, s.x_misc)
                        if s.x_mb:
                            dve.wait_ge(mb_free, s.x_mb)
                        if s.xin == "xl" and not preloaded(i):
                            dve.wait_ge(xl_loaded, 16)
                        if s.xin == "xe":
                            dve.wait_ge(xe_ready, 1)
                        dve.wait_ge(misc_full, s.misc + 1)
                        tt(X[s.xout][:, :, :], X[s.xin][:, :, :],
                           misc[:, :].rearrange("p (t d) -> p t d", t=TILES), ALU.add) \
                            .then_inc(misc_free, 1)
                        if s.c == 1 and isinstance(i, int) and i == BATCH + 1:
                            dve.wait_ge(misc_free, s.misc + 1)
                            dve.sem_inc(xe_final, 1)
                    elif k == "x_e":
                        if not isinstance(i, int) or i >= 3:
                            dve.wait_ge(out_stored, 16)
                        nc.vector.tensor_copy(X["xe"][:, :, :], X["xc"][:, :, :]) \
                            .then_inc(xe_ready, 1)
                    elif k == "x_a":
                        if s.x_misc:
                            dve.wait_ge(misc_free, s.x_misc)
                        nc.vector.tensor_copy(X["xa"][:, :, :], X["xl"][:, :, :])
                    elif k == "m_conv":
                        j = s.t
                        if j == 0:
                            dve.wait_ge(pad_zeroed, 1)
                            dve.wait_ge(mb_free, s.mb)
                            dve.wait_ge(mc_free, s.mc)
                        for h in range(HALVES):
                            src, dst = conv[(j + 1) % 2][:, h, :], conv[j % 2][:, h, :]
                            taken = x_in[:, h, j:j + SEQ], conv_w[:, h, j:j + 1]
                            if j == 0:
                                ts(dst, *taken, None, ALU.mult).then_inc(tap_done, 1)
                            else:
                                dve.wait_ge(tap_done, HALVES * (j - 1) + h + 1)
                                stt(dst, *taken, src, ALU.mult, ALU.add).then_inc(tap_done, 1)
                    elif k == "m_bc":
                        dve.wait_ge(bc_hi, 1)
                        tt(bc_rest, bc, bc3[0:STATES, :, :], ALU.subtract) \
                            .then_inc(bc_rest_ready, 1)
                    elif k == "m_bc2":
                        dve.wait_ge(bc_mid_ready, 1)
                        dve.wait_ge(bc_rest_ready, 1)
                        tt(bc3[64:64 + STATES, :, :], bc_rest, bc_mid, ALU.subtract) \
                            .then_inc(bc_ready, 1)
                    elif k == "m_sp":
                        if s.mb > 0:
                            dve.wait_ge(mb_free, s.mb)
                        if s.mc > 0:
                            dve.wait_ge(mc_free, s.mc)
                        stt(neg_abs, dt_pre, -1.0, dt_pre, ALU.mult, ALU.min) \
                            .then_inc(negabs_ready, 1)
                    elif k == "m_sp2":
                        dve.wait_ge(log_ready, 1)
                        stt(dt[:, :, :], dt_pre, 0.0, neg_abs, ALU.max, ALU.add) \
                            .then_inc(dt_ready, 1)
                    elif k == "m_even" and 1 <= s.n <= STATES:
                        n = s.n - 1
                        dve.wait_ge(decay_ready, HALVES * (n + 1))
                        dve.wait_ge(drive_ready, n + 1)
                        r = n % SCAN_RING
                        whole = scan[:, r, :, :].rearrange("p h t -> p (h t)")
                        nc.vector.tensor_tensor_scan(
                            whole, decay[:, n % DECAY_RING, :, :].rearrange("p h t -> p (h t)"), whole,
                            0.0, ALU.mult, ALU.add).then_inc(scan_done, 1)
                    elif k == "m_odd" and s.n >= 1:
                        if s.n <= STATES:
                            dve.wait_ge(mc_full, s.mc + 1)
                            dve.wait_ge(scan_done, s.n)
                            r = (s.n - 1) % SCAN_RING
                            tt(scan[:, r, :, :], scan[:, r, :, :],
                               m_c[:, :].unsqueeze(1).to_broadcast([P, HALVES, SEQ]), ALU.mult) \
                                .then_inc(mc_free, 1)
                        if s.dve_adds and s.n >= 2:
                            if s.n == 2:
                                dve.wait_ge(y_started, HALVES)
                            else:
                                dve.wait_ge(y_added, s.n - 2)
                            dve.wait_ge(mc_free, s.mc)
                            tt(u[:, :, :], u[:, :, :], scan[:, (s.n - 2) % SCAN_RING, :, :], ALU.add) \
                                .then_inc(y_added, 1)
                    elif k in ("m_out", "a_i"):
                        if s.x_misc:
                            dve.wait_ge(misc_free, s.x_misc)
                        if s.x_mb:
                            dve.wait_ge(mb_free, s.x_mb)
                        dve.wait_ge(mb_full, s.mb + 1)
                        tt(X[s.xout][:, :, :], X[s.xin][:, :, :],
                           m_b[:, :].rearrange("p (t d) -> p t d", t=TILES), ALU.add) \
                            .then_inc(mb_free, 1)
                    elif k == "a_f":
                        ps, full, free, uses = (m_b, mb_full, mb_free, s.mb) if s.t % 2 == 0 \
                            else (m_c, mc_full, mc_free, s.mc)
                        dve.wait_ge(full, uses + 1)
                        tt(spec[:, s.t].rearrange("p n d -> p (n d)"), ps[:, 0:3 * DIM], spec_bias[:, :],
                           ALU.add).then_inc(free, 1)
                    elif k == "a_rec":
                        dve.wait_ge(mags_ready, 1)
                        nc.vector.reciprocal(rkv, rkv)
                        nc.vector.reciprocal(rq, mag[:, :, 0, :]).then_inc(dve_chain, 1)
                        count.up()
                        if count.n > 0:
                            dve.wait_ge(dve_chain, count.n)
                    elif k == "a_kv":
                        q, ky, vl = (spec[:, :, j, :] for j in range(3))
                        tt(kv[:, :, re], ky[:, :, re], vl[:, :, re], ALU.mult)
                        tt(kv[:, :, im], ky[:, :, im], vl[:, :, re1], ALU.mult)
                        tt(prod[0], ky[:, :, im], vl[:, :, im], ALU.mult)
                        tt(prod[1], ky[:, :, re1], vl[:, :, im], ALU.mult).then_inc(dve_chain, 1)
                        dve.wait_ge(dve_chain, count.up())
                        tt(kv[:, :, re1], kv[:, :, re1], prod[0], ALU.subtract)
                        tt(kv[:, :, im], kv[:, :, im], prod[1], ALU.add).then_inc(dve_chain, 1)
                        dve.wait_ge(dve_chain, count.up())
                        tt(kv[:, :, re], kv[:, :, re], rkv, ALU.mult)
                        tt(kv[:, :, im], kv[:, :, im], rkv[:, :, re1], ALU.mult) \
                            .then_inc(kv_ready, 1)
                        tt(q[:, :, re], q[:, :, re], rq, ALU.mult)
                        tt(q[:, :, im], q[:, :, im], rq[:, :, re1], ALU.mult).then_inc(dve_chain, 1)
                        dve.wait_ge(dve_chain, count.up())
                    elif k == "a_o":
                        q = spec[:, :, 0, :]
                        sums = m_b[:, :].rearrange("p (t d) -> p t d", t=TILES)
                        if s.mb > 0:
                            dve.wait_ge(mb_full, s.mb)
                        tt(spec_out[:, :, re], sums[:, :, re], q[:, :, re], ALU.mult)
                        tt(spec_out[:, :, im], sums[:, :, im], q[:, :, re1], ALU.mult)
                        tt(prod[0], sums[:, :, im], q[:, :, im], ALU.mult)
                        tt(prod[1], sums[:, :, re1], q[:, :, im], ALU.mult).then_inc(mb_free, 1)
                        if s.mb > 0:
                            dve.wait_ge(mb_free, s.mb)
                        tt(spec_out[:, :, re1], spec_out[:, :, re1], prod[0], ALU.add)
                        tt(spec_out[:, :, im], spec_out[:, :, im], prod[1], ALU.subtract) \
                            .then_inc(out_spec_ready, 1)
                dve.drain()
                dve.sem_inc(arrived, 1)
                dve.wait_ge(go_dve, 1)
                dve.sem_clear(go_dve)
            run(dve, segment)

        @block.gpsimd
        def _(pool):
            tt = nc.gpsimd.tensor_tensor

            def meet_all():
                pool.drain()
                pool.wait_ge(arrived, len(go))
                pool.sem_clear(range(of_segment[0].num, of_segment[-1].num + 1))
                for sem in go:
                    pool.sem_inc(sem, 1)

            meet_all()

            def segment(i, steps):
                count = Count()

                for s in steps:
                    k = s.kind
                    if k == "ln_a":
                        if s.no > 0:
                            pool.wait_ge(ln_rstd, s.no)
                        pool.wait_ge(ln_stats, s.no + 1)
                        nc.gpsimd.tensor_scalar(var_eps[:, :], moments[:, s.no % 2, :, 1], LN_EPS,
                                                None, ALU.add).then_inc(pool_chain, 1)
                        pool.wait_ge(pool_chain, count.up())
                        tt(rstd[:, s.no % 2, :], var_eps[:, :], minus_half[:, :], ALU.pow) \
                            .then_inc(ln_rstd, 1)
                    elif k == "cb" and s.by_pool:
                        pool.wait_ge(silu_done, s.b + 1)
                        pool.wait_ge(spread_full[s.buf], s.filled)
                        v = s.b % RING
                        tt(val[:, v, :], val[:, v, :], spread_w[:, s.buf, :], ALU.mult) \
                            .then_inc(cb_pool, 1)
                    elif k == "m_in":
                        nc.gpsimd.memset(x_in[:, :, 0:TAPS - 1], 0.0).then_inc(pad_zeroed, 1)
                    elif k == "m_sp2":
                        pool.wait_ge(dt_ready, 1)
                        nc.gpsimd.memset(decay[:, :, :, 0:1], 0.0)
                        tt(dtu[:, :, :], dt[:, :, :], u[:, :, :], ALU.mult).then_inc(dtu_ready, 1)
                    elif k == "m_even" and s.n < STATES:
                        if s.n == 0:
                            pool.wait_ge(dtu_ready, 1)
                        pool.wait_ge(mb_free, s.mb + 1)
                        if s.n >= SCAN_RING:
                            pool.wait_ge(y_added, s.n - SCAN_RING + 1)
                        tt(scan[:, s.n % SCAN_RING, :, :], dtu[:, :, :],
                           b_sb[:, s.n % 2, :].unsqueeze(1).to_broadcast([P, HALVES, SEQ]), ALU.mult) \
                            .then_inc(drive_ready, 1)
                    elif k == "m_odd" and s.n >= 2 and not s.dve_adds:
                        if s.n == 2:
                            pool.wait_ge(y_started, HALVES)
                        else:
                            pool.wait_ge(y_added, s.n - 2)
                        pool.wait_ge(mc_free, s.mc)
                        tt(u[:, :, :], u[:, :, :], scan[:, (s.n - 2) % SCAN_RING, :, :], ALU.add) \
                            .then_inc(y_added, 1)
                    elif k == "m_gate":
                        if s.mb > 0:
                            pool.wait_ge(mb_free, s.mb)
                        if s.mc > 0:
                            pool.wait_ge(mc_free, s.mc)
                        pool.wait_ge(y_added, STATES)
                        tt(u[:, :, :], u[:, :, :], dt[:, :, :], ALU.mult).then_inc(yz_ready, 1)
                    elif k == "a_pow":
                        pool.wait_ge(sq_ready, 1)
                        pairs = power[:, :, :, 1:1 + IMAG]
                        tt(pairs, pairs, power[:, :, :, REAL:DIM], ALU.add) \
                            .then_inc(power_ready, 1)
                    elif k == "a_mag":
                        pool.wait_ge(mag_ready, 1)
                        nc.gpsimd.tensor_scalar(mag, mag, MAG_EPS, None, ALU.add) \
                            .then_inc(pool_chain, 1)
                        pool.wait_ge(pool_chain, count.up())
                        tt(rkv, mag[:, :, 1, :], mag[:, :, 2, :], ALU.mult) \
                            .then_inc(mags_ready, 1)
                meet_all()
            run(pool, segment)


def kernel(**inputs):
    import numpy as _np
    import concourse.bacc as _bacc
    from concourse.bass_utils import run_bass_kernel_spmd as _run

    a = {name: _np.asarray(v) for name, v in inputs.items()}

    def rows(w):
        n = w.shape[0] // P
        return w.reshape(n, P, -1).transpose(1, 0, 2).reshape(P, -1)

    def halves(v):
        return v.reshape(HALVES, P, -1).transpose(1, 0, 2)

    def ups(w):
        return w.transpose(1, 0, 2).reshape(DIM, -1)

    def with_shared(w, sw):
        return _np.concatenate([a["L1_ffn_" + w], a["L1_ffn_" + sw]], axis=0)

    split = _np.concatenate([
        a["L0_ffn_Wr"], a["L1_ffn_router_w"].T, ups(a["L0_ffn_W1"]), ups(a["L0_ffn_W3"]),
        a["L0_attn_W_in"].T, ups(with_shared("w1", "sw1")), ups(with_shared("w3", "sw3"))], axis=1)
    down = _np.concatenate([rows(a["L0_ffn_W2"].reshape(-1, DIM)),
                            rows(with_shared("w2", "sw2").reshape(-1, DIM))], axis=1)

    angle = 2 * _np.pi * _np.outer(_np.arange(DIM), _np.arange(REAL)) / DIM
    cos, sin = _np.cos(angle), _np.sin(angle)[:, 1:REAL - 1]
    dft = _np.concatenate([cos, -sin], axis=1).astype(_np.float32)
    weight = _np.where(_np.isin(_np.arange(REAL), (0, REAL - 1)), 1.0, 2.0) / DIM
    idft = _np.concatenate([cos * weight, -sin * 2.0 / DIM], axis=1).T.astype(_np.float32)

    proj = _np.concatenate([a["L1_attn_W" + n] for n in "qkv"] + [dft] +
                           [a["L1_attn_b" + n][:, None] for n in "qkv"], axis=1)
    xp = halves(a["L0_attn_W_xproj"].T)
    xproj = _np.zeros((P, HALVES, P), _np.float32)
    xproj[:, :, 0:RANK] = xp[:, :, 0:RANK]
    xproj[:, :, 32:32 + STATES] = xp[:, :, RANK:RANK + STATES]
    xproj[:, :, 64:64 + STATES] = xp[:, :, RANK + STATES:]
    vec = halves(_np.concatenate([a["L0_attn_conv_w"], a["L0_attn_A_log"]] +
                                 [a["L0_attn_" + n][:, None] for n in ("conv_b", "b_dt", "D_skip")],
                                 axis=1))
    const = _np.concatenate([_np.eye(P), _np.triu(_np.ones((P, P))), idft, _np.ones((P, P)),
                             _np.tile(_np.arange(EXPERTS), (P, 1))], axis=1).astype(_np.float32)
    bf16 = mybir.dt.np(mybir.dt.bfloat16)
    selbc = _np.zeros((PARTS * 32, STATES * P))
    for part in range(PARTS):
        for n in range(STATES):
            selbc[part * 32 + n, n * P:(n + 1) * P] = 1

    arrays = {
        "x_dram": a["L0_attn_x"], "split_dram": split, "down_dram": down, "proj_dram": proj, "xproj_dram": xproj,
        "wdt_dram": a["L0_attn_W_dt"].T, "wout_dram": halves(a["L0_attn_W_out"].T), "vec_dram": vec,
        "bias_dram": a["L1_ffn_experts_bias"], "const_dram": const,
        "selbc_dram": selbc.astype(bf16)}
    arrays = {name: _np.ascontiguousarray(v) for name, v in arrays.items()}

    nc = _bacc.Bacc("TRN2", target_bir_lowering=False, num_devices=1)
    args = [nc.dram_tensor(name, v.shape, mybir.dt.from_np(v.dtype), kind="ExternalInput").ap()
            for name, v in arrays.items()]
    args.append(nc.dram_tensor("comb_dram", (2, EXPERTS, SEQ), mybir.dt.float32, kind="Internal").ap())
    out = nc.dram_tensor("out_dram", (BATCH, SEQ, DIM), mybir.dt.float32, kind="ExternalOutput").ap()
    macaron_kernel(nc, *args, out)
    r = _run(nc, [arrays], core_ids=[0])
    return r.results[0]["out_dram"]
```
